# Optimizing a Trainium2 kernel written in Bass

```python
import numpy as np
import jax
import jax.numpy as jnp

def _softmax(x, axis=-1):
    return jax.nn.softmax(x, axis=axis)

def _gelu(x):
    return jax.nn.gelu(x, approximate=True)

def _silu(x):
    return jax.nn.silu(x)

def _sigmoid(x):
    return jax.nn.sigmoid(x)

def _layernorm(x, axis=-1, eps=1e-05):
    m = jnp.mean(x, axis=axis, keepdims=True)
    v = jnp.var(x, axis=axis, keepdims=True)
    return (x - m) / jnp.sqrt(v + eps)

def _scatter_add(tgt, idx, src, axis=0):
    return tgt.at[idx].add(src)

def _segment_sum(src, seg, n):
    return jax.ops.segment_sum(src, seg, n)
kernel_name = 'mk_gnn_ffn_d1_gnn_r8_e09ca1'

def setup_inputs(seed: int=0):
    np.random.seed(seed)
    _w = jnp.asarray

    def _rec_inputs():
        import jax
        import jax.numpy as jnp
        _gk = jax.random.key(seed)
        x = -0.0003713 + 1 * jax.random.normal(jax.random.fold_in(_gk, 1), (6250, 256), jnp.float32)
        src = jax.random.randint(jax.random.fold_in(_gk, 2), (100000,), 0, 6250, jnp.int32)
        dst = jnp.minimum((6250 * jax.random.uniform(jax.random.fold_in(_gk, 3), (100000,)) ** 2.0).astype(jnp.int32), 49999)
        _o = jnp.argsort(dst, stable=True)
        src = src[_o]
        dst = dst[_o]
        edge_attr_2 = 0.000452788 + 0.999756 * jax.random.normal(jax.random.fold_in(_gk, 11), (100000, 2), jnp.float32)
        return (x, src, dst, edge_attr_2)
    x, src, dst, edge_attr_2 = _rec_inputs()

    def _L0_gnn_setup():
        import jax, jax.numpy as jnp
        import numpy as np
        N = 6250
        E = 100000
        D = 256
        SLOPE = 0.2
        EPS = 1e-05

        def _add_self_loops(src, dst, edge_attr, n):
            deg = jax.ops.segment_sum(jnp.ones((src.shape[0],), edge_attr.dtype), dst, n)
            mean_attr = jax.ops.segment_sum(edge_attr, dst, n) / jnp.maximum(deg, 1.0)[:, None]
            loop = jnp.arange(n, dtype=src.dtype)
            return (jnp.concatenate([src, loop]), jnp.concatenate([dst, loop]), jnp.concatenate([edge_attr, mean_attr], axis=0))

        def _gatv2(x, src, dst, eattr, Wl, Wr, We, att, b, n):
            xl = x @ Wl
            xr = x @ Wr
            ee = eattr @ We
            xj = xl[src]
            h = jax.nn.leaky_relu(xj + xr[dst] + ee, SLOPE)
            logits = h @ att
            m = jax.ops.segment_max(logits, dst, n)
            ex = jnp.exp(logits - m[dst])
            denom = jax.ops.segment_sum(ex, dst, n)
            alpha = ex / denom[dst]
            out = jax.ops.segment_sum(xj * alpha[:, None], dst, n)
            return out + b

        def _bn_train(x, g, b):
            mu = jnp.mean(x, axis=0)
            var = jnp.var(x, axis=0)
            return (x - mu) * jax.lax.rsqrt(var + EPS) * g + b

        def _prelu(x, a):
            return jnp.where(x >= 0, x, a * x)
        key = jax.random.key(seed)
        ks = jax.random.split(key, 24)
        s = 0.05
        inp = {'x': jax.random.normal(ks[0], (N, D), jnp.float32), 'edge_index': jax.random.randint(ks[1], (2, E), 0, N, jnp.int32), 'edge_attr': jax.random.normal(ks[2], (E, 2), jnp.float32)}

        def conv_params(koff):
            return dict(Wl=jax.random.normal(ks[koff + 0], (D, D), jnp.float32) * s, Wr=jax.random.normal(ks[koff + 1], (D, D), jnp.float32) * s, We=jax.random.normal(ks[koff + 2], (2, D), jnp.float32) * s, att=jax.random.normal(ks[koff + 3], (D,), jnp.float32) * s, b=jnp.zeros((D,), jnp.float32))
        p1, p2 = (conv_params(3), conv_params(8))
        inp.update({k + '1': v for k, v in p1.items()})
        inp.update({k + '2': v for k, v in p2.items()})
        inp.update(g1=jnp.ones((D,), jnp.float32), beta1=jnp.zeros((D,), jnp.float32), g2=jnp.ones((D,), jnp.float32), beta2=jnp.zeros((D,), jnp.float32), a1=jnp.asarray(0.25, jnp.float32), a2=jnp.asarray(0.25, jnp.float32))
        return inp
    _L0_gnn_all = _L0_gnn_setup()
    _L0_gnn_in = {k: v for k, v in _L0_gnn_all.items() if k in ('Wl1', 'Wr1', 'We1', 'att1', 'b1', 'g1', 'beta1', 'a1', 'Wl2', 'Wr2', 'We2', 'att2', 'b2', 'g2', 'beta2', 'a2')}
    del _L0_gnn_all

    def _L0_ffn_setup():
        import math
        import jax, jax.numpy as jnp
        import numpy as np
        CAPACITY_FACTOR = 1.25
        key = jax.random.key(seed)
        ks = jax.random.split(key, 5)
        B, L, D, F, E = (8, 1024, 256, 1024, 8)
        h = jax.random.normal(ks[0], (B, L, D), dtype=jnp.float32)
        gate_w = jax.random.normal(ks[1], (D, E), dtype=jnp.float32) * 0.02
        gate_b = jnp.zeros((E,), dtype=jnp.float32)
        w1 = jax.random.normal(ks[2], (E, D, F), dtype=jnp.float32) * (1.0 / math.sqrt(D))
        b1 = jnp.zeros((E, F), dtype=jnp.float32)
        w2 = jax.random.normal(ks[3], (E, F, D), dtype=jnp.float32) * (1.0 / math.sqrt(F))
        b2 = jnp.zeros((E, D), dtype=jnp.float32)
        return {'h': h, 'gate_w': gate_w, 'gate_b': gate_b, 'w1': w1, 'b1': b1, 'w2': w2, 'b2': b2}
    _L0_ffn_all = _L0_ffn_setup()
    _L0_ffn_in = {k: v for k, v in _L0_ffn_all.items() if k in ('gate_w', 'gate_b', 'w1', 'b1', 'w2', 'b2')}
    del _L0_ffn_all
    return {'x': x, 'src': src, 'dst': dst, 'edge_attr_2': edge_attr_2, 'L0_gnn_Wl1': _L0_gnn_in['Wl1'], 'L0_gnn_Wr1': _L0_gnn_in['Wr1'], 'L0_gnn_We1': _L0_gnn_in['We1'], 'L0_gnn_att1': _L0_gnn_in['att1'], 'L0_gnn_b1': _L0_gnn_in['b1'], 'L0_gnn_g1': _L0_gnn_in['g1'], 'L0_gnn_beta1': _L0_gnn_in['beta1'], 'L0_gnn_a1': _L0_gnn_in['a1'], 'L0_gnn_Wl2': _L0_gnn_in['Wl2'], 'L0_gnn_Wr2': _L0_gnn_in['Wr2'], 'L0_gnn_We2': _L0_gnn_in['We2'], 'L0_gnn_att2': _L0_gnn_in['att2'], 'L0_gnn_b2': _L0_gnn_in['b2'], 'L0_gnn_g2': _L0_gnn_in['g2'], 'L0_gnn_beta2': _L0_gnn_in['beta2'], 'L0_gnn_a2': _L0_gnn_in['a2'], 'L0_ffn_gate_w': _L0_ffn_in['gate_w'], 'L0_ffn_gate_b': _L0_ffn_in['gate_b'], 'L0_ffn_w1': _L0_ffn_in['w1'], 'L0_ffn_b1': _L0_ffn_in['b1'], 'L0_ffn_w2': _L0_ffn_in['w2'], 'L0_ffn_b2': _L0_ffn_in['b2']}

def reference(x, src, dst, edge_attr_2, L0_gnn_Wl1, L0_gnn_Wr1, L0_gnn_We1, L0_gnn_att1, L0_gnn_b1, L0_gnn_g1, L0_gnn_beta1, L0_gnn_a1, L0_gnn_Wl2, L0_gnn_Wr2, L0_gnn_We2, L0_gnn_att2, L0_gnn_b2, L0_gnn_g2, L0_gnn_beta2, L0_gnn_a2, L0_ffn_gate_w, L0_ffn_gate_b, L0_ffn_w1, L0_ffn_b1, L0_ffn_w2, L0_ffn_b2):
    import jax
    import jax.numpy as jnp

    def _L0_gnn_ref(x, edge_index, edge_attr, Wl1, Wr1, We1, att1, b1, g1, beta1, a1, Wl2, Wr2, We2, att2, b2, g2, beta2, a2):
        import jax, jax.numpy as jnp
        import numpy as np
        N = 6250
        E = 100000
        D = 256
        SLOPE = 0.2
        EPS = 1e-05

        def _add_self_loops(src, dst, edge_attr, n):
            deg = jax.ops.segment_sum(jnp.ones((src.shape[0],), edge_attr.dtype), dst, n)
            mean_attr = jax.ops.segment_sum(edge_attr, dst, n) / jnp.maximum(deg, 1.0)[:, None]
            loop = jnp.arange(n, dtype=src.dtype)
            return (jnp.concatenate([src, loop]), jnp.concatenate([dst, loop]), jnp.concatenate([edge_attr, mean_attr], axis=0))

        def _gatv2(x, src, dst, eattr, Wl, Wr, We, att, b, n):
            xl = x @ Wl
            xr = x @ Wr
            ee = eattr @ We
            xj = xl[src]
            h = jax.nn.leaky_relu(xj + xr[dst] + ee, SLOPE)
            logits = h @ att
            m = jax.ops.segment_max(logits, dst, n)
            ex = jnp.exp(logits - m[dst])
            denom = jax.ops.segment_sum(ex, dst, n)
            alpha = ex / denom[dst]
            out = jax.ops.segment_sum(xj * alpha[:, None], dst, n)
            return out + b

        def _bn_train(x, g, b):
            mu = jnp.mean(x, axis=0)
            var = jnp.var(x, axis=0)
            return (x - mu) * jax.lax.rsqrt(var + EPS) * g + b

        def _prelu(x, a):
            return jnp.where(x >= 0, x, a * x)
        n = x.shape[0]
        src, dst, eattr = _add_self_loops(edge_index[0], edge_index[1], edge_attr, n)
        residual = x
        h = _gatv2(x, src, dst, eattr, Wl1, Wr1, We1, att1, b1, n)
        h = _prelu(_bn_train(h, g1, beta1), a1)
        h = _gatv2(h, src, dst, eattr, Wl2, Wr2, We2, att2, b2, n)
        h = _bn_train(h, g2, beta2)
        return _prelu(residual + h, a2)

    def _L0_ffn_ref(h, gate_w, gate_b, w1, b1, w2, b2):
        import math
        import jax, jax.numpy as jnp
        import numpy as np
        CAPACITY_FACTOR = 1.25
        B, L, D = h.shape
        E = gate_w.shape[1]
        T = B * L
        C = max(1, math.ceil(CAPACITY_FACTOR * T / E))
        x = h.reshape(T, D)
        logits = x @ gate_w + gate_b
        probs = jax.nn.softmax(logits, axis=-1)
        idx = jnp.argmax(probs, axis=-1)
        prb = jnp.take_along_axis(probs, idx[:, None], axis=1)[:, 0]
        one_hot = jax.nn.one_hot(idx, E, dtype=jnp.float32)
        pos = (jnp.cumsum(one_hot, axis=0) * one_hot).sum(-1).astype(jnp.int32) - 1
        kept = pos < C
        pos_safe = jnp.where(kept, pos, C)
        buf = jnp.zeros((E, C, D), dtype=h.dtype).at[idx, pos_safe].set(x, mode='drop')
        hmid = jax.nn.relu(jnp.einsum('ecd,edf->ecf', buf, w1) + b1[:, None, :])
        ybuf = jnp.einsum('ecf,efd->ecd', hmid, w2) + b2[:, None, :]
        pos_g = jnp.minimum(pos, C - 1)
        y_tok = ybuf[idx, pos_g] * (prb * kept)[:, None]
        y = y_tok.reshape(B, L, D)
        y = jnp.nan_to_num(y, nan=0.0, posinf=10000.0, neginf=-10000.0)
        return y
    edge_index = jnp.stack([src, dst])
    x = x + _L0_gnn_ref(_layernorm(x, axis=-1), edge_index, edge_attr_2, L0_gnn_Wl1, L0_gnn_Wr1, L0_gnn_We1, L0_gnn_att1, L0_gnn_b1, L0_gnn_g1, L0_gnn_beta1, L0_gnn_a1, L0_gnn_Wl2, L0_gnn_Wr2, L0_gnn_We2, L0_gnn_att2, L0_gnn_b2, L0_gnn_g2, L0_gnn_beta2, L0_gnn_a2)
    x = x + _L0_ffn_ref(_layernorm(x, axis=-1)[None], L0_ffn_gate_w, L0_ffn_gate_b, L0_ffn_w1, L0_ffn_b1, L0_ffn_w2, L0_ffn_b2)[0]
    return x

_drawn_inputs = setup_inputs


def setup_inputs(seed=0):
    import zlib

    import numpy as np

    out = dict(_drawn_inputs(seed))
    spreads = {'L0_gnn_b1': (0.0, 0.8),
     'L0_gnn_g1': (1.0, 0.2),
     'L0_gnn_beta1': (0.0, 0.333),
     'L0_gnn_b2': (0.0, 0.8),
     'L0_gnn_g2': (1.0, 0.2),
     'L0_gnn_beta2': (0.0, 0.1),
     'L0_ffn_gate_b': (0.0, 0.1),
     'L0_ffn_b1': (0.0, 0.8),
     'L0_ffn_b2': (0.0, 0.774)}
    factors = {'L0_gnn_We2': 3.945}
    for name, (base, spread) in spreads.items():
        noise = np.random.default_rng([zlib.crc32(name.encode()), seed]).standard_normal(out[name].shape)
        drawn = base * np.exp(spread * noise) if base else spread * noise
        out[name] = jnp.asarray(drawn.astype(out[name].dtype))
    for name, factor in factors.items():
        out[name] = (out[name] * factor).astype(out[name].dtype)
    return out
```

```python
from contextlib import ExitStack

import concourse.bass as bass
from concourse import mybir

ALU = mybir.AluOpType
ACT = mybir.ActivationFunctionType
AX_X = mybir.AxisListType.X
F32 = mybir.dt.float32
I32 = mybir.dt.int32
DVE_ONLY = (mybir.EngineType.DVE,)
ACT_ONLY = (mybir.EngineType.Activation,)
PE_ONLY = (mybir.EngineType.PE,)
POOL_ONLY = (mybir.EngineType.Pool,)
SP_ONLY = (mybir.EngineType.SP,)

BIG = 1.0e30
START = 1.0e29
EPS = 1e-5
PAD_DST = 1000000
IN_RANGE = "the staircase table holds block and tile numbers, which the chip works out in range"


def periods(engine, steps, unroll, lag):
    for k in range(unroll):
        yield k, k
    with engine.Fori(1, steps // unroll) as turn:
        for j in range(unroll):
            yield turn * unroll + j, j
    for k in range(steps, steps + lag):
        yield k, k % unroll


def live(k, lag, steps):
    return not isinstance(k, int) or 0 <= k - lag < steps


def reused(k, lag, ring):
    return not isinstance(k, int) or k - lag >= ring


def program(nc, x, src, dst, ea, layers, gate_w, gate_b, w1, b1, w2, b2, out):
    N, D = x.shape
    E = src.shape[0]
    NX, C_OUT = gate_w.shape[1], w1.shape[2]
    P = 128
    PB = 125
    NB = N // PB
    assert NB * PB == N and D == 256
    G = 2
    TE = G * P
    T = -(-E // TE)
    ROWS = T * G
    FULL = E // P
    REST = E - FULL * P
    K7 = -(-ROWS // P)
    LASTK = ROWS - (K7 - 1) * P
    STEPS = T + NB - 1
    W = D + 1
    UN = 8
    LAG = 5
    assert STEPS % UN == 0
    CAP = -(-5 * N // (4 * NX))
    HC = -(-CAP // 2)
    HALVES = [(0, HC), (HC, CAP - HC)]
    MT = [(m, min(P, CAP - m)) for m in range(0, CAP, P)]
    FC = C_OUT // P

    dst_rows = nc.dram_tensor("dst_rows", (ROWS * P,), F32, kind="Internal").ap()
    ea_rows = nc.dram_tensor("ea_rows", (2, ROWS * P), F32, kind="Internal").ap()
    xl_table = [nc.dram_tensor(f"xl_table{l}", (N, W), F32, kind="Internal").ap() for l in range(2)]
    tok_buf = nc.dram_tensor("tok_buf", (NX * CAP + N, D), F32, kind="Internal").ap()
    y_buf = nc.dram_tensor("y_buf", (NX * CAP, D), F32, kind="Internal").ap()

    with ExitStack() as ctx:
        def sb(name, shape, dt=F32):
            return ctx.enter_context(nc.sbuf_tensor(name, shape, dt))

        def sem(name):
            return ctx.enter_context(nc.semaphore(name))

        H = sb("H", [P, NB, D])
        XR = sb("XR", [P, NB, W])
        XL = sb("XL", [P, NB, W])
        Hn, XRn, XLn = H[0:PB], XR[0:PB, :, 0:D], XL[0:PB, :, 0:D]
        XLf = XL[:, :, :].rearrange("p b w -> p (b w)")
        XRf = XR[:, :, :].rearrange("p b w -> p (b w)")
        ps = ctx.enter_context(nc.psum_tensor("ps", [P, 8, 512], F32))

        ident = sb("ident", [P, P])
        ones = sb("ones", [P, P])
        iota_i = sb("iota_i", [P, P], I32)
        iota_ci = sb("iota_ci", [P, 1], I32)
        iota_row = sb("iota_row", [P, P])
        iota_col = sb("iota_col", [P, 1])
        node_id = sb("node_id", [P, NB])
        eps_col = sb("eps_col", [P, 1])
        src_cols = sb("src_cols", [P, K7 * P], I32)
        block_of = sb("block_of", [1, STEPS], I32)
        tile_of = sb("tile_of", [1, STEPS], I32)

        Wlr = sb("Wlr", [P, 2, 2 * W])
        WeB = sb("WeB", [P, 2, W])
        att_relu = sb("att_relu", [P, D])
        att_lin = sb("att_lin", [P, D])
        rows = sb("rows", [P, 3, D])
        slope = sb("slope", [P, 1])
        junk = sb("junk", [P, W])
        ln_mean = sb("ln_mean", [P, NB])
        ln_rstd = sb("ln_rstd", [P, NB])
        col_a = sb("col_a", [P, NB])

        XJ = 8
        xj = sb("xj", [P, XJ, G, W])
        dst_b = sb("dst_b", [P, 4, TE])
        ST = sb("ST", [P, 4, TE])
        mpos = sb("mpos", [P, 4, TE])
        zs = sb("zs", [P, 2, G, W])
        mu, scale_row = zs[:, 0, 0, 0:D], zs[:, 0, 1, 0:D]
        mk = sb("mk", [P, 2, TE])
        ETs = sb("ETs", [P, 2, TE])
        Es = sb("Es", [P, 2, G, PB])
        staged = mk
        hT = Es
        Srow = sb("Srow", [P, 2, G, P])
        src_slot = sb("src_slot", [P, XJ, G], I32)
        nlog = sb("nlog", [P, 4, G])
        tmin = sb("tmin", [P, 4])
        new_min = sb("new_min", [P, 4])
        resc = sb("resc", [P, 4])
        den_t = sb("den_t", [P, 4])
        NM = sb("NM", [P, NB])
        DEN = sb("DEN", [P, NB])
        EAS = sb("EAS", [P, NB, 3])
        ME = sb("ME", [P, 2, NB])
        LS = sb("LS", [P, NB])
        RS = sb("RS", [P, NB])
        PS_ = sb("PS_", [P, NB])
        ls_slot = sb("ls_slot", [P, 2])

        o = 0
        def carve(base, n, dt=F32):
            nonlocal o
            v = base[:, o:o + n]
            o += n
            return v if dt == F32 else v.bitcast(dt)
        src_i = carve(XLf, K7 * P, I32).rearrange("p (k e) -> p k e", k=K7)
        dst_i = carve(XLf, K7 * P, I32).rearrange("p (k e) -> p k e", k=K7)
        src_f = carve(XLf, K7 * P).rearrange("p (k e) -> p k e", k=K7)
        dst_f = carve(XLf, K7 * P).rearrange("p (k e) -> p k e", k=K7)
        ea_in = carve(XLf, 2 * K7 * P).rearrange("p (k e j) -> p k e j", k=K7, j=2)
        ea_pl = carve(XLf, 2 * K7 * P).rearrange("p (k j e) -> p k j e", k=K7, j=2)
        last_dst = carve(XLf, K7 * P)
        reached = carve(XLf, 512)
        after = carve(XLf, STEPS)
        step_iota = carve(XLf, STEPS)
        step_iota_i = carve(XLf, STEPS, I32)
        block_f = carve(XLf, STEPS)
        tau = carve(XLf, 2)

        o = 0
        w1_sb = carve(XRf, 2 * 2 * C_OUT).rearrange("p (s c f) -> p s c f", s=2, c=2)
        w2_sb = carve(XRf, 2 * FC * D).rearrange("p (s f d) -> p s f d", s=2, f=FC)
        tok = carve(XRf, len(MT) * D).rearrange("p (m d) -> p m d", m=len(MT))
        y_sb = carve(XRf, len(MT) * D).rearrange("p (m d) -> p m d", m=len(MT))
        o = 0
        tokT = carve(XLf, 2 * CAP).rearrange("p (c t) -> p c t", c=2)
        hidT = carve(XLf, FC * CAP).rearrange("p (f t) -> p f t", f=FC)
        o = 0
        xjf = xj[:, :, :, :].rearrange("p s g w -> p (s g w)")
        NE = NB * NX
        def be(v):
            return v.rearrange("p (b e) -> p b e", e=NX)
        probs, onehot, cum, base_eb, tot_eb, chain_mask = (carve(xjf, NE) for _ in range(6))
        b2_all = carve(xjf, 0)
        o = 0
        zf = zs[:, :, :, :].rearrange("p s g w -> p (s g w)")
        gw_sb = carve(zf, 2 * NX).rearrange("p (c e) -> p c e", c=2)
        gb_sb = carve(zf, NX)
        e_off = carve(zf, NX)
        top, first_e, pos, kept, slot_f, coef = (carve(zf, NB) for _ in range(6))
        slot_put = carve(zf, NB, I32)
        slot_get = carve(zf, NB, I32)
        triu = Srow[:, 0, 0, :]
        b1_rows = ETs[0:NX * FC, 0, 0:P]
        b1T = sb("b1T", [P, NX * FC])
        b2B = Wlr[:, :, :].rearrange("p c w -> p (c w)")
        zero_rows = mpos[:, 0, :]

        s_pad = sem("s_pad")
        s_fixed = sem("s_fixed")
        s_edges = sem("s_edges")
        s_edges_f = sem("s_edges_f")
        s_edges_out = sem("s_edges_out")
        s_consts = sem("s_consts")
        s_last = sem("s_last")
        s_srcT = sem("s_srcT")
        s_srcT_out = sem("s_srcT_out")
        s_after = sem("s_after")
        s_blocks = sem("s_blocks")
        s_stairs = sem("s_stairs")
        s_x = sem("s_x")
        s_var = sem("s_var")
        s_root = sem("s_root")
        s_w = sem("s_w")
        s_wext = sem("s_wext")
        s_we = sem("s_we")
        s_feat = sem("s_feat")
        s_staged = sem("s_staged")
        s_tp, s_hT, s_lin, s_xr, s_xl = (sem(n) for n in ("s_tp", "s_hT", "s_lin", "s_xr", "s_xl"))
        s_table = sem("s_table")
        s_state = sem("s_state")
        s_row = [sem(f"s_row{i}") for i in range(4)]
        s_xj = [sem(f"s_xj{i}") for i in range(XJ)]
        s_idx = sem("s_idx")
        s_tick = sem("s_tick")
        s_st, s_z, s_mpos, s_zs, s_relu, s_nlog, s_lbc, s_min, s_et, s_etT, s_e, s_agg, s_acc = (
            sem(n) for n in ("s_st", "s_z", "s_mpos", "s_zs", "s_relu", "s_nlog", "s_lbc", "s_min", "s_et", "s_etT",
                             "s_e", "s_agg", "s_acc"))
        s_sT, s_sT_out = sem("s_sT"), sem("s_sT_out")
        s_nm = sem("s_nm")
        s_eas = sem("s_eas")
        s_tmin = sem("s_tmin")
        s_num = sem("s_num")
        s_self_a, s_self_q = sem("s_self_a"), sem("s_self_q")
        s_link = sem("s_link")
        s_self_z, s_self_relu, s_self_l = sem("s_self_z"), sem("s_self_relu"), sem("s_self_l")
        s_self_d, s_self_e = sem("s_self_d"), sem("s_self_e")
        s_self_w, s_self_t, s_self_h = sem("s_self_w"), sem("s_self_t"), sem("s_self_h")
        s_h = sem("s_h")
        s_sum = sem("s_sum")
        s_sq_in, s_sq = sem("s_sq_in"), sem("s_sq")
        s_x2 = sem("s_x2")
        s_moe_w = sem("s_moe_w")
        s_b1T = sem("s_b1T")
        s_ln2 = sem("s_ln2")
        s_g_tp, s_g_T, s_gate = sem("s_g_tp"), sem("s_g_T"), sem("s_gate")
        s_shift, s_exp = sem("s_shift"), sem("s_exp")
        s_onehot, s_cum = sem("s_onehot"), sem("s_cum")
        s_slots = sem("s_slots")
        s_zero = sem("s_zero")
        s_zero_src = sem("s_zero_src")
        s_put = sem("s_put")
        s_wx = [sem(f"s_wx{i}") for i in range(2)]
        s_tok = sem("s_tok")
        s_tokT, s_tokT_out = sem("s_tokT"), sem("s_tokT_out")
        s_up, s_hid, s_down, s_y = sem("s_up"), sem("s_hid"), sem("s_down"), sem("s_y")
        s_y_out = sem("s_y_out")
        s_b2 = sem("s_b2")
        s_get = sem("s_get")
        s_fin = sem("s_fin")
        s_out = sem("s_out")

        PARTS = [(0, 112), (112, PB)]
        block = ctx.enter_context(nc.Block())

        @block.sync
        def _(sp):
            x_v = x.rearrange("(b p) d -> p b d", p=PB)
            out_v = out.rearrange("(b p) d -> p b d", p=PB)

            sp.wait_ge(s_pad, 1)
            KF = K7 - 1
            for flat, tile in ((src, src_i), (dst, dst_i)):
                sp.dma_start(tile[:, 0:KF, :], flat[0:KF * P * P].rearrange("(k q e) -> q k e", q=P, e=P)).then_inc(s_edges, 16)
                sp.dma_start(tile[0:FULL - KF * P, KF, :], flat[KF * P * P:FULL * P].rearrange("(q e) -> q e", e=P)).then_inc(s_edges, 16)
                sp.dma_start(tile[FULL - KF * P:FULL - KF * P + 1, KF, 0:REST], flat[FULL * P:E].rearrange("(q e) -> q e", q=1)).then_inc(s_edges, 16)
            sp.dma_start(ea_in[:, 0:KF], ea[0:KF * P * P, :].rearrange("(k q e) j -> q k e j", q=P, e=P)).then_inc(s_edges, 16)
            sp.dma_start(ea_in[0:FULL - KF * P, KF], ea[KF * P * P:FULL * P, :].rearrange("(q e) j -> q e j", e=P)).then_inc(s_edges, 16)
            sp.dma_start(ea_in[FULL - KF * P:FULL - KF * P + 1, KF, 0:REST, :], ea[FULL * P:E, :].rearrange("(q e) j -> q e j", q=1)).then_inc(s_edges, 16)
            for a, b_ in PARTS:
                sp.dma_start(H[a:b_], x_v[a:b_]).then_inc(s_x, 16)

            sp.wait_ge(s_edges_f, 2)
            sp.dma_start(dst_rows[0:KF * P * P].rearrange("(k q e) -> q k e", q=P, e=P), dst_f[:, 0:KF, :]).then_inc(s_edges_out, 16)
            sp.dma_start(dst_rows[KF * P * P:].rearrange("(q e) -> q e", e=P), dst_f[0:LASTK, KF, :]).then_inc(s_edges_out, 16)
            for j in range(2):
                sp.dma_start(ea_rows[j, 0:KF * P * P].rearrange("(k q e) -> q k e", q=P, e=P), ea_pl[:, 0:KF, j, :]).then_inc(s_edges_out, 16)
                sp.dma_start(ea_rows[j, KF * P * P:].rearrange("(q e) -> q e", e=P), ea_pl[0:LASTK, KF, j, :]).then_inc(s_edges_out, 16)

            for l, (Wl, Wr, We, att_d, b_d, g_d, beta_d, a_d) in enumerate(layers):
                base = l * STEPS
                if l:
                    sp.wait_ge(s_feat, 2)
                sp.dma_start(Wlr[:, :, 0:D], Wl.rearrange("(c k) n -> k c n", c=2)).then_inc(s_w, 16)
                sp.dma_start(Wlr[:, :, W:W + D], Wr.rearrange("(c k) n -> k c n", c=2)).then_inc(s_w, 16)
                sp.dma_start(WeB[:, :, 0:D], We.partition_broadcast(P)).then_inc(s_w, 16)
                sp.dma_start(att_relu[:, :], att_d.partition_broadcast(P)).then_inc(s_w, 16)
                for i, v in enumerate((b_d, g_d, beta_d)):
                    sp.dma_start(rows[:, i, :], v.partition_broadcast(P)).then_inc(s_w, 16)
                sp.dma_start(slope[:, :], a_d.partition_broadcast(P)).then_inc(s_w, 16)
                sp.wait_ge(s_fixed, 1)
                sp.wait_ge(s_wext, l + 1)
                for j in range(2):
                    sp.dma_start(XR[PB + j:PB + j + 1, :, :], WeB[0:1, j:j + 1, :].to_broadcast([1, NB, W])).then_inc(s_we, 16)
                sp.wait_ge(s_xl, NB * (l + 1))
                xl_v = xl_table[l].rearrange("(b p) w -> p b w", p=PB)
                for a, b_ in PARTS:
                    sp.dma_start(xl_v[a:b_], XL[a:b_]).then_inc(s_table, 16)
                sp.wait_ge(s_edges_out, 16 * 6)
                sp.wait_ge(s_stairs, 1)
                tiles = None
                for k, j in periods(sp, STEPS, UN, 0):
                    if j == 0:
                        _, tiles = nc.values_load_multi_w_load_instructions(
                            tile_of[0:1, bass.ds(k, UN)], engines=SP_ONLY, min_val=0, max_val=T - 1,
                            skip_runtime_bounds_check_because=IN_RANGE)
                    s = k % 4 if isinstance(k, int) else j % 4
                    if reused(k, 0, 4) or l:
                        sp.wait_ge(s_z, base + k - 3)
                    if l == 0 and reused(k, 0, 4):
                        sp.wait_ge(s_sT, k - 3)
                    sp.dma_start(dst_b[:, s, :], dst_rows[bass.ds(tiles[j] * TE, TE)].partition_broadcast(P)).then_inc(s_row[s], 16)
                    sp.dma_start(ST[PB:PB + 2, s, :], ea_rows[:, bass.ds(tiles[j] * TE, TE)]).then_inc(s_row[s], 16)

            sp.wait_ge(s_self_h, 2 * NB)
            for a, b_ in PARTS:
                sp.dma_start(XL[a:b_, :, 0:D], x_v[a:b_]).then_inc(s_x2, 16)

            sp.wait_ge(s_ln2, 1)
            sp.dma_start(gw_sb, gate_w.rearrange("(c k) e -> k c e", c=2)).then_inc(s_moe_w, 16)
            sp.dma_start(gb_sb, gate_b.partition_broadcast(P)).then_inc(s_moe_w, 16)
            sp.dma_start(b1_rows, b1.rearrange("e (f k) -> (e f) k", k=P)).then_inc(s_moe_w, 16)
            sp.wait_ge(s_zero_src, 1)
            R = NX * CAP
            RP = R // P * P
            sp.dma_start(tok_buf[0:RP, :].rearrange("(p r) d -> p r d", p=P), zero_rows[:, 0:D].unsqueeze(1).to_broadcast([P, RP // P, D])).then_inc(s_zero, 16)
            if R > RP:
                sp.dma_start(tok_buf[RP:R, :], zero_rows[0:R - RP, 0:D]).then_inc(s_zero, 16)

            def expert_weights(e, s):
                sp.dma_start(w1_sb[:, s], w1[bass.ds(e, 1), :, :].rearrange("o (c k) f -> k (o c) f", c=2)).then_inc(s_wx[s], 16)
                sp.dma_start(w2_sb[:, s], w2[bass.ds(e, 1), :, :].rearrange("o (f k) d -> k (o f) d", f=FC)).then_inc(s_wx[s], 16)
                sp.dma_start(b2B[:, s * D:(s + 1) * D], b2[bass.ds(e, 1), :].rearrange("o d -> (o d)").partition_broadcast(P)).then_inc(s_wx[s], 16)

            M = len(MT)
            last = MT[-1][1]

            def tokens(e):
                sp.dma_start(tok[:, 0:M - 1, :], tok_buf[bass.ds(e * CAP, P * (M - 1)), :].rearrange("(m p) d -> p m d", p=P)).then_inc(s_tok, 16)
                sp.dma_start(tok[0:last, M - 1, :], tok_buf[bass.ds(e * CAP + P * (M - 1), last), :]).then_inc(s_tok, 16)

            def store_y(e):
                sp.wait_ge(s_y, (e + 1) * M)
                sp.dma_start(y_buf[bass.ds(e * CAP, P * (M - 1)), :].rearrange("(m p) d -> p m d", p=P), y_sb[:, 0:M - 1, :]).then_inc(s_y_out, 16)
                sp.dma_start(y_buf[bass.ds(e * CAP + P * (M - 1), last), :], y_sb[0:last, M - 1, :]).then_inc(s_y_out, 16)

            expert_weights(0, 0)
            expert_weights(1, 1)
            sp.wait_ge(s_put, 16 * NB)
            tokens(0)

            def pair_of_experts(pair, more):
                for s in range(2):
                    e = pair * 2 + s
                    if s == 0 or more:
                        sp.wait_ge(s_tokT, (e + 1) * M)
                        tokens(e + 1)
                    store_y(e)
                    if more:
                        expert_weights(e + 2, s)

            with sp.Fori(0, NX // 2 - 1) as pair:
                pair_of_experts(pair, True)
            pair_of_experts(NX // 2 - 1, False)
            sp.wait_ge(s_fin, 1)
            for a, b_ in PARTS:
                sp.dma_start(out_v[a:b_], H[a:b_]).then_inc(s_out, 16)
            sp.wait_ge(s_out, 32)

        @block.gpsimd
        def _(pool):
            g = nc.gpsimd
            g.memset(src_i, 0)
            g.memset(ea_in, 0.0)
            g.memset(dst_i, PAD_DST).then_inc(s_pad, 1)
            g.iota(iota_i[:, :], pattern=[[1, P]], base=0, channel_multiplier=0)
            g.iota(iota_ci[:, :], pattern=[[0, 1]], base=0, channel_multiplier=1)
            g.iota(step_iota_i, pattern=[[1, STEPS]], base=0, channel_multiplier=0).then_inc(s_pad, 1)

            def stage(feats, done, first):
                for k, j in periods(pool, NB, 2, 0):
                    if reused(k, 0, 2):
                        pool.wait_ge(done, first + k - 1)
                        pool.sem_inc(s_tick)
                    g.tensor_copy(staged[0:PB, j % 2:j % 2 + 1, :], feats[0:PB, bass.ds(k, 1), 0:D]).then_inc(s_staged, 1)

            for l in range(2):
                base = l * STEPS
                pool.wait_ge(s_feat, l + 1)
                stage(H, s_tp, l * NB)
                pool.wait_ge(s_srcT_out, 1)
                pool.wait_ge(s_stairs, 1)
                pool.wait_ge(s_table, 32 * (l + 1))
                tiles = None
                for k, j in periods(pool, STEPS, UN, 0):
                    if j == 0:
                        _, tiles = nc.values_load_multi_w_load_instructions(
                            tile_of[0:1, bass.ds(k, UN)], engines=POOL_ONLY, min_val=0, max_val=T - 1,
                            skip_runtime_bounds_check_because=IN_RANGE)
                    s = j % XJ
                    if reused(k, 0, XJ) or l:
                        pool.wait_ge(s_agg, base + k - XJ + 1)
                        pool.sem_inc(s_tick)
                    g.tensor_copy(src_slot[:, s, :], src_cols[:, bass.ds(tiles[j] * G, G)]).then_inc(s_idx, 1)
                    pool.wait_ge(s_idx, base + k + 1)
                    pool.sem_inc(s_tick)
                    for u in range(G):
                        g.indirect_dma_start(xj[:, s, u, :], None, xl_table[l],
                                             bass.IndirectOffsetOnAxis(src_slot[:, s, u:u + 1], 0)).then_inc(s_xj[s], 16)
            pool.wait_ge(s_ln2, 1)
            stage(XL, s_g_tp, 0)
            pool.wait_ge(s_slots, 1)
            pool.wait_ge(s_zero, 16 * (1 + (NX * CAP % P > 0)))
            for b_ in range(NB):
                g.indirect_dma_start(tok_buf, bass.IndirectOffsetOnAxis(slot_put[0:PB, b_:b_ + 1], 0),
                                     XL[0:PB, b_, 0:D], None).then_inc(s_put, 16)
            pool.wait_ge(s_y_out, 32 * NX)
            pool.wait_ge(s_down, NX * len(MT))
            for b_ in range(NB):
                g.indirect_dma_start(XL[0:PB, b_, 0:D], None, y_buf,
                                     bass.IndirectOffsetOnAxis(slot_get[0:PB, b_:b_ + 1], 0)).then_inc(s_get, 16)

        @block.scalar
        def _(act):
            a = nc.scalar
            act.wait_ge(s_var, 1)
            a.activation(ln_rstd[0:PB, :], col_a[0:PB, :], ACT.Sqrt, bias=eps_col[0:PB, :], scale=1.0 / D).then_inc(s_root, 1)
            for l in range(2):
                base = l * STEPS
                if l == 0:
                    act.wait_ge(s_edges_out, 16 * 6)
                    act.wait_ge(s_srcT_out, 1)
                    act.wait_ge(s_stairs, 1)
                for k, j in periods(act, NB, 2, 1):
                    if live(k, 0, NB):
                        s = j % 2
                        act.wait_ge(s_tp, l * NB + k + 1)
                        if reused(k, 0, 2) or l:
                            act.wait_ge(s_lin, l * NB + k - 1)
                        a.activation(hT[:, s, :, :], ps[:, 4 + s, 0:2 * PB].rearrange("p (c n) -> p c n", c=2), ACT.Copy).then_inc(s_hT, 1)
                    if live(k, 1, NB):
                        s = (j - 1) % 2
                        act.wait_ge(s_lin, l * NB + k)
                        act.sem_inc(s_tick)
                        a.activation(XL[0:PB, bass.ds(k - 1, 1), :], ps[0:PB, 2 * s:2 * s + 1, 0:W], ACT.Copy).then_inc(s_xl, 1)
                act.wait_ge(s_stairs, 1)
                act.wait_ge(s_state, l + 1)
                old = [act.alloc_register(f"old_block_act{l}_{i}") for i in range(LAG)]
                blocks = held = None
                for k, j in periods(act, STEPS, UN, LAG):
                    if j == 0:
                        held = [act.snap(r, min_val=0, max_val=NB - 1) for r in old] if not (isinstance(k, int) and k == 0) else None
                        if live(k, 0, STEPS):
                            _, blocks = nc.values_load_multi_w_load_instructions(
                                block_of[0:1, bass.ds(k, UN)], engines=ACT_ONLY, min_val=0, max_val=NB - 1,
                                skip_runtime_bounds_check_because=IN_RANGE)
                    if live(k, 2, STEPS):
                        s = (j - 2) % 2
                        act.wait_ge(s_zs, base + k - 1)
                        a.activation(zs[:, s, :, 0:D], zs[:, s, :, 0:D], ACT.Relu).then_inc(s_relu, 1)
                    if live(k, 4, STEPS):
                        s = (j - 4) % 2
                        act.wait_ge(s_etT, base + k - 3)
                        if reused(k, 4, 2) or l:
                            act.wait_ge(s_agg, base + k - 5)
                        a.activation(Es[:, s, :, :], ps[:, 5, 0:G * PB].rearrange("p (g n) -> p g n", g=G), ACT.Copy).then_inc(s_e, 1)
                    if l == 0 and live(k, 1, STEPS):
                        act.wait_ge(s_sT, k)
                        if reused(k, 1, 2):
                            act.wait_ge(s_lbc, k - 2)
                        a.activation(Srow[:, (j - 1) % 2, :, :], ps[:, 7, 0:TE].rearrange("p (g n) -> p g n", g=G), ACT.Copy).then_inc(s_sT_out, 1)
                    if live(k, 3, STEPS):
                        s, q = (j - 3) % 2, (j - 3) % 4
                        b_ = blocks[j - 3] if j >= 3 else held[LAG + j - 3]
                        act.wait_ge(s_min, base + k - 2)
                        if reused(k, 3, 2) or l:
                            act.wait_ge(s_etT, base + k - 4)
                        if reused(k, 3, 4) or l:
                            act.wait_ge(s_acc, base + k - 6)
                        if reused(k, 3, 1):
                            act.wait_ge(s_nm, base + k - 3)
                        act.sem_inc(s_tick)
                        a.activation(ETs[0:PB, s, :], mk[0:PB, s, :], ACT.Exp, bias=new_min[0:PB, q:q + 1], scale=-1.0,
                                     accum_out=den_t[0:PB, q:q + 1]).then_inc(s_num, 1)
                        a.activation(resc[0:PB, q:q + 1], NM[0:PB, bass.ds(b_, 1)], ACT.Exp, bias=new_min[0:PB, q:q + 1],
                                     scale=-1.0).then_inc(s_et, 1)
                        act.wait_ge(s_et, base + k - 2)
                        act.sem_inc(s_tick)
                        a.activation(NM[0:PB, bass.ds(b_, 1)], new_min[0:PB, q:q + 1], ACT.Copy).then_inc(s_nm, 1)
                    if live(k, 0, STEPS):
                        s = j % 4
                        act.wait_ge(s_st, base + k + 1)
                        if reused(k, 0, 4) or l:
                            act.wait_ge(s_min, base + k - 3)
                        a.activation(mpos[0:PB, s, :], ST[0:PB, s, :], ACT.Copy, bias=BIG, scale=-BIG).then_inc(s_mpos, 1)
                    if j == UN - 1 and live(k, 0, STEPS):
                        for i in range(LAG):
                            act.reg_mov(old[i], blocks[UN - LAG + i])
                for k, j in periods(act, NB, 2, 0):
                    act.wait_ge(s_self_z, l * NB + k + 1)
                    a.activation(zs[0:PB, j % 2, 0, 0:D], zs[0:PB, j % 2, 0, 0:D], ACT.Relu).then_inc(s_self_relu, 1)
                act.wait_ge(s_self_d, l + 1)
                a.activation(RS[0:PB, :], RS[0:PB, :], ACT.Exp)
                a.activation(PS_[0:PB, :], PS_[0:PB, :], ACT.Exp).then_inc(s_self_e, 1)
                act.wait_ge(s_self_w, l + 1)
                for k, j in periods(act, NB, 2, 0):
                    if reused(k, 0, 2) or l:
                        act.wait_ge(s_self_h, l * NB + k - 1)
                        act.sem_inc(s_tick)
                    a.activation(zs[0:PB, j % 2, 0, 0:D].unsqueeze(1), H[0:PB, bass.ds(k, 1), :], ACT.Copy,
                                 scale=RS[0:PB, bass.ds(k, 1)]).then_inc(s_self_t, 1)
                act.wait_ge(s_sq_in, l + 1)
                a.activation(XRn, Hn, ACT.Square).then_inc(s_sq, 1)
                act.wait_ge(s_var, 2 + l)
                a.activation(scale_row, scale_row, ACT.Sqrt, bias=eps_col[:, :], scale=1.0).then_inc(s_root, 1)
            act.wait_ge(s_var, 4)
            a.activation(col_a[0:PB, :], col_a[0:PB, :], ACT.Sqrt, bias=eps_col[0:PB, :], scale=1.0 / D).then_inc(s_root, 1)
            for k, j in periods(act, NB, 2, 0):
                s = j % 2
                act.wait_ge(s_g_tp, k + 1)
                if reused(k, 0, 2):
                    act.wait_ge(s_gate, k - 1)
                a.activation(hT[:, s, :, :], ps[:, 4 + s, 0:2 * PB].rearrange("p (c n) -> p c n", c=2), ACT.Copy).then_inc(s_g_T, 1)
            act.wait_ge(s_shift, 1)
            a.activation(probs[0:PB, :], probs[0:PB, :], ACT.Exp).then_inc(s_exp, 1)
            act.wait_ge(s_b1T, 2)
            with act.Fori(0, NX) as e:
                for f in range(FC):
                    for h, (t0, tn) in enumerate(HALVES):
                        i = 2 * f + h
                        act.wait_ge(s_up, e * 2 * FC + i + 1)
                        act.sem_inc(s_tick)
                        a.activation(hidT[:, f, t0:t0 + tn], ps[:, i % 4, 0:tn], ACT.Relu,
                                     bias=b1T[:, bass.ds(e * FC + f, 1)]).then_inc(s_hid, 1)

        @block.tensor
        def _(pe):
            t = nc.tensor
            pe.wait_ge(s_consts, 1)
            pe.wait_ge(s_edges_f, 2)
            for k in range(K7):
                mm = t.matmul(ps[0:NB - 1, k // 4, (k % 4) * P:(k % 4 + 1) * P], dst_f[:, k, P - 1:P].to_broadcast([P, NB - 1]), ident[:, :], start=True, stop=True)
            mm.then_inc(s_last, 1)
            for k in range(K7):
                mm = t.transpose(ps[:, 2 + k // 4, (k % 4) * P:(k % 4 + 1) * P], src_f[:, k, :], ident[:, :])
            mm.then_inc(s_srcT, 1)
            pe.wait_ge(s_after, 1)
            t.matmul(ps[0:1, 4, 0:STEPS], ones[0:NB - 1, 0:1], after[0:NB - 1, :], start=True, stop=True).then_inc(s_blocks, 1)

            def node_sums(srcv, n_wait):
                pe.wait_ge(s_h, n_wait)
                def one(b_, **flags):
                    return t.matmul(ps[:, 0, 0:D], ones[0:PB, :], srcv[0:PB, bass.ds(b_, 1), 0:D], **flags)
                one(0, start=True, stop=False)
                with pe.Fori(0, (NB - 2) // 4) as q:
                    for u in range(4):
                        one(q * 4 + u + 1, start=False, stop=False)
                one(NB - 1, start=False, stop=True).then_inc(s_sum, 1)

            def transposed(j, done):
                for c in range(2):
                    mm = t.transpose(ps[:, 4 + j % 2, c * PB:(c + 1) * PB],
                                     staged[0:PB, j % 2, c * P:(c + 1) * P], ident[0:PB, 0:PB])
                mm.then_inc(done, 1)

            for l in range(2):
                base = l * STEPS
                pe.wait_ge(s_feat, l + 1)
                pe.wait_ge(s_wext, l + 1)
                for k, j in periods(pe, NB, 2, 1):
                    if live(k, 0, NB):
                        if reused(k, 0, 2) or l:
                            pe.wait_ge(s_hT, l * NB + k - 1)
                        pe.wait_ge(s_staged, l * NB + k + 1)
                        transposed(j, s_tp)
                    if live(k, 1, NB):
                        s = (j - 1) % 2
                        pe.wait_ge(s_hT, l * NB + k)
                        if reused(k, 1, 2) or l:
                            pe.wait_ge(s_xl, l * NB + k - 2)
                            pe.wait_ge(s_xr, l * NB + k - 2)
                        for h in range(2):
                            for c in range(2):
                                mm = t.matmul(ps[0:PB, 2 * s + h, 0:W], hT[:, s, c, :], Wlr[:, c, h * W:(h + 1) * W], start=c == 0, stop=c == 1)
                        mm.then_inc(s_lin, 1)
                pe.wait_ge(s_we, 32 * (l + 1))
                pe.wait_ge(s_xr, NB * (l + 1))
                pe.wait_ge(s_xl, NB * (l + 1))
                pe.wait_ge(s_stairs, 1)
                blocks = None
                for k, j in periods(pe, STEPS, UN, LAG):
                    if live(k, 4, STEPS):
                        s, r = (j - 4) % 2, (j - 4) % XJ
                        pe.wait_ge(s_e, base + k - 3)
                        if reused(k, 4, 1) or l:
                            pe.wait_ge(s_acc, base + k - 4)
                        for u in range(G):
                            mm = t.matmul(ps[0:PB, 6, 0:D], Es[:, s, u, :], xj[:, r, u, 0:D], start=u == 0, stop=u == G - 1)
                        mm.then_inc(s_agg, 1)
                    if live(k, 3, STEPS):
                        s = (j - 3) % 2
                        pe.wait_ge(s_num, base + k - 2)
                        if reused(k, 3, 1) or l:
                            pe.wait_ge(s_e, base + k - 3)
                        for u in range(G):
                            mm = t.transpose(ps[:, 5, u * PB:(u + 1) * PB], ETs[0:PB, s, u * P:(u + 1) * P], ident[0:PB, 0:PB])
                        mm.then_inc(s_etT, 1)
                    if live(k, 2, STEPS):
                        s, r = (j - 2) % 2, (j - 2) % 4
                        pe.wait_ge(s_nlog, base + k - 1)
                        if reused(k, 2, 1) or l:
                            pe.wait_ge(s_tmin, base + k - 2)
                        if l == 0 and reused(k, 2, 1):
                            pe.wait_ge(s_eas, k - 2)
                        for u in range(G):
                            mm = t.matmul(ps[0:PB, 4, u * P:(u + 1) * P], nlog[:, r, u:u + 1].to_broadcast([P, PB]), ident[:, :], start=True, stop=True)
                        if l == 0:
                            pe.wait_ge(s_sT_out, k - 1)
                            for u in range(G):
                                mm = t.matmul(ps[0:PB, 4, TE:TE + 3], Srow[:, s, u, 0:PB], Srow[:, s, u, PB:P], start=u == 0, stop=u == G - 1)
                        mm.then_inc(s_lbc, 1)
                    if live(k, 0, STEPS):
                        if j == 0:
                            _, blocks = nc.values_load_multi_w_load_instructions(
                                block_of[0:1, bass.ds(k, UN)], engines=PE_ONLY, min_val=0, max_val=NB - 1,
                                skip_runtime_bounds_check_because=IN_RANGE)
                        s, r = j % 2, j % 4
                        pe.wait_ge(s_st, base + k + 1)
                        if reused(k, 0, 2) or l:
                            pe.wait_ge(s_zs, base + k - 1)
                        for u in range(G):
                            mm = t.matmul(ps[:, 2 * s + u, 0:W], ST[:, r, u * P:(u + 1) * P],
                                          XR[:, bass.ds(blocks[j], 1), :].rearrange("p o w -> p (o w)"), start=True, stop=True)
                        mm.then_inc(s_z, 1)
                    if l == 0 and live(k, 0, STEPS):
                        if reused(k, 0, 1):
                            pe.wait_ge(s_sT_out, k)
                        for u in range(G):
                            mm = t.transpose(ps[:, 7, u * P:(u + 1) * P], ST[:, j % 4, u * P:(u + 1) * P], ident[:, :])
                        mm.then_inc(s_sT, 1)
                node_sums(H, 2 * l + 1)
                pe.wait_ge(s_sq, l + 1)
                node_sums(XR, 2 * l + 2)
            pe.wait_ge(s_ln2, 1)
            pe.wait_ge(s_moe_w, 48)
            t.transpose(ps[:, 6, 0:NX * FC], b1_rows, ident[0:NX * FC, 0:NX * FC]).then_inc(s_b1T, 1)
            for k, j in periods(pe, NB, 2, 1):
                if live(k, 0, NB):
                    if reused(k, 0, 2):
                        pe.wait_ge(s_g_T, k - 1)
                    pe.wait_ge(s_staged, 2 * NB + k + 1)
                    transposed(j, s_g_tp)
                if live(k, 1, NB):
                    s = (j - 1) % 2
                    pe.wait_ge(s_g_T, k)
                    for c in range(2):
                        mm = t.matmul(ps[0:PB, 7, bass.ds((k - 1) * NX, NX)], hT[:, s, c, :], gw_sb[:, c, :], start=c == 0, stop=c == 1)
                    mm.then_inc(s_gate, 1)
            pe.wait_ge(s_onehot, 1)
            t.matmul(ps[0:PB, 0, 0:NE], triu[0:PB, 0:PB], onehot[0:PB, :], start=True, stop=True)
            t.matmul(ps[0:PB, 1, 0:NE], ones[0:PB, 0:PB], onehot[0:PB, :], start=True, stop=True).then_inc(s_cum, 1)
            pe.wait_ge(s_slots, 1)
            M = len(MT)
            with pe.Fori(0, NX // 2) as pair:
                for s in range(2):
                    e = pair * 2 + s
                    pe.wait_ge(s_tok, (e + 1) * 32)
                    for m, (m0, mn) in enumerate(MT):
                        if m >= 2:
                            pe.wait_ge(s_tokT_out, e * M + m - 1)
                        for c in range(2):
                            mm = t.transpose(ps[:, 6 + m % 2, c * P:c * P + mn], tok[0:mn, m, c * P:(c + 1) * P], ident[0:mn, 0:mn])
                        mm.then_inc(s_tokT, 1)
                    pe.wait_ge(s_tokT_out, (e + 1) * M)
                    pe.wait_ge(s_wx[s], pair * 48 + 48)
                    for f in range(FC):
                        for h, (t0, tn) in enumerate(HALVES):
                            i = 2 * f + h
                            if i >= 4:
                                pe.wait_ge(s_hid, e * 2 * FC + i - 3)
                            for c in range(2):
                                mm = t.matmul(ps[:, i % 4, 0:tn], w1_sb[:, s, c, f * P:(f + 1) * P], tokT[:, c, t0:t0 + tn], start=c == 0, stop=c == 1)
                            mm.then_inc(s_up, 1)
                    pe.wait_ge(s_hid, (e + 1) * 2 * FC)
                    for m, (m0, mn) in enumerate(MT):
                        if m >= 2:
                            pe.wait_ge(s_y, e * M + m - 1)
                        for f in range(FC):
                            mm = t.matmul(ps[0:mn, 4 + m % 2, 0:D], hidT[:, f, m0:m0 + mn], w2_sb[:, s, f, :], start=f == 0, stop=f == FC - 1)
                        mm.then_inc(s_down, 1)

        @block.vector
        def _(dve):
            v = nc.vector
            links = [0]

            def link(ins):
                links[0] += 1
                ins.then_inc(s_link, 1)
                dve.wait_ge(s_link, links[0])

            dve.wait_ge(s_pad, 2)
            v.memset(XR[96:P, :, :], 0.0)
            link(v.memset(ST[96:P, :, :], 1.0))
            v.engine_nop().then_inc(s_fixed, 1)
            v.memset(ones[:, :], 1.0)
            v.memset(eps_col[:, :], EPS)
            link(v.tensor_copy(iota_row[:, :], iota_i[:, :]))
            link(v.tensor_copy(iota_col[:, :], iota_ci[:, :]))
            v.tensor_scalar(ident[:, :], iota_row[:, :], iota_col[:, :], None, ALU.is_equal)
            link(v.tensor_scalar(node_id[:, :], iota_row[:, 0:NB], float(PB), iota_col[:, :], ALU.mult, ALU.add))
            v.engine_nop().then_inc(s_consts, 1)
            dve.wait_ge(s_edges, 16 * 9)
            v.tensor_copy(src_f, src_i)
            v.tensor_copy(dst_f, dst_i).then_inc(s_edges_f, 1)
            v.tensor_copy(ea_pl.rearrange("p k j e -> p k e j"), ea_in).then_inc(s_edges_f, 1)
            dve.wait_ge(s_srcT, 1)
            v.tensor_copy(src_cols[:, 0:512], ps[:, 2, :])
            v.tensor_copy(src_cols[:, 512:K7 * P], ps[:, 3, 0:K7 * P - 512]).then_inc(s_srcT_out, 1)
            dve.wait_ge(s_last, 1)
            q = NB - 1
            v.tensor_copy(last_dst[0:q, 0:512], ps[0:q, 0, :])
            link(v.tensor_copy(last_dst[0:q, 512:K7 * P], ps[0:q, 1, 0:K7 * P - 512]))
            link(v.tensor_scalar(tau[0:q, 0:1], iota_col[0:q, :], float(PB), float(PB), ALU.mult, ALU.add))
            link(v.tensor_scalar(reached[0:q, 0:T - 1], last_dst[0:q, 1:2 * (T - 1):2], tau[0:q, 0:1], None, ALU.is_lt))
            link(v.tensor_reduce(tau[0:q, 1:2], reached[0:q, 0:T - 1], AX_X, ALU.add))
            link(v.tensor_scalar(tau[0:q, 1:2], tau[0:q, 1:2], iota_col[0:q, :], 1.0, ALU.add, ALU.add))
            link(v.tensor_copy(step_iota, step_iota_i))
            v.tensor_scalar(after[0:q, :], step_iota[0:q, :], tau[0:q, 1:2], None, ALU.is_ge).then_inc(s_after, 1)
            dve.wait_ge(s_blocks, 1)
            link(v.tensor_copy(block_f[0:1, :], ps[0:1, 4, 0:STEPS]))
            v.tensor_copy(block_of[:, :], block_f[0:1, :])
            link(v.tensor_tensor(step_iota[0:1, :], step_iota[0:1, :], block_f[0:1, :], ALU.subtract))
            v.tensor_copy(tile_of[:, :], step_iota[0:1, :]).then_inc(s_stairs, 1)

            def wide(col):
                return col[0:PB, :].unsqueeze(2).to_broadcast([PB, NB, D])

            def over(row):
                return row[0:PB, :].unsqueeze(1).to_broadcast([PB, NB, D])

            def layer_norm(srcv, dstv, tmp, mean, rstd, n):
                link(v.tensor_reduce(mean[0:PB, :], srcv, AX_X, ALU.add))
                link(v.tensor_scalar(mean[0:PB, :], mean[0:PB, :], 1.0 / D, None, ALU.mult))
                link(v.tensor_tensor(dstv, srcv, wide(mean), ALU.subtract))
                link(v.tensor_tensor(tmp, dstv, dstv, ALU.mult))
                v.tensor_reduce(col_a[0:PB, :], tmp, AX_X, ALU.add).then_inc(s_var, 1)
                dve.wait_ge(s_root, n)
                link(v.reciprocal(rstd[0:PB, :], rstd[0:PB, :]))
                link(v.tensor_tensor(dstv, dstv, wide(rstd), ALU.mult))

            dve.wait_ge(s_x, 32)
            layer_norm(Hn, Hn, XRn, ln_mean, ln_rstd, 1)
            v.engine_nop().then_inc(s_feat, 1)

            for l in range(2):
                base = l * STEPS
                dve.wait_ge(s_w, 16 * 8 * (l + 1))
                v.tensor_scalar(att_lin[:, :], att_relu[:, :], -0.2, None, ALU.mult)
                link(v.tensor_scalar(att_relu[:, :], att_relu[:, :], -0.8, None, ALU.mult))
                for view in (Wlr[:, 0, 0:W], Wlr[:, 0, W:2 * W], Wlr[:, 1, 0:W], Wlr[:, 1, W:2 * W], WeB[:, 0, :], WeB[:, 1, :]):
                    ins = v.tensor_tensor_reduce(junk[:, 0:D], view[:, 0:D], att_lin[:, :], 1.0, 0.0, ALU.mult, ALU.add, view[:, D:D + 1])
                    link(ins)
                v.engine_nop().then_inc(s_wext, 1)
                for k, j in periods(dve, NB, 2, 0):
                    dve.wait_ge(s_lin, l * NB + k + 1)
                    v.tensor_copy(XR[0:PB, bass.ds(k, 1), :], ps[0:PB, 2 * (j % 2) + 1:2 * (j % 2) + 2, 0:W]).then_inc(s_xr, 1)
                v.memset(Hn, 0.0)
                v.memset(NM[:, :], START)
                v.memset(DEN[:, :], 0.0)
                if l == 0:
                    v.memset(EAS[:, :, :], 0.0)
                v.engine_nop().then_inc(s_state, 1)
                dve.wait_ge(s_state, l + 1)
                dve.wait_ge(s_stairs, 1)
                old = [dve.alloc_register(f"old_block{l}_{i}") for i in range(LAG)]
                blocks = held = None
                for k, j in periods(dve, STEPS, UN, LAG):
                    if j == 0:
                        held = [dve.snap(r, min_val=0, max_val=NB - 1) for r in old] if not (isinstance(k, int) and k == 0) else None
                        if live(k, 0, STEPS):
                            _, blocks = nc.values_load_multi_w_load_instructions(
                                block_of[0:1, bass.ds(k, UN)], engines=DVE_ONLY, min_val=0, max_val=NB - 1,
                                skip_runtime_bounds_check_because=IN_RANGE)

                    def block_at(lag):
                        return blocks[j - lag] if j >= lag else held[LAG + j - lag]

                    if live(k, 5, STEPS):
                        r = (j - 5) % 4
                        b_ = block_at(5)
                        dve.wait_ge(s_agg, base + k - 4)
                        dve.wait_ge(s_et, base + k - 4)
                        if reused(k, 5, 1):
                            dve.wait_ge(s_acc, base + k - 5)
                        dve.sem_inc(s_tick)
                        v.scalar_tensor_tensor(H[0:PB, bass.ds(b_, 1), :].rearrange("p o d -> p (o d)"), H[0:PB, bass.ds(b_, 1), :].rearrange("p o d -> p (o d)"),
                                               resc[0:PB, r:r + 1], ps[0:PB, 6, 0:D], ALU.mult, ALU.add)
                        v.scalar_tensor_tensor(DEN[0:PB, bass.ds(b_, 1)], DEN[0:PB, bass.ds(b_, 1)], resc[0:PB, r:r + 1],
                                               den_t[0:PB, r:r + 1], ALU.mult, ALU.add).then_inc(s_acc, 1)
                    if live(k, 3, STEPS):
                        s, r = (j - 3) % 2, (j - 3) % 4
                        dve.wait_ge(s_lbc, base + k - 2)
                        dve.wait_ge(s_mpos, base + k - 2)
                        if reused(k, 3, 2) or l:
                            dve.wait_ge(s_num, base + k - 4)
                        b_ = block_at(3)
                        if l == 0 and reused(k, 3, 1):
                            dve.wait_ge(s_eas, k - 3)
                        dve.sem_inc(s_tick)
                        if l == 0:
                            v.tensor_tensor(EAS[0:PB, bass.ds(b_, 1), :], EAS[0:PB, bass.ds(b_, 1), :],
                                            ps[0:PB, 4, TE:TE + 3].unsqueeze(1), ALU.add).then_inc(s_eas, 1)
                        v.tensor_tensor_reduce(mk[0:PB, s, :], mpos[0:PB, r, :], ps[0:PB, 4, 0:TE], 1.0, 4.0 * BIG,
                                               ALU.add, ALU.min, tmin[0:PB, r:r + 1]).then_inc(s_tmin, 1)

                    def weighted(u):
                        s, r = (j - 2) % 2, (j - 2) % 4
                        return v.tensor_tensor_reduce(zs[:, s, u, 0:D], zs[:, s, u, 0:D], att_relu[:, :], 1.0, zs[:, s, u, D:W],
                                                      ALU.mult, ALU.add, nlog[:, r, u:u + 1])

                    if live(k, 2, STEPS):
                        dve.wait_ge(s_relu, base + k - 1)
                        if reused(k, 2, 4) or l:
                            dve.wait_ge(s_lbc, base + k - 5)
                        weighted(0)
                    if live(k, 3, STEPS):
                        r = (j - 3) % 4
                        dve.wait_ge(s_tmin, base + k - 2)
                        if reused(k, 3, 1) or l:
                            dve.wait_ge(s_nm, base + k - 3)
                        if reused(k, 3, 4) or l:
                            dve.wait_ge(s_et, base + k - 6)
                        dve.sem_inc(s_tick)
                        v.tensor_scalar(new_min[0:PB, r:r + 1], tmin[0:PB, r:r + 1], NM[0:PB, bass.ds(block_at(3), 1)], None, ALU.min).then_inc(s_min, 1)
                    if live(k, 0, STEPS):
                        s = j % 4
                        dve.wait_ge(s_row[s], (base + k - s) // 4 * 32 + 32 if isinstance(k, int) else (base // 4 + 1) * 32 + (k - s) * 8)
                        if reused(k, 0, 4) or l:
                            dve.wait_ge(s_mpos, base + k - 3)
                        v.tensor_scalar(ST[0:PB, s, :], dst_b[0:PB, s, :], node_id[0:PB, bass.ds(block_at(0), 1)], None, ALU.is_equal).then_inc(s_st, 1)
                    if live(k, 2, STEPS):
                        weighted(1).then_inc(s_nlog, 1)
                    if live(k, 1, STEPS):
                        s, r = (j - 1) % 2, (j - 1) % XJ
                        dve.wait_ge(s_z, base + k)
                        kk = k - 1
                        dve.wait_ge(s_xj[r], (base + kk - r) // XJ * 32 + 32 if isinstance(k, int) else (base // XJ + 1) * 32 + (kk - r) * (32 // XJ))
                        if reused(k, 1, 2) or l:
                            dve.wait_ge(s_nlog, base + k - 2)
                        v.tensor_tensor(zs[:, s, :, :], xj[:, r, :, :], ps[:, 2 * s:2 * s + 2, 0:W], ALU.add).then_inc(s_zs, 1)
                    if j == UN - 1 and live(k, 0, STEPS):
                        for i in range(LAG):
                            dve.reg_mov(old[i], blocks[UN - LAG + i])
                dve.wait_ge(s_acc, base + STEPS)
                dve.wait_ge(s_nm, base + STEPS)
                if l == 0:
                    link(v.tensor_scalar(col_a[0:PB, :], EAS[0:PB, :, 2], 1.0, None, ALU.max))
                    link(v.reciprocal(col_a[0:PB, :], col_a[0:PB, :]))
                    for i in range(2):
                        link(v.tensor_tensor(ME[0:PB, i, :], EAS[0:PB, :, i], col_a[0:PB, :], ALU.mult))
                for k, j in periods(dve, NB, 2, 1):
                    if live(k, 0, NB):
                        s = j % 2
                        zz = zs[0:PB, s, 0, :]
                        if reused(k, 0, 2):
                            dve.wait_ge(s_self_l, (l * NB + k - 1))
                        v.tensor_tensor(zz.unsqueeze(1), XL[0:PB, bass.ds(k, 1), :], XR[0:PB, bass.ds(k, 1), :], ALU.add).then_inc(s_self_a, 1)
                        for i in range(2):
                            dve.wait_ge(s_self_a, (l * NB + k) * 2 + i + 1)
                            v.scalar_tensor_tensor(zz, WeB[0:PB, i, :], ME[0:PB, i, bass.ds(k, 1)], zz, ALU.mult, ALU.add).then_inc(s_self_a if i == 0 else s_self_z, 1)
                    if live(k, 1, NB):
                        s = (j - 1) % 2
                        dve.wait_ge(s_self_relu, l * NB + k)
                        if reused(k, 1, 1) or l:
                            dve.wait_ge(s_self_l, l * NB + k - 1)
                        v.tensor_tensor_reduce(zs[0:PB, s, 0, 0:D], zs[0:PB, s, 0, 0:D], att_relu[0:PB, :], 1.0, zs[0:PB, s, 0, D:W],
                                               ALU.mult, ALU.add, ls_slot[0:PB, s:s + 1]).then_inc(s_self_q, 1)
                        dve.wait_ge(s_self_q, l * NB + k)
                        v.tensor_copy(LS[0:PB, bass.ds(k - 1, 1)], ls_slot[0:PB, s:s + 1]).then_inc(s_self_l, 1)
                dve.wait_ge(s_self_l, NB * (l + 1))
                link(v.tensor_tensor(col_a[0:PB, :], NM[0:PB, :], LS[0:PB, :], ALU.min))
                v.tensor_tensor(RS[0:PB, :], col_a[0:PB, :], NM[0:PB, :], ALU.subtract)
                v.tensor_tensor(PS_[0:PB, :], col_a[0:PB, :], LS[0:PB, :], ALU.subtract).then_inc(s_self_d, 1)
                dve.wait_ge(s_self_e, l + 1)
                link(v.tensor_tensor(DEN[0:PB, :], DEN[0:PB, :], RS[0:PB, :], ALU.mult))
                link(v.tensor_tensor(DEN[0:PB, :], DEN[0:PB, :], PS_[0:PB, :], ALU.add))
                link(v.reciprocal(DEN[0:PB, :], DEN[0:PB, :]))
                v.tensor_tensor(RS[0:PB, :], RS[0:PB, :], DEN[0:PB, :], ALU.mult)
                link(v.tensor_tensor(PS_[0:PB, :], PS_[0:PB, :], DEN[0:PB, :], ALU.mult))
                v.engine_nop().then_inc(s_self_w, 1)
                for k, j in periods(dve, NB, 2, 0):
                    dve.wait_ge(s_self_t, l * NB + k + 1)
                    v.scalar_tensor_tensor(H[0:PB, bass.ds(k, 1), :].rearrange("p o d -> p (o d)"), XL[0:PB, bass.ds(k, 1), 0:D].rearrange("p o d -> p (o d)"),
                                           PS_[0:PB, bass.ds(k, 1)], zs[0:PB, j % 2, 0, 0:D], ALU.mult, ALU.add).then_inc(s_self_h, 1)
                dve.wait_ge(s_self_h, NB * (l + 1))
                v.tensor_tensor(Hn, Hn, over(rows[:, 0, :]), ALU.add).then_inc(s_h, 1)
                dve.wait_ge(s_sum, 2 * l + 1)
                link(v.tensor_scalar(mu, ps[:, 0, 0:D], 1.0 / N, None, ALU.mult))
                v.tensor_tensor(Hn, Hn, over(mu), ALU.subtract).then_inc(s_sq_in, 1)
                dve.wait_ge(s_sq_in, l + 1)
                v.engine_nop().then_inc(s_h, 1)
                dve.wait_ge(s_sum, 2 * l + 2)
                v.tensor_scalar(scale_row, ps[:, 0, 0:D], 1.0 / N, None, ALU.mult).then_inc(s_var, 1)
                dve.wait_ge(s_root, 2 + l)
                link(v.reciprocal(scale_row, scale_row))
                link(v.tensor_tensor(scale_row, scale_row, rows[:, 1, :], ALU.mult))
                link(v.tensor_tensor(Hn, Hn, over(scale_row), ALU.mult))
                link(v.tensor_tensor(Hn, Hn, over(rows[:, 2, :]), ALU.add))
                if l == 1:
                    dve.wait_ge(s_x2, 32)
                    link(v.tensor_tensor(XRn, XLn, wide(ln_mean), ALU.subtract))
                    link(v.tensor_tensor(XRn, XRn, wide(ln_rstd), ALU.mult))
                    link(v.tensor_tensor(Hn, Hn, XRn, ALU.add))
                link(v.tensor_scalar(XRn, Hn, 0.0, slope[0:PB, :], ALU.min, ALU.mult))
                link(v.tensor_scalar(Hn, Hn, 0.0, None, ALU.max))
                link(v.tensor_tensor(Hn, Hn, XRn, ALU.add))
                if l == 0:
                    v.engine_nop().then_inc(s_feat, 1)
            link(v.tensor_tensor(Hn, Hn, XLn, ALU.add))
            layer_norm(Hn, XLn, XRn, ln_mean, col_a, 4)
            v.engine_nop().then_inc(s_ln2, 1)
            v.memset(zero_rows, 0.0).then_inc(s_zero_src, 1)
            v.tensor_scalar(triu[0:PB, 0:PB], iota_row[0:PB, 0:PB], iota_col[0:PB, :], None, ALU.is_ge)
            v.tensor_scalar(e_off, iota_row[:, 0:NX], -float(NX), None, ALU.add)
            link(v.memset(chain_mask, 1.0))
            link(v.memset(chain_mask.rearrange("p (e b) -> p e b", e=NX)[:, :, 0:1], 0.0))
            dve.wait_ge(s_b1T, 1)
            v.tensor_copy(b1T[:, :], ps[:, 6, 0:NX * FC]).then_inc(s_b1T, 1)
            dve.wait_ge(s_gate, NB)

            def per_b(col):
                return col[0:PB, :].unsqueeze(2).to_broadcast([PB, NB, NX])

            def per_e(row):
                return row[0:PB, :].unsqueeze(1).to_broadcast([PB, NB, NX])

            n = PB
            pr, oh = be(probs[0:n]), be(onehot[0:n])
            link(v.tensor_tensor(pr, be(ps[0:n, 7, 0:NE]), per_e(gb_sb), ALU.add))
            link(v.tensor_reduce(top[0:n], pr, AX_X, ALU.max))
            v.tensor_tensor(pr, pr, per_b(top), ALU.subtract).then_inc(s_shift, 1)
            dve.wait_ge(s_exp, 1)
            link(v.tensor_reduce(top[0:n], pr, AX_X, ALU.add))
            link(v.reciprocal(top[0:n], top[0:n]))
            link(v.tensor_tensor(pr, pr, per_b(top), ALU.mult))
            link(v.tensor_reduce(top[0:n], pr, AX_X, ALU.max))
            link(v.tensor_tensor(oh, pr, per_b(top), ALU.is_ge))
            link(v.tensor_tensor(oh, oh, per_e(e_off), ALU.mult))
            link(v.tensor_reduce(first_e[0:n], oh, AX_X, ALU.min))
            v.tensor_tensor(oh, per_e(e_off), per_b(first_e), ALU.is_equal).then_inc(s_onehot, 1)
            dve.wait_ge(s_cum, 1)
            tot_v = tot_eb[0:n].rearrange("p (e b) -> p b e", e=NX)
            link(v.tensor_copy(tot_v, be(ps[0:n, 1, 0:NE])))
            link(v.tensor_tensor_scan(base_eb[0:n], chain_mask[0:n], tot_eb[0:n], 0.0, ALU.mult, ALU.add))
            link(v.tensor_tensor(base_eb[0:n], base_eb[0:n], tot_eb[0:n], ALU.subtract))
            link(v.tensor_tensor(be(cum[0:n]), be(ps[0:n, 0, 0:NE]), base_eb[0:n].rearrange("p (e b) -> p b e", e=NX), ALU.add))
            link(v.tensor_tensor(be(cum[0:n]), be(cum[0:n]), oh, ALU.mult))
            link(v.tensor_reduce(pos[0:n], be(cum[0:n]), AX_X, ALU.add))
            link(v.tensor_scalar(pos[0:n], pos[0:n], -1.0, None, ALU.add))
            link(v.tensor_scalar(kept[0:n], pos[0:n], float(CAP), None, ALU.is_lt))
            link(v.tensor_tensor(coef[0:n], top[0:n], kept[0:n], ALU.mult))
            link(v.tensor_scalar(first_e[0:n], first_e[0:n], float(NX), float(CAP), ALU.add, ALU.mult))
            link(v.tensor_tensor(slot_f[0:n], first_e[0:n], pos[0:n], ALU.add))
            link(v.tensor_scalar(slot_f[0:n], slot_f[0:n], -float(NX * CAP), None, ALU.add))
            link(v.tensor_tensor(slot_f[0:n], slot_f[0:n], node_id[0:n, :], ALU.subtract))
            link(v.tensor_tensor(slot_f[0:n], slot_f[0:n], kept[0:n], ALU.mult))
            link(v.tensor_tensor(slot_f[0:n], slot_f[0:n], node_id[0:n, :], ALU.add))
            link(v.tensor_scalar(slot_f[0:n], slot_f[0:n], float(NX * CAP), None, ALU.add))
            link(v.tensor_copy(slot_put[0:n], slot_f[0:n]))
            link(v.tensor_scalar(pos[0:n], pos[0:n], float(CAP - 1), None, ALU.min))
            link(v.tensor_tensor(slot_f[0:n], first_e[0:n], pos[0:n], ALU.add))
            link(v.tensor_copy(slot_get[0:n], slot_f[0:n]))
            v.engine_nop().then_inc(s_slots, 1)
            M = len(MT)
            dve.wait_ge(s_put, 16 * NB)
            with dve.Fori(0, NX // 2) as pair:
                for s in range(2):
                    e = pair * 2 + s
                    for m, (m0, mn) in enumerate(MT):
                        dve.wait_ge(s_tokT, e * M + m + 1)
                        v.tensor_copy(tokT[:, :, m0:m0 + mn], ps[:, 6 + m % 2, 0:D].rearrange("p (c t) -> p c t", c=2)[:, :, 0:mn]).then_inc(s_tokT_out, 1)
                    for m, (m0, mn) in enumerate(MT):
                        dve.wait_ge(s_down, e * M + m + 1)
                        if m == 0:
                            dve.wait_ge(s_y_out, e * 32)
                            dve.wait_ge(s_wx[s], pair * 48 + 48)
                        v.tensor_tensor(y_sb[0:mn, m, :], ps[0:mn, 4 + m % 2, 0:D], b2B[0:mn, s * D:(s + 1) * D], ALU.add).then_inc(s_y, 1)
            dve.wait_ge(s_get, 16 * NB)
            link(v.tensor_tensor(XLn, XLn, wide(coef), ALU.mult))
            FMAX = 3.4028234663852886e38
            half = NB // 2
            cells = half * D
            for h in range(2):
                y = XL[0:PB, h * half:(h + 1) * half, 0:D]
                mask = XRf[0:PB, 0:cells].bitcast(I32).rearrange("p (b d) -> p b d", b=half)
                clean = XRf[0:PB, cells:2 * cells].rearrange("p (b d) -> p b d", b=half)
                link(v.memset(clean, 0.0))
                link(v.tensor_tensor(mask, y, y, ALU.is_equal))
                link(v.copy_predicated(clean, mask, y))
                for op, bound, value in ((ALU.is_gt, FMAX, 1.0e4), (ALU.is_lt, -FMAX, -1.0e4)):
                    link(v.memset(junk[:, 0:1], value))
                    link(v.tensor_scalar(mask, y, bound, None, op))
                    link(v.copy_predicated(clean, mask, junk[0:PB, 0:1].unsqueeze(1).to_broadcast([PB, half, D])))
                link(v.tensor_tensor(H[0:PB, h * half:(h + 1) * half, :], H[0:PB, h * half:(h + 1) * half, :], clean, ALU.add))
            v.engine_nop().then_inc(s_fin, 1)


_INS = ["x", "src", "dst", "edge_attr_2"]
_LAYER = ["Wl", "Wr", "We", "att", "b", "g", "beta", "a"]
_FFN = ["gate_w", "gate_b", "w1", "b1", "w2", "b2"]


def kernel(**inputs):
    import numpy as np
    import concourse.bacc as bacc
    from concourse.bass_utils import run_bass_kernel_spmd as run

    nc = bacc.Bacc("TRN2", target_bir_lowering=False, num_devices=1, dynamic_dma_scratch_size=8192)
    arrays = {}

    def given(name):
        a = np.ascontiguousarray(inputs[name])
        if a.ndim == 0:
            a = a.reshape(1)
        arrays["in_" + name] = a
        return nc.dram_tensor("in_" + name, a.shape, mybir.dt.from_np(a.dtype), kind="ExternalInput").ap()

    ins = [given(n) for n in _INS]
    layers = [[given(f"L0_gnn_{n}{l}") for n in _LAYER] for l in (1, 2)]
    ffn = [given("L0_ffn_" + n) for n in _FFN]
    out = nc.dram_tensor("out_0", inputs["x"].shape, F32, kind="ExternalOutput").ap()
    program(nc, *ins, layers, *ffn, out)
    return run(nc, [arrays], core_ids=[0]).results[0]["out_0"]
```

```python
from contextlib import ExitStack

import concourse.bass as bass
from concourse import mybir

ALU = mybir.AluOpType
ACT = mybir.ActivationFunctionType
AX_X = mybir.AxisListType.X
F32 = mybir.dt.float32
I32 = mybir.dt.int32
DVE_ONLY = (mybir.EngineType.DVE,)
ACT_ONLY = (mybir.EngineType.Activation,)
PE_ONLY = (mybir.EngineType.PE,)
POOL_ONLY = (mybir.EngineType.Pool,)
SP_ONLY = (mybir.EngineType.SP,)

BIG = 1.0e30
START = 1.0e29
EPS = 1e-5
PAD_DST = 1000000
IN_RANGE = "the staircase table holds block and tile numbers, which the chip works out in range"


def periods(engine, steps, unroll, lag):
    for k in range(unroll):
        yield k, k
    with engine.Fori(1, steps // unroll) as turn:
        for j in range(unroll):
            yield turn * unroll + j, j
    for k in range(steps, steps + lag):
        yield k, k % unroll


def live(k, lag, steps):
    return not isinstance(k, int) or 0 <= k - lag < steps


def reused(k, lag, ring):
    return not isinstance(k, int) or k - lag >= ring


def program(nc, x, src, dst, ea, layers, gate_w, gate_b, w1, b1, w2, b2, out):
    N, D = x.shape
    E = src.shape[0]
    NX, C_OUT = gate_w.shape[1], w1.shape[2]
    P = 128
    PB = 125
    NB = N // PB
    assert NB * PB == N and D == 256
    G = 2
    TE = G * P
    T = -(-E // TE)
    ROWS = T * G
    FULL = E // P
    REST = E - FULL * P
    K7 = -(-ROWS // P)
    LASTK = ROWS - (K7 - 1) * P
    STEPS = T + NB - 1
    W = D + 1
    UN = 8
    LAG = 5
    assert STEPS % UN == 0
    CAP = -(-5 * N // (4 * NX))
    HC = -(-CAP // 2)
    HALVES = [(0, HC), (HC, CAP - HC)]
    MT = [(m, min(P, CAP - m)) for m in range(0, CAP, P)]
    FC = C_OUT // P
    CH = 5
    CB = NB // CH
    assert CH * CB == NB
    SL = 5
    assert NB % SL == 0 and CB % 2 == 0

    SC = E // PB
    assert SC * PB == E
    NPAD = ROWS * P - E
    assert NPAD <= P

    sorted_edges = nc.dram_tensor("sorted_edges", (ROWS * P, 4), F32, kind="Internal").ap()
    dst_rows = nc.dram_tensor("dst_rows", (ROWS * P,), F32, kind="Internal").ap()
    ea_rows = nc.dram_tensor("ea_rows", (2, ROWS * P), F32, kind="Internal").ap()
    xl_table = [nc.dram_tensor(f"xl_table{l}", (N, W), F32, kind="Internal").ap() for l in range(2)]
    tok_buf = nc.dram_tensor("tok_buf", (NX * CAP + N, D), F32, kind="Internal").ap()
    me_rows = nc.dram_tensor("me_rows", (2, N), F32, kind="Internal").ap()
    y_buf = nc.dram_tensor("y_buf", (NX * CAP, D), F32, kind="Internal").ap()

    with ExitStack() as ctx:
        def sb(name, shape, dt=F32):
            return ctx.enter_context(nc.sbuf_tensor(name, shape, dt))

        def sem(name):
            return ctx.enter_context(nc.semaphore(name))

        H = sb("H", [P, NB, D])
        XR = sb("XR", [P, NB, W])
        XL = sb("XL", [P, NB, W])
        Hn, XRn, XLn = H[0:PB], XR[0:PB, :, 0:D], XL[0:PB, :, 0:D]
        XLf = XL[:, :, :].rearrange("p b w -> p (b w)")
        XRf = XR[:, :, :].rearrange("p b w -> p (b w)")
        ps = ctx.enter_context(nc.psum_tensor("ps", [P, 8, 512], F32))

        ident = sb("ident", [P, P])
        ones = sb("ones", [P, P])
        iota_i = sb("iota_i", [P, P], I32)
        iota_ci = sb("iota_ci", [P, 1], I32)
        iota_row = sb("iota_row", [P, P])
        iota_col = sb("iota_col", [P, 1])
        node_id = sb("node_id", [P, NB])
        eps_col = sb("eps_col", [P, 1])
        src_cols = sb("src_cols", [P, K7 * P], I32)
        block_of = sb("block_of", [1, STEPS], I32)
        tile_of = sb("tile_of", [1, STEPS], I32)

        Wlr = sb("Wlr", [P, 2, 2 * W])
        WeB = sb("WeB", [P, 2, W])
        att_relu = sb("att_relu", [P, D])
        att_lin = sb("att_lin", [P, D])
        rows = sb("rows", [P, 3, D])
        slope = sb("slope", [P, 1])
        junk = sb("junk", [P, W])
        ln_mean = sb("ln_mean", [P, NB])
        ln_rstd = sb("ln_rstd", [P, NB])
        col_a = sb("col_a", [P, NB])
        slope_1 = sb("slope_1", [P, 1])

        XJ = 8
        xj = sb("xj", [P, XJ, G, W])
        dst_b = sb("dst_b", [P, 4, TE])
        ST = sb("ST", [P, 4, TE])
        mpos = sb("mpos", [P, 4, TE])
        zs = sb("zs", [P, 2, G, W])
        mu, scale_row = zs[:, 0, 0, 0:D], zs[:, 0, 1, 0:D]
        mk = sb("mk", [P, 2, TE])
        ETs = sb("ETs", [P, 2, TE])
        Es = sb("Es", [P, 2, G, PB])
        staged = mk
        hT = Es
        Srow = sb("Srow", [P, 2, G, P])
        src_slot = sb("src_slot", [P, XJ, G], I32)
        nlog = sb("nlog", [P, 4, G])
        tmin = sb("tmin", [P, 4])
        new_min = sb("new_min", [P, 4])
        resc = sb("resc", [P, 4])
        den_t = sb("den_t", [P, 4])
        NM = sb("NM", [P, NB])
        DEN = sb("DEN", [P, NB])
        EAS = sb("EAS", [P, NB, 3])
        ME = sb("ME", [P, 2, NB])
        LS = sb("LS", [P, NB])
        RS = sb("RS", [P, NB])
        PS_ = sb("PS_", [P, NB])
        ls_slot = sb("ls_slot", [P, SL])
        STf = ST[:, :, :].rearrange("p s e -> p (s e)")
        eye = [STf[:, i * PB:(i + 1) * PB] for i in range(SL)]
        ME_T = Srow[0:2 * NB, 0, 0, 0:PB]
        bad = sb("bad", [P, 1])
        not_finite = sb("not_finite", [1, 1], I32)

        unsorted_f = sb("unsorted_f", [P, 1])
        unsorted = sb("unsorted", [1, 1], I32)
        place_f = sb("place_f", [P, 1])
        place = sb("place", [P, 1], I32)
        edge_slot = sb("edge_slot", [P, 4])

        o = 0
        def carve(base, n, dt=F32):
            nonlocal o
            v = base[:, o:o + n]
            o += n
            return v if dt == F32 else v.bitcast(dt)
        src_i = carve(XLf, K7 * P, I32).rearrange("p (k e) -> p k e", k=K7)
        dst_i = carve(XLf, K7 * P, I32).rearrange("p (k e) -> p k e", k=K7)
        src_f = carve(XLf, K7 * P).rearrange("p (k e) -> p k e", k=K7)
        dst_f = carve(XLf, K7 * P).rearrange("p (k e) -> p k e", k=K7)
        ea_in = carve(XLf, 2 * K7 * P).rearrange("p (k e j) -> p k e j", k=K7, j=2)
        loaded_edges = XLf[:, o:o + 4 * K7 * P].rearrange("p (k e f) -> p k e f", k=K7, f=4)
        ea_pl = carve(XLf, 2 * K7 * P).rearrange("p (k j e) -> p k j e", k=K7, j=2)
        last_dst = carve(XLf, K7 * P)
        reached = carve(XLf, 512)
        after = carve(XLf, STEPS)
        step_iota = carve(XLf, STEPS)
        step_iota_i = carve(XLf, STEPS, I32)
        block_f = carve(XLf, STEPS)
        tau = carve(XLf, 2)
        dst_s = carve(XLf, SC + 1, I32)
        descents = carve(XLf, SC)
        o = 0
        src_s = carve(XRf, SC, I32)
        ea_s = carve(XRf, 2 * SC).rearrange("p (c j) -> p c j", j=2)
        edge_s = carve(XRf, 4 * SC).rearrange("p (c f) -> p c f", f=4)
        edge_dst = carve(XRf, SC)
        block_start = carve(XRf, NB + 1)
        beyond = carve(XRf, NB + 1)
        is_beyond = carve(XRf, NB + 1)
        in_block = carve(XRf, NB)
        places = carve(XRf, NB)
        place_of = carve(XRf, NB)
        before = carve(XRf, PB)
        pad_edge = carve(XRf, 4)

        o = 0
        w1_sb = carve(XRf, 2 * 2 * C_OUT).rearrange("p (s c f) -> p s c f", s=2, c=2)
        w2_sb = carve(XRf, 2 * FC * D).rearrange("p (s f d) -> p s f d", s=2, f=FC)
        tok = carve(XRf, len(MT) * D).rearrange("p (m d) -> p m d", m=len(MT))
        y_sb = carve(XRf, len(MT) * D).rearrange("p (m d) -> p m d", m=len(MT))
        o = 0
        tokT = carve(XLf, 2 * CAP).rearrange("p (c t) -> p c t", c=2)
        hidT = carve(XLf, FC * CAP).rearrange("p (f t) -> p f t", f=FC)
        o = 0
        xjf = xj[:, :, :, :].rearrange("p s g w -> p (s g w)")
        NE = NB * NX
        def be(v):
            return v.rearrange("p (b e) -> p b e", e=NX)
        probs, onehot, cum, base_eb, tot_eb, chain_mask = (carve(xjf, NE) for _ in range(6))
        stats = carve(xjf, NB * 6).rearrange("p (b s) -> p b s", s=6)
        y_zero = carve(xjf, len(MT))
        y_zeros = carve(xjf, len(MT))
        o = 0
        zf = zs[:, :, :, :].rearrange("p s g w -> p (s g w)")
        gw_sb = carve(zf, 2 * NX).rearrange("p (c e) -> p c e", c=2)
        gb_sb = carve(zf, NX)
        e_off = carve(zf, NX)
        top, first_e, pos, kept, slot_f, coef = (carve(zf, NB) for _ in range(6))
        slot_put = carve(zf, NB, I32)
        slot_get = carve(zf, NB, I32)
        triu = Srow[:, 0, 0, :]
        b1_rows = ETs[0:NX * FC, 0, 0:P]
        b1T = sb("b1T", [P, NX * FC])
        b2B = Wlr[:, :, :].rearrange("p c w -> p (c w)")
        zero_rows = mpos[:, 0, :]

        s_pad = sem("s_pad")
        s_fixed = sem("s_fixed")
        s_edges = sem("s_edges")
        s_dst_s = sem("s_dst_s")
        s_descents = sem("s_descents")
        s_descents_sum = sem("s_descents_sum")
        s_flag = sem("s_flag")
        s_sort_in = sem("s_sort_in")
        s_sort_pad = sem("s_sort_pad")
        s_sort_link = sem("s_sort_link")
        s_sort_total = sem("s_sort_total")
        s_sort_rank = sem("s_sort_rank")
        s_sort_slot = sem("s_sort_slot")
        s_sort_put = sem("s_sort_put")
        s_sort_pads = sem("s_sort_pads")
        s_sort_back = sem("s_sort_back")
        s_edges_f = sem("s_edges_f")
        s_edges_out = sem("s_edges_out")
        s_consts = sem("s_consts")
        s_last = sem("s_last")
        s_srcT = sem("s_srcT")
        s_srcT_out = sem("s_srcT_out")
        s_after = sem("s_after")
        s_blocks = sem("s_blocks")
        s_stairs = sem("s_stairs")
        s_x = sem("s_x")
        s_var = sem("s_var")
        s_root = sem("s_root")
        s_w = sem("s_w")
        s_wext = sem("s_wext")
        s_we = sem("s_we")
        s_feat = sem("s_feat")
        s_rows = sem("s_rows")
        s_me = sem("s_me")
        s_me_T = sem("s_me_T")
        s_me_T_out = sem("s_me_T_out")
        s_me_rows = sem("s_me_rows")
        s_eye = sem("s_eye")
        s_eye_me = [sem(f"s_eye_me{i}") for i in range(SL)]
        s_self_mm = sem("s_self_mm")
        s_staged = sem("s_staged")
        s_tp, s_hT, s_lin, s_xr, s_xl = (sem(n) for n in ("s_tp", "s_hT", "s_lin", "s_xr", "s_xl"))
        s_table = sem("s_table")
        s_state = sem("s_state")
        s_row = [sem(f"s_row{i}") for i in range(4)]
        s_xj = [sem(f"s_xj{i}") for i in range(XJ)]
        s_idx = sem("s_idx")
        s_tick = sem("s_tick")
        s_st, s_z, s_mpos, s_zs, s_relu, s_nlog, s_lbc, s_min, s_et, s_etT, s_e, s_agg, s_acc = (
            sem(n) for n in ("s_st", "s_z", "s_mpos", "s_zs", "s_relu", "s_nlog", "s_lbc", "s_min", "s_et", "s_etT",
                             "s_e", "s_agg", "s_acc"))
        s_sT, s_sT_out = sem("s_sT"), sem("s_sT_out")
        s_nm = sem("s_nm")
        s_eas = sem("s_eas")
        s_tmin = sem("s_tmin")
        s_num = sem("s_num")
        s_self_q = sem("s_self_q")
        s_link = sem("s_link")
        s_self_z, s_self_relu, s_self_l = sem("s_self_z"), sem("s_self_relu"), sem("s_self_l")
        s_self_d, s_self_e = sem("s_self_d"), sem("s_self_e")
        s_self_w, s_self_t, s_self_h = sem("s_self_w"), sem("s_self_t"), sem("s_self_h")
        s_sum = sem("s_sum")
        s_sq_in, s_sq = sem("s_sq_in"), sem("s_sq")
        s_x2 = sem("s_x2")
        s_resid_d = sem("s_resid_d")
        s_resid = sem("s_resid")
        s_sum_h = sem("s_sum_h")
        s_neg = sem("s_neg")
        s_free = sem("s_free")
        s_moe_w = sem("s_moe_w")
        s_b1T = sem("s_b1T")
        s_ln2 = sem("s_ln2")
        s_g_tp, s_g_T, s_gate = sem("s_g_tp"), sem("s_g_T"), sem("s_gate")
        s_shift, s_exp = sem("s_shift"), sem("s_exp")
        s_onehot, s_cum = sem("s_onehot"), sem("s_cum")
        s_slots = sem("s_slots")
        s_zero = sem("s_zero")
        s_zero_src = sem("s_zero_src")
        s_put = sem("s_put")
        s_wx = [sem(f"s_wx{i}") for i in range(2)]
        s_tok = sem("s_tok")
        s_tokT, s_tokT_out = sem("s_tokT"), sem("s_tokT_out")
        s_up, s_hid, s_down, s_y = sem("s_up"), sem("s_hid"), sem("s_down"), sem("s_y")
        s_y_out = sem("s_y_out")
        s_b2 = sem("s_b2")
        s_get = [sem(f"s_get{c}") for c in range(CH)]
        s_bad = sem("s_bad")
        s_bad_sum = sem("s_bad_sum")
        s_bad_flag = sem("s_bad_flag")
        s_y_chk = sem("s_y_chk")
        s_fin = sem("s_fin")
        s_out = sem("s_out")

        PARTS = [(0, 112), (112, PB)]

        def flag_of(engines):
            return nc.values_load(unsorted[0:1, 0:1], engines=engines, min_val=0, max_val=1,
                                  skip_runtime_bounds_check_because="DVE writes 0 or 1")

        STEP_LINKS = 5
        SORT_LINKS = 2 + SC

        def chunk(v, c):
            return v[:, c * CB:(c + 1) * CB]

        block = ctx.enter_context(nc.Block())

        @block.sync
        def _(sp):
            x_v = x.rearrange("(b p) d -> p b d", p=PB)
            out_v = out.rearrange("(b p) d -> p b d", p=PB)

            sp.wait_ge(s_pad, 1)
            KF = K7 - 1
            sp.dma_start(dst_s[0:PB, 0:SC], dst.rearrange("(p c) -> p c", p=PB)).then_inc(s_dst_s, 16)
            sp.dma_start(dst_s[0:PB - 1, SC:SC + 1], dst[SC:E].rearrange("(p c) -> p c", c=SC)[:, 0:1], allow_slow_non_contiguous=True).then_inc(s_dst_s, 16)
            for flat, tile in ((src, src_i), (dst, dst_i)):
                sp.dma_start(tile[:, 0:KF, :], flat[0:KF * P * P].rearrange("(k q e) -> q k e", q=P, e=P)).then_inc(s_edges, 16)
                sp.dma_start(tile[0:FULL - KF * P, KF, :], flat[KF * P * P:FULL * P].rearrange("(q e) -> q e", e=P)).then_inc(s_edges, 16)
                sp.dma_start(tile[FULL - KF * P:FULL - KF * P + 1, KF, 0:REST], flat[FULL * P:E].rearrange("(q e) -> q e", q=1)).then_inc(s_edges, 16)
            sp.dma_start(ea_in[:, 0:KF], ea[0:KF * P * P, :].rearrange("(k q e) j -> q k e j", q=P, e=P)).then_inc(s_edges, 16)
            sp.dma_start(ea_in[0:FULL - KF * P, KF], ea[KF * P * P:FULL * P, :].rearrange("(q e) j -> q e j", e=P)).then_inc(s_edges, 16)
            sp.dma_start(ea_in[FULL - KF * P:FULL - KF * P + 1, KF, 0:REST, :], ea[FULL * P:E, :].rearrange("(q e) j -> q e j", q=1)).then_inc(s_edges, 16)
            for a, b_ in PARTS:
                sp.dma_start(H[a:b_], x_v[a:b_]).then_inc(s_x, 16)

            sp.wait_ge(s_flag, 1)
            with sp.If(flag_of(SP_ONLY) != 0):
                sp.wait_ge(s_sort_pad, 1)
                sp.dma_start(src_s[0:PB], src.rearrange("(p c) -> p c", p=PB)).then_inc(s_sort_in, 16)
                sp.dma_start(ea_s[0:PB], ea.rearrange("(p c) j -> p c j", p=PB)).then_inc(s_sort_in, 16)
                sp.dma_start(sorted_edges[E:ROWS * P, :], pad_edge[0:NPAD, :]).then_inc(s_sort_pads, 16)
                sp.wait_ge(s_sort_pads, 16)
                sp.wait_ge(s_sort_put, 16 * SC)
                sp.dma_start(loaded_edges[:, 0:KF], sorted_edges[0:KF * P * P, :].rearrange("(k q e) f -> q k e f", q=P, e=P)).then_inc(s_sort_back, 16)
                sp.dma_start(loaded_edges[0:LASTK, KF], sorted_edges[KF * P * P:, :].rearrange("(q e) f -> q e f", e=P)).then_inc(s_sort_back, 16)

            sp.wait_ge(s_edges_f, 2)
            sp.dma_start(dst_rows[0:KF * P * P].rearrange("(k q e) -> q k e", q=P, e=P), dst_f[:, 0:KF, :]).then_inc(s_edges_out, 16)
            sp.dma_start(dst_rows[KF * P * P:].rearrange("(q e) -> q e", e=P), dst_f[0:LASTK, KF, :]).then_inc(s_edges_out, 16)
            for j in range(2):
                sp.dma_start(ea_rows[j, 0:KF * P * P].rearrange("(k q e) -> q k e", q=P, e=P), ea_pl[:, 0:KF, j, :]).then_inc(s_edges_out, 16)
                sp.dma_start(ea_rows[j, KF * P * P:].rearrange("(q e) -> q e", e=P), ea_pl[0:LASTK, KF, j, :]).then_inc(s_edges_out, 16)

            for l, (Wl, Wr, We, att_d, b_d, g_d, beta_d, a_d) in enumerate(layers):
                base = l * STEPS
                if l:
                    sp.wait_ge(s_self_l, NB)
                sp.dma_start(Wlr[:, :, 0:D], Wl.rearrange("(c k) n -> k c n", c=2)).then_inc(s_w, 16)
                sp.dma_start(Wlr[:, :, W:W + D], Wr.rearrange("(c k) n -> k c n", c=2)).then_inc(s_w, 16)
                sp.dma_start(WeB[:, :, 0:D], We.partition_broadcast(P)).then_inc(s_w, 16)
                sp.dma_start(att_relu[:, :], att_d.partition_broadcast(P)).then_inc(s_w, 16)
                sp.wait_ge(s_fixed, 1)
                sp.wait_ge(s_wext, l + 1)
                for j in range(2):
                    sp.dma_start(XR[PB + j:PB + j + 1, :, :], WeB[0:1, j:j + 1, :].to_broadcast([1, NB, W])).then_inc(s_we, 16)
                if l:
                    sp.wait_ge(s_feat, 1 + CH)
                for i, v in enumerate((b_d, g_d, beta_d)):
                    sp.dma_start(rows[:, i, :], v.partition_broadcast(P)).then_inc(s_rows, 16)
                sp.dma_start(slope[:, :], a_d.partition_broadcast(P)).then_inc(s_rows, 16)
                xl_v = xl_table[l].rearrange("(b p) w -> p b w", p=PB)
                for c in range(CH):
                    sp.wait_ge(s_xl, NB * l + CB * (c + 1))
                    for a, b_ in PARTS:
                        sp.dma_start(xl_v[a:b_, c * CB:(c + 1) * CB], XL[a:b_, c * CB:(c + 1) * CB]).then_inc(s_table, 16)
                sp.wait_ge(s_edges_out, 16 * 6)
                sp.wait_ge(s_stairs, 1)
                tiles = None
                for k, j in periods(sp, STEPS, UN, 0):
                    if j == 0:
                        _, tiles = nc.values_load_multi_w_load_instructions(
                            tile_of[0:1, bass.ds(k, UN)], engines=SP_ONLY, min_val=0, max_val=T - 1,
                            skip_runtime_bounds_check_because=IN_RANGE)
                    s = k % 4 if isinstance(k, int) else j % 4
                    if reused(k, 0, 4) or l:
                        sp.wait_ge(s_z, base + k - 3)
                    if l == 0 and reused(k, 0, 4):
                        sp.wait_ge(s_sT, k - 3)
                    sp.dma_start(dst_b[:, s, :], dst_rows[bass.ds(tiles[j] * TE, TE)].partition_broadcast(P)).then_inc(s_row[s], 16)
                    sp.dma_start(ST[PB:PB + 2, s, :], ea_rows[:, bass.ds(tiles[j] * TE, TE)]).then_inc(s_row[s], 16)
                if l == 0:
                    sp.wait_ge(s_me_T_out, 1)
                    sp.dma_start(me_rows.rearrange("j (b p) -> (j b) p", p=PB), ME_T).then_inc(s_me_rows, 16)
                    sp.wait_ge(s_me_rows, 16)
                sp.wait_ge(s_z, base + STEPS)
                for k, j in periods(sp, NB, SL, 0):
                    if reused(k, 0, SL) or l:
                        sp.wait_ge(s_self_mm, l * NB + k - SL + 1)
                    sp.dma_start(eye[j][PB:PB + 2, :], me_rows[:, bass.ds(k * PB, PB)]).then_inc(s_eye_me[j], 16)

            sp.wait_ge(s_self_h, 2 * NB)
            for a, b_ in PARTS:
                sp.dma_start(XL[a:b_, :, 0:D], x_v[a:b_]).then_inc(s_x2, 16)

            sp.wait_ge(s_free, 1)
            sp.dma_start(gw_sb, gate_w.rearrange("(c k) e -> k c e", c=2)).then_inc(s_moe_w, 16)
            sp.dma_start(gb_sb, gate_b.partition_broadcast(P)).then_inc(s_moe_w, 16)
            sp.dma_start(b1_rows, b1.rearrange("e (f k) -> (e f) k", k=P)).then_inc(s_moe_w, 16)
            sp.wait_ge(s_zero_src, 1)
            R = NX * CAP
            RP = R // P * P
            sp.dma_start(tok_buf[0:RP, :].rearrange("(p r) d -> p r d", p=P), zero_rows[:, 0:D].unsqueeze(1).to_broadcast([P, RP // P, D])).then_inc(s_zero, 16)
            if R > RP:
                sp.dma_start(tok_buf[RP:R, :], zero_rows[0:R - RP, 0:D]).then_inc(s_zero, 16)

            def expert_weights(e, s):
                sp.dma_start(w1_sb[:, s], w1[bass.ds(e, 1), :, :].rearrange("o (c k) f -> k (o c) f", c=2)).then_inc(s_wx[s], 16)
                sp.dma_start(w2_sb[:, s], w2[bass.ds(e, 1), :, :].rearrange("o (f k) d -> k (o f) d", f=FC)).then_inc(s_wx[s], 16)
                sp.dma_start(b2B[:, s * D:(s + 1) * D], b2[bass.ds(e, 1), :].rearrange("o d -> (o d)").partition_broadcast(P)).then_inc(s_wx[s], 16)

            M = len(MT)
            last = MT[-1][1]

            def tokens(e):
                sp.dma_start(tok[:, 0:M - 1, :], tok_buf[bass.ds(e * CAP, P * (M - 1)), :].rearrange("(m p) d -> p m d", p=P)).then_inc(s_tok, 16)
                sp.dma_start(tok[0:last, M - 1, :], tok_buf[bass.ds(e * CAP + P * (M - 1), last), :]).then_inc(s_tok, 16)

            def store_y(e):
                sp.wait_ge(s_y, (e + 1) * M)
                sp.dma_start(y_buf[bass.ds(e * CAP, P * (M - 1)), :].rearrange("(m p) d -> p m d", p=P), y_sb[:, 0:M - 1, :]).then_inc(s_y_out, 16)
                sp.dma_start(y_buf[bass.ds(e * CAP + P * (M - 1), last), :], y_sb[0:last, M - 1, :]).then_inc(s_y_out, 16)

            expert_weights(0, 0)
            expert_weights(1, 1)
            sp.wait_ge(s_put, 16 * NB)
            tokens(0)

            def pair_of_experts(pair, more):
                for s in range(2):
                    e = pair * 2 + s
                    if s == 0 or more:
                        sp.wait_ge(s_tokT, (e + 1) * M)
                        tokens(e + 1)
                    store_y(e)
                    if more:
                        expert_weights(e + 2, s)

            with sp.Fori(0, NX // 2 - 1) as pair:
                pair_of_experts(pair, True)
            pair_of_experts(NX // 2 - 1, False)
            for c in range(CH):
                sp.wait_ge(s_fin, CB * (c + 1))
                for a, b_ in PARTS:
                    sp.dma_start(out_v[a:b_, c * CB:(c + 1) * CB], H[a:b_, c * CB:(c + 1) * CB]).then_inc(s_out, 16)
            sp.wait_ge(s_out, 32 * CH)

        @block.gpsimd
        def _(pool):
            g = nc.gpsimd
            g.memset(dst_s[:, SC:SC + 1], PAD_DST)
            g.memset(src_i, 0)
            g.memset(ea_in, 0.0)
            g.memset(dst_i, PAD_DST).then_inc(s_pad, 1)
            g.iota(iota_i[:, :], pattern=[[1, P]], base=0, channel_multiplier=0)
            g.iota(iota_ci[:, :], pattern=[[0, 1]], base=0, channel_multiplier=1)
            g.iota(step_iota_i, pattern=[[1, STEPS]], base=0, channel_multiplier=0).then_inc(s_pad, 1)

            pool.wait_ge(s_flag, 1)
            with pool.If(flag_of(POOL_ONLY) != 0):
                with pool.Fori(0, SC) as c:
                    pool.wait_ge(s_sort_link, SORT_LINKS + (c + 1) * STEP_LINKS)
                    pool.wait_ge(s_sort_put, c * 16)
                    pool.sem_inc(s_tick)
                    g.tensor_copy(edge_slot[0:PB, :].unsqueeze(1), edge_s[0:PB, bass.ds(c, 1), :]).then_inc(s_sort_slot, 1)
                    pool.wait_ge(s_sort_slot, c + 1)
                    pool.sem_inc(s_tick)
                    g.indirect_dma_start(sorted_edges, bass.IndirectOffsetOnAxis(place[0:PB, 0:1], 0),
                                         edge_slot[0:PB, :], None).then_inc(s_sort_put, 16)

            def slot_free(k, done, first):
                if not isinstance(k, int) or k >= 2 or first:
                    pool.wait_ge(done, first + k - 1)
                    pool.sem_inc(s_tick)

            def staged_copy(feats, k, j):
                g.tensor_copy(staged[0:PB, j:j + 1, :], feats[0:PB, bass.ds(k, 1), 0:D]).then_inc(s_staged, 1)

            for l in range(2):
                base = l * STEPS
                if l:
                    for c in range(CH):
                        pool.wait_ge(s_feat, 2 + c)
                        with pool.Fori(0, CB // 2) as turn:
                            for j in range(2):
                                slot_free(turn * 2 + (c * CB + j), s_tp, NB)
                                staged_copy(H, turn * 2 + (c * CB + j), j)
                pool.wait_ge(s_srcT_out, 1)
                pool.wait_ge(s_stairs, 1)
                pool.wait_ge(s_table, 32 * CH * (l + 1))
                tiles = None
                for k, j in periods(pool, STEPS, UN, 0):
                    if j == 0:
                        _, tiles = nc.values_load_multi_w_load_instructions(
                            tile_of[0:1, bass.ds(k, UN)], engines=POOL_ONLY, min_val=0, max_val=T - 1,
                            skip_runtime_bounds_check_because=IN_RANGE)
                    s = j % XJ
                    if reused(k, 0, XJ) or l:
                        pool.wait_ge(s_agg, base + k - XJ + 1)
                        pool.sem_inc(s_tick)
                    g.tensor_copy(src_slot[:, s, :], src_cols[:, bass.ds(tiles[j] * G, G)]).then_inc(s_idx, 1)
                    pool.wait_ge(s_idx, base + k + 1)
                    pool.sem_inc(s_tick)
                    for u in range(G):
                        g.indirect_dma_start(xj[:, s, u, :], None, xl_table[l],
                                             bass.IndirectOffsetOnAxis(src_slot[:, s, u:u + 1], 0)).then_inc(s_xj[s], 16)
            pool.wait_ge(s_x2, 32)
            pool.wait_ge(s_sum, 4)
            for c in range(CH):
                mean_c, rstd_c = (chunk(v, c)[0:PB].unsqueeze(2).to_broadcast([PB, CB, D]) for v in (ln_mean, ln_rstd))
                g.tensor_tensor(chunk(XRn, c), chunk(XLn, c), mean_c, ALU.subtract).then_inc(s_resid_d, 1)
                pool.wait_ge(s_resid_d, c + 1)
                g.tensor_tensor(chunk(XRn, c), chunk(XRn, c), rstd_c, ALU.mult).then_inc(s_resid, 1)
            for k, j in periods(pool, NB, 2, 0):
                pool.wait_ge(s_ln2, k + 1)
                pool.sem_inc(s_tick)
                slot_free(k, s_g_tp, 0)
                staged_copy(XL, k, j)
            pool.wait_ge(s_slots, 1)
            pool.wait_ge(s_zero, 16 * (1 + (NX * CAP % P > 0)))
            for b_ in range(NB):
                g.indirect_dma_start(tok_buf, bass.IndirectOffsetOnAxis(slot_put[0:PB, b_:b_ + 1], 0),
                                     XL[0:PB, b_, 0:D], None).then_inc(s_put, 16)
            pool.wait_ge(s_y_out, 32 * NX)
            pool.wait_ge(s_down, NX * len(MT))
            for b_ in range(NB):
                g.indirect_dma_start(XL[0:PB, b_, 0:D], None, y_buf,
                                     bass.IndirectOffsetOnAxis(slot_get[0:PB, b_:b_ + 1], 0)).then_inc(s_get[b_ // CB], 16)

        @block.scalar
        def _(act):
            a = nc.scalar
            act.wait_ge(s_var, 1)
            a.activation(ln_rstd[0:PB, :], col_a[0:PB, :], ACT.Sqrt, bias=eps_col[0:PB, :], scale=1.0 / D).then_inc(s_root, 1)
            for l in range(2):
                base = l * STEPS
                if l == 0:
                    act.wait_ge(s_edges_out, 16 * 6)
                    act.wait_ge(s_srcT_out, 1)
                    act.wait_ge(s_stairs, 1)
                for k, j in periods(act, NB, 2, 1):
                    if live(k, 0, NB):
                        s = j % 2
                        act.wait_ge(s_tp, l * NB + k + 1)
                        if reused(k, 0, 2) or l:
                            act.wait_ge(s_lin, l * NB + k - 1)
                        a.activation(hT[:, s, :, :], ps[:, 4 + s, 0:2 * PB].rearrange("p (c n) -> p c n", c=2), ACT.Copy).then_inc(s_hT, 1)
                    if live(k, 1, NB):
                        s = (j - 1) % 2
                        act.wait_ge(s_lin, l * NB + k)
                        act.sem_inc(s_tick)
                        a.activation(XL[0:PB, bass.ds(k - 1, 1), :], ps[0:PB, 2 * s:2 * s + 1, 0:W], ACT.Copy).then_inc(s_xl, 1)
                act.wait_ge(s_stairs, 1)
                act.wait_ge(s_state, l + 1)
                old = [act.alloc_register(f"old_block_act{l}_{i}") for i in range(LAG)]
                blocks = held = None
                for k, j in periods(act, STEPS, UN, LAG):
                    if j == 0:
                        held = [act.snap(r, min_val=0, max_val=NB - 1) for r in old] if not (isinstance(k, int) and k == 0) else None
                        if live(k, 0, STEPS):
                            _, blocks = nc.values_load_multi_w_load_instructions(
                                block_of[0:1, bass.ds(k, UN)], engines=ACT_ONLY, min_val=0, max_val=NB - 1,
                                skip_runtime_bounds_check_because=IN_RANGE)
                    if live(k, 2, STEPS):
                        s = (j - 2) % 2
                        act.wait_ge(s_zs, base + k - 1)
                        a.activation(zs[:, s, :, 0:D], zs[:, s, :, 0:D], ACT.Relu).then_inc(s_relu, 1)
                    if live(k, 4, STEPS):
                        s = (j - 4) % 2
                        act.wait_ge(s_etT, base + k - 3)
                        if reused(k, 4, 2) or l:
                            act.wait_ge(s_agg, base + k - 5)
                        a.activation(Es[:, s, :, :], ps[:, 5, 0:G * PB].rearrange("p (g n) -> p g n", g=G), ACT.Copy).then_inc(s_e, 1)
                    if l == 0 and live(k, 1, STEPS):
                        act.wait_ge(s_sT, k)
                        if reused(k, 1, 2):
                            act.wait_ge(s_lbc, k - 2)
                        a.activation(Srow[:, (j - 1) % 2, :, :], ps[:, 7, 0:TE].rearrange("p (g n) -> p g n", g=G), ACT.Copy).then_inc(s_sT_out, 1)
                    if live(k, 3, STEPS):
                        s, q = (j - 3) % 2, (j - 3) % 4
                        b_ = blocks[j - 3] if j >= 3 else held[LAG + j - 3]
                        act.wait_ge(s_min, base + k - 2)
                        if reused(k, 3, 2) or l:
                            act.wait_ge(s_etT, base + k - 4)
                        if reused(k, 3, 4) or l:
                            act.wait_ge(s_acc, base + k - 6)
                        if reused(k, 3, 1):
                            act.wait_ge(s_nm, base + k - 3)
                        act.sem_inc(s_tick)
                        a.activation(ETs[0:PB, s, :], mk[0:PB, s, :], ACT.Exp, bias=new_min[0:PB, q:q + 1], scale=-1.0,
                                     accum_out=den_t[0:PB, q:q + 1]).then_inc(s_num, 1)
                        a.activation(resc[0:PB, q:q + 1], NM[0:PB, bass.ds(b_, 1)], ACT.Exp, bias=new_min[0:PB, q:q + 1],
                                     scale=-1.0).then_inc(s_et, 1)
                        act.wait_ge(s_et, base + k - 2)
                        act.sem_inc(s_tick)
                        a.activation(NM[0:PB, bass.ds(b_, 1)], new_min[0:PB, q:q + 1], ACT.Copy).then_inc(s_nm, 1)
                    if live(k, 0, STEPS):
                        s = j % 4
                        act.wait_ge(s_st, base + k + 1)
                        if reused(k, 0, 4) or l:
                            act.wait_ge(s_min, base + k - 3)
                        a.activation(mpos[0:PB, s, :], ST[0:PB, s, :], ACT.Copy, bias=BIG, scale=-BIG).then_inc(s_mpos, 1)
                    if j == UN - 1 and live(k, 0, STEPS):
                        for i in range(LAG):
                            act.reg_mov(old[i], blocks[UN - LAG + i])
                for k, j in periods(act, NB, SL, 0):
                    act.wait_ge(s_self_z, l * NB + k + 1)
                    a.activation(xj[0:PB, j, 0, 0:D], xj[0:PB, j, 0, 0:D], ACT.Relu).then_inc(s_self_relu, 1)
                act.wait_ge(s_self_d, l + 1)
                a.activation(RS[0:PB, :], RS[0:PB, :], ACT.Exp)
                a.activation(PS_[0:PB, :], PS_[0:PB, :], ACT.Exp).then_inc(s_self_e, 1)
                act.wait_ge(s_self_w, l + 1)
                for k, j in periods(act, NB, SL, 0):
                    if reused(k, 0, SL) or l:
                        act.wait_ge(s_self_h, l * NB + k - SL + 1)
                        act.sem_inc(s_tick)
                    a.activation(xj[0:PB, j, 1, 0:D].unsqueeze(1), H[0:PB, bass.ds(k, 1), :], ACT.Copy,
                                 scale=RS[0:PB, bass.ds(k, 1)]).then_inc(s_self_t, 1)
                for c in range(CH):
                    act.wait_ge(s_sq_in, l * CH + c + 1)
                    a.activation(chunk(XRn, c), chunk(Hn, c), ACT.Square).then_inc(s_sq, 1)
                act.wait_ge(s_var, 2 + l)
                a.activation(scale_row, scale_row, ACT.Sqrt, bias=eps_col[:, :], scale=1.0).then_inc(s_root, 1)
            for c in range(CH):
                act.wait_ge(s_sum_h, c + 1)
                a.activation(chunk(XRn, c), chunk(Hn, c), ACT.Relu, scale=-1.0).then_inc(s_neg, 1)
            act.wait_ge(s_var, 4)
            a.activation(ln_rstd[0:PB, :], col_a[0:PB, :], ACT.Sqrt, bias=eps_col[0:PB, :], scale=1.0 / D).then_inc(s_root, 1)
            for k, j in periods(act, NB, 2, 0):
                s = j % 2
                act.wait_ge(s_g_tp, k + 1)
                if reused(k, 0, 2):
                    act.wait_ge(s_gate, k - 1)
                a.activation(hT[:, s, :, :], ps[:, 4 + s, 0:2 * PB].rearrange("p (c n) -> p c n", c=2), ACT.Copy).then_inc(s_g_T, 1)
            act.wait_ge(s_shift, 1)
            a.activation(probs[0:PB, :], probs[0:PB, :], ACT.Exp).then_inc(s_exp, 1)
            act.wait_ge(s_b1T, 2)
            with act.Fori(0, NX) as e:
                for f in range(FC):
                    for h, (t0, tn) in enumerate(HALVES):
                        i = 2 * f + h
                        act.wait_ge(s_up, e * 2 * FC + i + 1)
                        act.sem_inc(s_tick)
                        a.activation(hidT[:, f, t0:t0 + tn], ps[:, i % 4, 0:tn], ACT.Relu,
                                     bias=b1T[:, bass.ds(e * FC + f, 1)]).then_inc(s_hid, 1)

        @block.tensor
        def _(pe):
            t = nc.tensor
            pe.wait_ge(s_consts, 1)
            pe.wait_ge(s_descents, 1)
            t.matmul(ps[0:1, 7, 0:1], ones[0:PB, 0:1], unsorted_f[0:PB, :], start=True, stop=True).then_inc(s_descents_sum, 1)
            pe.wait_ge(s_flag, 1)
            with pe.If(flag_of(PE_ONLY) != 0):
                pe.wait_ge(s_sort_link, SORT_LINKS - 1)
                t.matmul(ps[0:PB, 0, 0:NB + 1], ones[0:PB, 0:PB], beyond[0:PB, :], start=True, stop=True).then_inc(s_sort_total, 1)
                with pe.Fori(0, SC) as c:
                    pe.wait_ge(s_sort_link, SORT_LINKS + c * STEP_LINKS + 2)
                    pe.sem_inc(s_tick)
                    t.matmul(ps[0:PB, 1, 0:NB], before[0:PB, :], in_block[0:PB, :], start=True, stop=True)
                    t.matmul(ps[0:PB, 2, 0:NB], ones[0:PB, 0:PB], in_block[0:PB, :], start=True, stop=True).then_inc(s_sort_rank, 1)
            pe.wait_ge(s_edges_f, 2)
            for k in range(K7):
                mm = t.matmul(ps[0:NB - 1, k // 4, (k % 4) * P:(k % 4 + 1) * P], dst_f[:, k, P - 1:P].to_broadcast([P, NB - 1]), ident[:, :], start=True, stop=True)
            mm.then_inc(s_last, 1)
            for k in range(K7):
                mm = t.transpose(ps[:, 2 + k // 4, (k % 4) * P:(k % 4 + 1) * P], src_f[:, k, :], ident[:, :])
            mm.then_inc(s_srcT, 1)
            pe.wait_ge(s_after, 1)
            t.matmul(ps[0:1, 4, 0:STEPS], ones[0:NB - 1, 0:1], after[0:NB - 1, :], start=True, stop=True).then_inc(s_blocks, 1)

            def node_sum(srcv, b_, **flags):
                return t.matmul(ps[:, 0, 0:D], ones[0:PB, :], srcv[0:PB, bass.ds(b_, 1), 0:D], **flags)

            def transposed(j, done):
                for c in range(2):
                    mm = t.transpose(ps[:, 4 + j % 2, c * PB:(c + 1) * PB],
                                     staged[0:PB, j % 2, c * P:(c + 1) * P], ident[0:PB, 0:PB])
                mm.then_inc(done, 1)

            for l in range(2):
                base = l * STEPS
                pe.wait_ge(s_wext, l + 1)
                for k, j in periods(pe, NB, 2, 1):
                    if live(k, 0, NB):
                        if reused(k, 0, 2) or l:
                            pe.wait_ge(s_hT, l * NB + k - 1)
                        pe.wait_ge(s_staged, l * NB + k + 1)
                        transposed(j, s_tp)
                    if live(k, 1, NB):
                        s = (j - 1) % 2
                        pe.wait_ge(s_hT, l * NB + k)
                        if reused(k, 1, 2) or l:
                            pe.wait_ge(s_xl, l * NB + k - 2)
                            pe.wait_ge(s_xr, l * NB + k - 2)
                        for h in range(2):
                            for c in range(2):
                                mm = t.matmul(ps[0:PB, 2 * s + h, 0:W], hT[:, s, c, :], Wlr[:, c, h * W:(h + 1) * W], start=c == 0, stop=c == 1)
                        mm.then_inc(s_lin, 1)
                pe.wait_ge(s_we, 32 * (l + 1))
                pe.wait_ge(s_xr, NB * (l + 1))
                pe.wait_ge(s_xl, NB * (l + 1))
                pe.wait_ge(s_stairs, 1)
                blocks = None
                for k, j in periods(pe, STEPS, UN, LAG):
                    if live(k, 4, STEPS):
                        s, r = (j - 4) % 2, (j - 4) % XJ
                        pe.wait_ge(s_e, base + k - 3)
                        if reused(k, 4, 1) or l:
                            pe.wait_ge(s_acc, base + k - 4)
                        for u in range(G):
                            mm = t.matmul(ps[0:PB, 6, 0:D], Es[:, s, u, :], xj[:, r, u, 0:D], start=u == 0, stop=u == G - 1)
                        mm.then_inc(s_agg, 1)
                    if live(k, 3, STEPS):
                        s = (j - 3) % 2
                        pe.wait_ge(s_num, base + k - 2)
                        if reused(k, 3, 1) or l:
                            pe.wait_ge(s_e, base + k - 3)
                        for u in range(G):
                            mm = t.transpose(ps[:, 5, u * PB:(u + 1) * PB], ETs[0:PB, s, u * P:(u + 1) * P], ident[0:PB, 0:PB])
                        mm.then_inc(s_etT, 1)
                    if live(k, 2, STEPS):
                        s, r = (j - 2) % 2, (j - 2) % 4
                        pe.wait_ge(s_nlog, base + k - 1)
                        if reused(k, 2, 1) or l:
                            pe.wait_ge(s_tmin, base + k - 2)
                        if l == 0 and reused(k, 2, 1):
                            pe.wait_ge(s_eas, k - 2)
                        for u in range(G):
                            mm = t.matmul(ps[0:PB, 4, u * P:(u + 1) * P], nlog[:, r, u:u + 1].to_broadcast([P, PB]), ident[:, :], start=True, stop=True)
                        if l == 0:
                            pe.wait_ge(s_sT_out, k - 1)
                            for u in range(G):
                                mm = t.matmul(ps[0:PB, 4, TE:TE + 3], Srow[:, s, u, 0:PB], Srow[:, s, u, PB:P], start=u == 0, stop=u == G - 1)
                        mm.then_inc(s_lbc, 1)
                    if live(k, 0, STEPS):
                        if j == 0:
                            _, blocks = nc.values_load_multi_w_load_instructions(
                                block_of[0:1, bass.ds(k, UN)], engines=PE_ONLY, min_val=0, max_val=NB - 1,
                                skip_runtime_bounds_check_because=IN_RANGE)
                        s, r = j % 2, j % 4
                        pe.wait_ge(s_st, base + k + 1)
                        if reused(k, 0, 2) or l:
                            pe.wait_ge(s_zs, base + k - 1)
                        for u in range(G):
                            mm = t.matmul(ps[:, 2 * s + u, 0:W], ST[:, r, u * P:(u + 1) * P],
                                          XR[:, bass.ds(blocks[j], 1), :].rearrange("p o w -> p (o w)"), start=True, stop=True)
                        mm.then_inc(s_z, 1)
                    if l == 0 and live(k, 0, STEPS):
                        if reused(k, 0, 1):
                            pe.wait_ge(s_sT_out, k)
                        for u in range(G):
                            mm = t.transpose(ps[:, 7, u * P:(u + 1) * P], ST[:, j % 4, u * P:(u + 1) * P], ident[:, :])
                        mm.then_inc(s_sT, 1)
                if l == 0:
                    pe.wait_ge(s_me, 1)
                    t.transpose(ps[0:2 * NB, 5, 0:PB], ME[0:PB, :, :].rearrange("p j b -> p (j b)"), ident[0:PB, 0:PB]).then_inc(s_me_T, 1)
                pe.wait_ge(s_eye, l + 1)
                for k, j in periods(pe, NB, SL, 0):
                    turn = (k - j) // SL if isinstance(k, int) else None
                    done = NB // SL * 16 * l
                    pe.wait_ge(s_eye_me[j], done + (turn + 1) * 16 if turn is not None else (k - j) * 16 // SL + (done + 16))
                    if reused(k, 0, SL) or l:
                        pe.wait_ge(s_self_z, l * NB + k - SL + 1)
                    t.matmul(ps[0:PB, j, 0:W], eye[j], XR[:, bass.ds(k, 1), :].rearrange("p o w -> p (o w)"),
                             start=True, stop=True).then_inc(s_self_mm, 1)
                pe.wait_ge(s_self_z, NB * (l + 1))
                for k, j in periods(pe, NB - SL, SL, SL):
                    pe.wait_ge(s_self_h, l * NB + k + 1)
                    ins = node_sum(H, k, start=isinstance(k, int) and k == 0, stop=isinstance(k, int) and k == NB - 1)
                ins.then_inc(s_sum, 1)
                for c in range(CH):
                    pe.wait_ge(s_sq, l * CH + c + 1)
                    node_sum(XR, c * CB, start=c == 0, stop=False)
                    with pe.Fori(0, CB // 2 - 1) as turn:
                        for u in range(2):
                            node_sum(XR, turn * 2 + (c * CB + 1 + u), start=False, stop=False)
                    ins = node_sum(XR, (c + 1) * CB - 1, start=False, stop=c == CH - 1)
                ins.then_inc(s_sum, 1)
            pe.wait_ge(s_moe_w, 48)
            t.transpose(ps[:, 6, 0:NX * FC], b1_rows, ident[0:NX * FC, 0:NX * FC]).then_inc(s_b1T, 1)
            for k, j in periods(pe, NB, 2, 1):
                if live(k, 0, NB):
                    if reused(k, 0, 2):
                        pe.wait_ge(s_g_T, k - 1)
                    pe.wait_ge(s_staged, 2 * NB + k + 1)
                    transposed(j, s_g_tp)
                if live(k, 1, NB):
                    s = (j - 1) % 2
                    pe.wait_ge(s_g_T, k)
                    for c in range(2):
                        mm = t.matmul(ps[0:PB, 7, bass.ds((k - 1) * NX, NX)], hT[:, s, c, :], gw_sb[:, c, :], start=c == 0, stop=c == 1)
                    mm.then_inc(s_gate, 1)
            pe.wait_ge(s_onehot, 1)
            t.matmul(ps[0:PB, 0, 0:NE], triu[0:PB, 0:PB], onehot[0:PB, :], start=True, stop=True)
            t.matmul(ps[0:PB, 1, 0:NE], ones[0:PB, 0:PB], onehot[0:PB, :], start=True, stop=True).then_inc(s_cum, 1)
            pe.wait_ge(s_slots, 1)
            M = len(MT)
            with pe.Fori(0, NX // 2) as pair:
                for s in range(2):
                    e = pair * 2 + s
                    pe.wait_ge(s_tok, (e + 1) * 32)
                    for m, (m0, mn) in enumerate(MT):
                        if m >= 2:
                            pe.wait_ge(s_tokT_out, e * M + m - 1)
                        for c in range(2):
                            mm = t.transpose(ps[:, 6 + m % 2, c * P:c * P + mn], tok[0:mn, m, c * P:(c + 1) * P], ident[0:mn, 0:mn])
                        mm.then_inc(s_tokT, 1)
                    pe.wait_ge(s_tokT_out, (e + 1) * M)
                    pe.wait_ge(s_wx[s], pair * 48 + 48)
                    for f in range(FC):
                        for h, (t0, tn) in enumerate(HALVES):
                            i = 2 * f + h
                            if i >= 4:
                                pe.wait_ge(s_hid, e * 2 * FC + i - 3)
                            for c in range(2):
                                mm = t.matmul(ps[:, i % 4, 0:tn], w1_sb[:, s, c, f * P:(f + 1) * P], tokT[:, c, t0:t0 + tn], start=c == 0, stop=c == 1)
                            mm.then_inc(s_up, 1)
                    pe.wait_ge(s_hid, (e + 1) * 2 * FC)
                    for m, (m0, mn) in enumerate(MT):
                        if m >= 2:
                            pe.wait_ge(s_y, e * M + m - 1)
                        for f in range(FC):
                            mm = t.matmul(ps[0:mn, 4 + m % 2, 0:D], hidT[:, f, m0:m0 + mn], w2_sb[:, s, f, :], start=f == 0, stop=f == FC - 1)
                        mm.then_inc(s_down, 1)

            pe.wait_ge(s_bad, 1)
            t.matmul(ps[0:1, 7, 0:1], ones[:, 0:1], bad[:, :], start=True, stop=True).then_inc(s_bad_sum, 1)

        @block.vector
        def _(dve):
            v = nc.vector
            links = [0]

            def link(ins):
                links[0] += 1
                ins.then_inc(s_link, 1)
                dve.wait_ge(s_link, links[0])

            dve.wait_ge(s_pad, 2)
            v.memset(XR[96:P, :, :], 0.0)
            link(v.memset(ST[96:P, :, :], 1.0))
            v.engine_nop().then_inc(s_fixed, 1)
            v.memset(ones[:, :], 1.0)
            v.memset(eps_col[:, :], EPS)
            link(v.tensor_copy(iota_row[:, :], iota_i[:, :]))
            link(v.tensor_copy(iota_col[:, :], iota_ci[:, :]))
            v.tensor_scalar(ident[:, :], iota_row[:, :], iota_col[:, :], None, ALU.is_equal)
            link(v.tensor_scalar(node_id[:, :], iota_row[:, 0:NB], float(PB), iota_col[:, :], ALU.mult, ALU.add))
            v.engine_nop().then_inc(s_consts, 1)
            dve.wait_ge(s_dst_s, 32)
            link(v.tensor_tensor(descents[0:PB], dst_s[0:PB, 0:SC], dst_s[0:PB, 1:SC + 1], ALU.is_gt))
            v.tensor_reduce(unsorted_f[0:PB, :], descents[0:PB], AX_X, ALU.add).then_inc(s_descents, 1)
            dve.wait_ge(s_descents_sum, 1)
            v.tensor_scalar(unsorted[:, :], ps[0:1, 7, 0:1], 0.0, None, ALU.is_gt).then_inc(s_flag, 1)
            dve.wait_ge(s_flag, 1)
            dve.wait_ge(s_edges, 16 * 9)
            with dve.If(flag_of(DVE_ONLY) != 0):
                def sort_link(ins, count):
                    ins.then_inc(s_sort_link, 1)
                    dve.wait_ge(s_sort_link, count)
                    dve.sem_inc(s_tick)

                v.memset(pad_edge[0:NPAD, :], 0.0)
                v.memset(beyond[0:PB, :], 0.0)
                v.tensor_scalar(before[0:PB, :], iota_row[0:PB, 0:PB], iota_col[0:PB, :], None, ALU.is_gt)
                v.tensor_scalar(block_start[0:PB, :], iota_row[0:PB, 0:NB + 1], float(PB), None, ALU.mult)
                sort_link(v.tensor_copy(edge_dst[0:PB], dst_s[0:PB, 0:SC]), 1)
                v.memset(pad_edge[0:NPAD, 1:2], float(PAD_DST)).then_inc(s_sort_pad, 1)
                dve.wait_ge(s_sort_in, 32)
                v.tensor_copy(edge_s[0:PB, :, 0], src_s[0:PB])
                v.tensor_copy(edge_s[0:PB, :, 1], dst_s[0:PB, 0:SC])
                v.tensor_copy(edge_s[0:PB, :, 2:4], ea_s[0:PB])
                with dve.Fori(0, SC) as c:
                    sort_link(v.scalar_tensor_tensor(beyond[0:PB, :], block_start[0:PB, :], edge_dst[0:PB, bass.ds(c, 1)],
                                                     beyond[0:PB, :], ALU.is_le, ALU.add), c + 2)
                dve.wait_ge(s_sort_total, 1)
                sort_link(v.tensor_scalar(places[0:PB, :], ps[0:PB, 0, 0:NB], -1.0, float(E), ALU.mult, ALU.add), SORT_LINKS)
                with dve.Fori(0, SC) as c:
                    first = SORT_LINKS + c * STEP_LINKS
                    sort_link(v.tensor_scalar(is_beyond[0:PB, :], block_start[0:PB, :], edge_dst[0:PB, bass.ds(c, 1)], None, ALU.is_le), first + 1)
                    sort_link(v.tensor_tensor(in_block[0:PB, :], is_beyond[0:PB, 0:NB], is_beyond[0:PB, 1:NB + 1], ALU.subtract), first + 2)
                    dve.wait_ge(s_sort_rank, c + 1)
                    dve.sem_inc(s_tick)
                    sort_link(v.tensor_tensor(place_of[0:PB, :], places[0:PB, :], ps[0:PB, 1, 0:NB], ALU.add), first + 3)
                    v.tensor_tensor(places[0:PB, :], places[0:PB, :], ps[0:PB, 2, 0:NB], ALU.add)
                    sort_link(v.tensor_tensor_reduce(place_of[0:PB, :], place_of[0:PB, :], in_block[0:PB, :], 1.0, 0.0,
                                                     ALU.mult, ALU.add, place_f[0:PB, :]), first + 4)
                    dve.wait_ge(s_sort_put, c * 16)
                    dve.sem_inc(s_tick)
                    sort_link(v.tensor_copy(place[0:PB, :], place_f[0:PB, :]), first + 5)
                dve.wait_ge(s_sort_back, 32)
                KF = K7 - 1
                for tile, f in ((src_i, 0), (dst_i, 1)):
                    v.tensor_copy(tile[:, 0:KF, :], loaded_edges[:, 0:KF, :, f])
                    v.tensor_copy(tile[0:LASTK, KF, :], loaded_edges[0:LASTK, KF, :, f])
                v.tensor_copy(ea_in[:, 0:KF], loaded_edges[:, 0:KF, :, 2:4])
                sort_link(v.tensor_copy(ea_in[0:LASTK, KF], loaded_edges[0:LASTK, KF, :, 2:4]), SORT_LINKS + SC * STEP_LINKS + 1)
            v.tensor_copy(src_f, src_i)
            v.tensor_copy(dst_f, dst_i).then_inc(s_edges_f, 1)
            v.tensor_copy(ea_pl.rearrange("p k j e -> p k e j"), ea_in).then_inc(s_edges_f, 1)
            dve.wait_ge(s_srcT, 1)
            v.tensor_copy(src_cols[:, 0:512], ps[:, 2, :])
            v.tensor_copy(src_cols[:, 512:K7 * P], ps[:, 3, 0:K7 * P - 512]).then_inc(s_srcT_out, 1)
            dve.wait_ge(s_last, 1)
            q = NB - 1
            v.tensor_copy(last_dst[0:q, 0:512], ps[0:q, 0, :])
            link(v.tensor_copy(last_dst[0:q, 512:K7 * P], ps[0:q, 1, 0:K7 * P - 512]))
            link(v.tensor_scalar(tau[0:q, 0:1], iota_col[0:q, :], float(PB), float(PB), ALU.mult, ALU.add))
            link(v.tensor_scalar(reached[0:q, 0:T - 1], last_dst[0:q, 1:2 * (T - 1):2], tau[0:q, 0:1], None, ALU.is_lt))
            link(v.tensor_reduce(tau[0:q, 1:2], reached[0:q, 0:T - 1], AX_X, ALU.add))
            link(v.tensor_scalar(tau[0:q, 1:2], tau[0:q, 1:2], iota_col[0:q, :], 1.0, ALU.add, ALU.add))
            link(v.tensor_copy(step_iota, step_iota_i))
            v.tensor_scalar(after[0:q, :], step_iota[0:q, :], tau[0:q, 1:2], None, ALU.is_ge).then_inc(s_after, 1)
            dve.wait_ge(s_blocks, 1)
            link(v.tensor_copy(block_f[0:1, :], ps[0:1, 4, 0:STEPS]))
            v.tensor_copy(block_of[:, :], block_f[0:1, :])
            link(v.tensor_tensor(step_iota[0:1, :], step_iota[0:1, :], block_f[0:1, :], ALU.subtract))
            v.tensor_copy(tile_of[:, :], step_iota[0:1, :]).then_inc(s_stairs, 1)

            def wide(col):
                return col[0:PB, :].unsqueeze(2).to_broadcast([PB, NB, D])

            def over(row, blocks):
                return row[0:PB, :].unsqueeze(1).to_broadcast([PB, blocks, D])

            def layer_norm_sums(srcv, turns):
                half = D // 2
                with dve.Fori(0, NB // turns) as turn:
                    for u in range(turns):
                        k = turn * turns + u
                        v.bn_stats(stats[0:PB, bass.ds(k, 1), :].rearrange("p o s -> p (o s)"), srcv[:, bass.ds(k, 1), :].rearrange("p o d -> p (o d)"))
                link(v.engine_nop())
                v.tensor_tensor(ln_mean[0:PB, :], stats[0:PB, :, 1], stats[0:PB, :, 4], ALU.add)
                link(v.tensor_tensor(col_a[0:PB, :], stats[0:PB, :, 1], stats[0:PB, :, 4], ALU.subtract))
                link(v.tensor_scalar(ln_mean[0:PB, :], ln_mean[0:PB, :], 0.5, None, ALU.mult))
                link(v.tensor_tensor(col_a[0:PB, :], col_a[0:PB, :], col_a[0:PB, :], ALU.mult))
                link(v.scalar_tensor_tensor(col_a[0:PB, :], col_a[0:PB, :], half / 2.0, stats[0:PB, :, 2], ALU.mult, ALU.add))
                v.tensor_tensor(col_a[0:PB, :], col_a[0:PB, :], stats[0:PB, :, 5], ALU.add).then_inc(s_var, 1)

            dve.wait_ge(s_x, 32)
            layer_norm_sums(Hn, 5)
            dve.wait_ge(s_root, 1)
            v.reciprocal(ln_rstd[0:PB, :], ln_rstd[0:PB, :]).then_inc(s_feat, 1)

            def weight_products(l):
                dve.wait_ge(s_w, 16 * 4 * (l + 1))
                v.tensor_scalar(att_lin[:, :], att_relu[:, :], -0.2, None, ALU.mult)
                link(v.tensor_scalar(att_relu[:, :], att_relu[:, :], -0.8, None, ALU.mult))
                for view in (Wlr[:, 0, 0:W], Wlr[:, 0, W:2 * W], Wlr[:, 1, 0:W], Wlr[:, 1, W:2 * W], WeB[:, 0, :], WeB[:, 1, :]):
                    link(v.tensor_tensor_reduce(junk[:, 0:D], view[:, 0:D], att_lin[:, :], 1.0, 0.0, ALU.mult, ALU.add, view[:, D:D + 1]))
                v.engine_nop().then_inc(s_wext, 1)

            def scaled(c):
                h = chunk(Hn, c)
                link(v.tensor_tensor(h, h, over(scale_row, CB), ALU.mult))
                link(v.tensor_tensor(h, h, over(rows[:, 2, :], CB), ALU.add))

            def next_input(c):
                h, neg = chunk(Hn, c), chunk(XRn, c)
                scaled(c)
                link(v.tensor_scalar(neg, h, 0.0, slope_1[0:PB, :], ALU.min, ALU.mult))
                v.tensor_tensor(h, h, neg, ALU.add).then_inc(s_feat, 1)
                dve.wait_ge(s_feat, 2 + c)

            def xr_out(l, k, j):
                dve.wait_ge(s_lin, l * NB + k + 1)
                v.tensor_copy(XR[0:PB, bass.ds(k, 1), :], ps[0:PB, 2 * (j % 2) + 1:2 * (j % 2) + 2, 0:W]).then_inc(s_xr, 1)

            for l in range(2):
                base = l * STEPS
                if l == 0:
                    weight_products(0)
                    for k, j in periods(dve, NB, 2, 2):
                        if live(k, 0, NB):
                            if reused(k, 0, 2):
                                dve.wait_ge(s_tp, k - 1)
                                dve.sem_inc(s_tick)
                            v.tensor_scalar(staged[0:PB, j, :], H[0:PB, bass.ds(k, 1), :].rearrange("p o d -> p (o d)"),
                                            ln_mean[0:PB, bass.ds(k, 1)], ln_rstd[0:PB, bass.ds(k, 1)],
                                            ALU.subtract, ALU.mult).then_inc(s_staged, 1)
                        if live(k, 2, NB):
                            xr_out(l, k - 2, j)
                else:
                    next_input(0)
                    for c in range(CH):
                        if c + 1 < CH:
                            next_input(c + 1)
                        with dve.Fori(0, CB // 2) as turn:
                            for j in range(2):
                                xr_out(l, turn * 2 + (c * CB + j), j)
                v.memset(Hn, 0.0)
                v.memset(NM[:, :], START)
                v.memset(DEN[:, :], 0.0)
                if l == 0:
                    v.memset(EAS[:, :, :], 0.0)
                v.engine_nop().then_inc(s_state, 1)
                dve.wait_ge(s_state, l + 1)
                dve.wait_ge(s_stairs, 1)
                old = [dve.alloc_register(f"old_block{l}_{i}") for i in range(LAG)]
                blocks = held = None
                for k, j in periods(dve, STEPS, UN, LAG):
                    if j == 0:
                        held = [dve.snap(r, min_val=0, max_val=NB - 1) for r in old] if not (isinstance(k, int) and k == 0) else None
                        if live(k, 0, STEPS):
                            _, blocks = nc.values_load_multi_w_load_instructions(
                                block_of[0:1, bass.ds(k, UN)], engines=DVE_ONLY, min_val=0, max_val=NB - 1,
                                skip_runtime_bounds_check_because=IN_RANGE)

                    def block_at(lag):
                        return blocks[j - lag] if j >= lag else held[LAG + j - lag]

                    if live(k, 5, STEPS):
                        r = (j - 5) % 4
                        b_ = block_at(5)
                        dve.wait_ge(s_agg, base + k - 4)
                        dve.wait_ge(s_et, base + k - 4)
                        if reused(k, 5, 1):
                            dve.wait_ge(s_acc, base + k - 5)
                        dve.sem_inc(s_tick)
                        v.scalar_tensor_tensor(H[0:PB, bass.ds(b_, 1), :].rearrange("p o d -> p (o d)"), H[0:PB, bass.ds(b_, 1), :].rearrange("p o d -> p (o d)"),
                                               resc[0:PB, r:r + 1], ps[0:PB, 6, 0:D], ALU.mult, ALU.add)
                        v.scalar_tensor_tensor(DEN[0:PB, bass.ds(b_, 1)], DEN[0:PB, bass.ds(b_, 1)], resc[0:PB, r:r + 1],
                                               den_t[0:PB, r:r + 1], ALU.mult, ALU.add).then_inc(s_acc, 1)
                    if live(k, 3, STEPS):
                        s, r = (j - 3) % 2, (j - 3) % 4
                        dve.wait_ge(s_lbc, base + k - 2)
                        dve.wait_ge(s_mpos, base + k - 2)
                        if reused(k, 3, 2) or l:
                            dve.wait_ge(s_num, base + k - 4)
                        b_ = block_at(3)
                        if l == 0 and reused(k, 3, 1):
                            dve.wait_ge(s_eas, k - 3)
                        dve.sem_inc(s_tick)
                        if l == 0:
                            v.tensor_tensor(EAS[0:PB, bass.ds(b_, 1), :], EAS[0:PB, bass.ds(b_, 1), :],
                                            ps[0:PB, 4, TE:TE + 3].unsqueeze(1), ALU.add).then_inc(s_eas, 1)
                        v.tensor_tensor_reduce(mk[0:PB, s, :], mpos[0:PB, r, :], ps[0:PB, 4, 0:TE], 1.0, 4.0 * BIG,
                                               ALU.add, ALU.min, tmin[0:PB, r:r + 1]).then_inc(s_tmin, 1)

                    def weighted(u):
                        s, r = (j - 2) % 2, (j - 2) % 4
                        return v.tensor_tensor_reduce(zs[:, s, u, 0:D], zs[:, s, u, 0:D], att_relu[:, :], 1.0, zs[:, s, u, D:W],
                                                      ALU.mult, ALU.add, nlog[:, r, u:u + 1])

                    if live(k, 2, STEPS):
                        dve.wait_ge(s_relu, base + k - 1)
                        if reused(k, 2, 4) or l:
                            dve.wait_ge(s_lbc, base + k - 5)
                        weighted(0)
                    if live(k, 3, STEPS):
                        r = (j - 3) % 4
                        dve.wait_ge(s_tmin, base + k - 2)
                        if reused(k, 3, 1) or l:
                            dve.wait_ge(s_nm, base + k - 3)
                        if reused(k, 3, 4) or l:
                            dve.wait_ge(s_et, base + k - 6)
                        dve.sem_inc(s_tick)
                        v.tensor_scalar(new_min[0:PB, r:r + 1], tmin[0:PB, r:r + 1], NM[0:PB, bass.ds(block_at(3), 1)], None, ALU.min).then_inc(s_min, 1)
                    if live(k, 0, STEPS):
                        s = j % 4
                        dve.wait_ge(s_row[s], (base + k - s) // 4 * 32 + 32 if isinstance(k, int) else (base // 4 + 1) * 32 + (k - s) * 8)
                        if reused(k, 0, 4) or l:
                            dve.wait_ge(s_mpos, base + k - 3)
                        v.tensor_scalar(ST[0:PB, s, :], dst_b[0:PB, s, :], node_id[0:PB, bass.ds(block_at(0), 1)], None, ALU.is_equal).then_inc(s_st, 1)
                    if live(k, 2, STEPS):
                        weighted(1).then_inc(s_nlog, 1)
                    if live(k, 1, STEPS):
                        s, r = (j - 1) % 2, (j - 1) % XJ
                        dve.wait_ge(s_z, base + k)
                        kk = k - 1
                        dve.wait_ge(s_xj[r], (base + kk - r) // XJ * 32 + 32 if isinstance(k, int) else (base // XJ + 1) * 32 + (kk - r) * (32 // XJ))
                        if reused(k, 1, 2) or l:
                            dve.wait_ge(s_nlog, base + k - 2)
                        v.tensor_tensor(zs[:, s, :, :], xj[:, r, :, :], ps[:, 2 * s:2 * s + 2, 0:W], ALU.add).then_inc(s_zs, 1)
                    if j == UN - 1 and live(k, 0, STEPS):
                        for i in range(LAG):
                            dve.reg_mov(old[i], blocks[UN - LAG + i])
                dve.wait_ge(s_acc, base + STEPS)
                dve.wait_ge(s_nm, base + STEPS)
                if l == 0:
                    link(v.tensor_scalar(col_a[0:PB, :], EAS[0:PB, :, 2], 1.0, None, ALU.max))
                    link(v.reciprocal(col_a[0:PB, :], col_a[0:PB, :]))
                    for i in range(2):
                        link(v.tensor_tensor(ME[0:PB, i, :], EAS[0:PB, :, i], col_a[0:PB, :], ALU.mult))
                    v.engine_nop().then_inc(s_me, 1)
                    dve.wait_ge(s_me_T, 1)
                    dve.wait_ge(s_sT_out, STEPS)
                    v.tensor_copy(ME_T, ps[0:2 * NB, 5, 0:PB]).then_inc(s_me_T_out, 1)
                dve.wait_ge(s_mpos, base + STEPS)
                for i in range(SL):
                    ins = v.tensor_copy(eye[i][0:PB, :], ident[0:PB, 0:PB])
                ins.then_inc(s_eye, 1)
                for k, j in periods(dve, NB, SL, 2):
                    if live(k, 0, NB):
                        dve.wait_ge(s_self_mm, l * NB + k + 1)
                        if reused(k, 0, SL):
                            dve.wait_ge(s_self_q, l * NB + k - SL + 1)
                        dve.sem_inc(s_tick)
                        v.tensor_tensor(xj[0:PB, j, 0:1, :], XL[0:PB, bass.ds(k, 1), :], ps[0:PB, j:j + 1, 0:W], ALU.add).then_inc(s_self_z, 1)
                    if live(k, 2, NB):
                        i = (j - 2) % SL
                        dve.wait_ge(s_self_relu, l * NB + k - 1)
                        if i == 0 and reused(k, 2, SL):
                            dve.wait_ge(s_self_l, l * NB + k - 2)
                        v.tensor_tensor_reduce(xj[0:PB, i, 0, 0:D], xj[0:PB, i, 0, 0:D], att_relu[0:PB, :], 1.0, xj[0:PB, i, 0, D:W],
                                               ALU.mult, ALU.add, ls_slot[0:PB, i:i + 1]).then_inc(s_self_q, 1)
                    if j == 1 and live(k, SL + 1, NB):
                        dve.wait_ge(s_self_q, l * NB + k - 1)
                        dve.sem_inc(s_tick)
                        v.tensor_copy(LS[0:PB, bass.ds(k - SL - 1, SL)], ls_slot[0:PB, :]).then_inc(s_self_l, SL)
                dve.wait_ge(s_self_l, NB * (l + 1))
                link(v.tensor_tensor(col_a[0:PB, :], NM[0:PB, :], LS[0:PB, :], ALU.min))
                v.tensor_tensor(RS[0:PB, :], col_a[0:PB, :], NM[0:PB, :], ALU.subtract)
                v.tensor_tensor(PS_[0:PB, :], col_a[0:PB, :], LS[0:PB, :], ALU.subtract).then_inc(s_self_d, 1)
                dve.wait_ge(s_self_e, l + 1)
                link(v.tensor_tensor(DEN[0:PB, :], DEN[0:PB, :], RS[0:PB, :], ALU.mult))
                link(v.tensor_tensor(DEN[0:PB, :], DEN[0:PB, :], PS_[0:PB, :], ALU.add))
                link(v.reciprocal(DEN[0:PB, :], DEN[0:PB, :]))
                v.tensor_tensor(RS[0:PB, :], RS[0:PB, :], DEN[0:PB, :], ALU.mult)
                link(v.tensor_tensor(PS_[0:PB, :], PS_[0:PB, :], DEN[0:PB, :], ALU.mult))
                v.engine_nop().then_inc(s_self_w, 1)
                for k, j in periods(dve, NB, SL, 0):
                    dve.wait_ge(s_self_t, l * NB + k + 1)
                    dve.sem_inc(s_tick)
                    v.scalar_tensor_tensor(H[0:PB, bass.ds(k, 1), :].rearrange("p o d -> p (o d)"), XL[0:PB, bass.ds(k, 1), 0:D].rearrange("p o d -> p (o d)"),
                                           PS_[0:PB, bass.ds(k, 1)], xj[0:PB, j, 1, 0:D], ALU.mult, ALU.add).then_inc(s_self_h, 1)
                dve.wait_ge(s_self_h, NB * (l + 1))
                dve.wait_ge(s_sum, 2 * l + 1)
                dve.wait_ge(s_rows, 64 * (l + 1))
                link(v.scalar_tensor_tensor(mu, ps[:, 0, 0:D], 1.0 / N, rows[:, 0, :], ALU.mult, ALU.add))
                link(v.tensor_tensor(mu, rows[:, 0, :], mu, ALU.subtract))
                for c in range(CH):
                    v.tensor_tensor(chunk(Hn, c), chunk(Hn, c), over(mu, CB), ALU.add).then_inc(s_sq_in, 1)
                if l == 0:
                    weight_products(1)
                link(v.tensor_scalar(slope_1[:, :], slope[:, :], 1.0, -1.0 if l else 1.0, ALU.subtract, ALU.mult))
                dve.wait_ge(s_sum, 2 * l + 2)
                v.tensor_scalar(scale_row, ps[:, 0, 0:D], 1.0 / N, None, ALU.mult).then_inc(s_var, 1)
                dve.wait_ge(s_root, 2 + l)
                link(v.reciprocal(scale_row, scale_row))
                link(v.tensor_tensor(scale_row, scale_row, rows[:, 1, :], ALU.mult))
            for c in range(CH + 1):
                if c < CH:
                    scaled(c)
                    dve.wait_ge(s_resid, c + 1)
                    v.tensor_tensor(chunk(Hn, c), chunk(Hn, c), chunk(XRn, c), ALU.add).then_inc(s_sum_h, 1)
                if c:
                    h = chunk(Hn, c - 1)
                    dve.wait_ge(s_neg, c)
                    link(v.scalar_tensor_tensor(h, chunk(XRn, c - 1), slope_1[0:PB, :], h, ALU.mult, ALU.add))
                    link(v.tensor_tensor(h, h, chunk(XLn, c - 1), ALU.add))
            v.engine_nop().then_inc(s_free, 1)
            layer_norm_sums(Hn, 5)
            dve.wait_ge(s_root, 4)
            link(v.reciprocal(ln_rstd[0:PB, :], ln_rstd[0:PB, :]))
            with dve.Fori(0, NB // 5) as turn:
                for u in range(5):
                    k = turn * 5 + u
                    v.tensor_scalar(XL[0:PB, bass.ds(k, 1), 0:D].rearrange("p o d -> p (o d)"), H[0:PB, bass.ds(k, 1), :].rearrange("p o d -> p (o d)"),
                                    ln_mean[0:PB, bass.ds(k, 1)], ln_rstd[0:PB, bass.ds(k, 1)], ALU.subtract, ALU.mult).then_inc(s_ln2, 1)
            v.memset(zero_rows, 0.0).then_inc(s_zero_src, 1)
            v.tensor_scalar(triu[0:PB, 0:PB], iota_row[0:PB, 0:PB], iota_col[0:PB, :], None, ALU.is_ge)
            v.tensor_scalar(e_off, iota_row[:, 0:NX], -float(NX), None, ALU.add)
            link(v.memset(chain_mask, 1.0))
            link(v.memset(chain_mask.rearrange("p (e b) -> p e b", e=NX)[:, :, 0:1], 0.0))
            dve.wait_ge(s_b1T, 1)
            v.tensor_copy(b1T[:, :], ps[:, 6, 0:NX * FC]).then_inc(s_b1T, 1)
            dve.wait_ge(s_gate, NB)

            def per_b(col):
                return col[0:PB, :].unsqueeze(2).to_broadcast([PB, NB, NX])

            def per_e(row):
                return row[0:PB, :].unsqueeze(1).to_broadcast([PB, NB, NX])

            n = PB
            pr, oh = be(probs[0:n]), be(onehot[0:n])
            link(v.tensor_tensor(pr, be(ps[0:n, 7, 0:NE]), per_e(gb_sb), ALU.add))
            link(v.tensor_reduce(top[0:n], pr, AX_X, ALU.max))
            v.tensor_tensor(pr, pr, per_b(top), ALU.subtract).then_inc(s_shift, 1)
            dve.wait_ge(s_exp, 1)
            link(v.tensor_reduce(top[0:n], pr, AX_X, ALU.add))
            link(v.reciprocal(top[0:n], top[0:n]))
            link(v.tensor_tensor(pr, pr, per_b(top), ALU.mult))
            link(v.tensor_reduce(top[0:n], pr, AX_X, ALU.max))
            link(v.tensor_tensor(oh, pr, per_b(top), ALU.is_ge))
            link(v.tensor_tensor(oh, oh, per_e(e_off), ALU.mult))
            link(v.tensor_reduce(first_e[0:n], oh, AX_X, ALU.min))
            v.tensor_tensor(oh, per_e(e_off), per_b(first_e), ALU.is_equal).then_inc(s_onehot, 1)
            dve.wait_ge(s_cum, 1)
            tot_v = tot_eb[0:n].rearrange("p (e b) -> p b e", e=NX)
            link(v.tensor_copy(tot_v, be(ps[0:n, 1, 0:NE])))
            link(v.tensor_tensor_scan(base_eb[0:n], chain_mask[0:n], tot_eb[0:n], 0.0, ALU.mult, ALU.add))
            link(v.tensor_tensor(base_eb[0:n], base_eb[0:n], tot_eb[0:n], ALU.subtract))
            link(v.tensor_tensor(be(cum[0:n]), be(ps[0:n, 0, 0:NE]), base_eb[0:n].rearrange("p (e b) -> p b e", e=NX), ALU.add))
            link(v.tensor_tensor(be(cum[0:n]), be(cum[0:n]), oh, ALU.mult))
            link(v.tensor_reduce(pos[0:n], be(cum[0:n]), AX_X, ALU.add))
            link(v.tensor_scalar(pos[0:n], pos[0:n], -1.0, None, ALU.add))
            link(v.tensor_scalar(kept[0:n], pos[0:n], float(CAP), None, ALU.is_lt))
            link(v.tensor_tensor(coef[0:n], top[0:n], kept[0:n], ALU.mult))
            link(v.tensor_scalar(first_e[0:n], first_e[0:n], float(NX), float(CAP), ALU.add, ALU.mult))
            link(v.tensor_tensor(slot_f[0:n], first_e[0:n], pos[0:n], ALU.add))
            link(v.tensor_scalar(slot_f[0:n], slot_f[0:n], -float(NX * CAP), None, ALU.add))
            link(v.tensor_tensor(slot_f[0:n], slot_f[0:n], node_id[0:n, :], ALU.subtract))
            link(v.tensor_tensor(slot_f[0:n], slot_f[0:n], kept[0:n], ALU.mult))
            link(v.tensor_tensor(slot_f[0:n], slot_f[0:n], node_id[0:n, :], ALU.add))
            link(v.tensor_scalar(slot_f[0:n], slot_f[0:n], float(NX * CAP), None, ALU.add))
            link(v.tensor_copy(slot_put[0:n], slot_f[0:n]))
            link(v.tensor_scalar(pos[0:n], pos[0:n], float(CAP - 1), None, ALU.min))
            link(v.tensor_tensor(slot_f[0:n], first_e[0:n], pos[0:n], ALU.add))
            link(v.tensor_copy(slot_get[0:n], slot_f[0:n]))
            v.engine_nop().then_inc(s_slots, 1)
            M = len(MT)
            n = PB
            v.memset(y_zero, 0.0)
            link(v.memset(y_zeros, 0.0))
            link(v.tensor_scalar(slot_f[0:n], coef[0:n], 0.0, None, ALU.mult))
            link(v.tensor_reduce(y_zeros[0:n, 0:1], slot_f[0:n], AX_X, ALU.add))
            dve.wait_ge(s_put, 16 * NB)
            with dve.Fori(0, NX // 2) as pair:
                for s in range(2):
                    e = pair * 2 + s
                    for m, (m0, mn) in enumerate(MT):
                        dve.wait_ge(s_tokT, e * M + m + 1)
                        v.tensor_copy(tokT[:, :, m0:m0 + mn], ps[:, 6 + m % 2, 0:D].rearrange("p (c t) -> p c t", c=2)[:, :, 0:mn]).then_inc(s_tokT_out, 1)
                    for m, (m0, mn) in enumerate(MT):
                        dve.wait_ge(s_down, e * M + m + 1)
                        if m == 0:
                            dve.wait_ge(s_y_out, e * 32)
                            dve.wait_ge(s_wx[s], pair * 48 + 48)
                        v.tensor_tensor(y_sb[0:mn, m, :], ps[0:mn, 4 + m % 2, 0:D], b2B[0:mn, s * D:(s + 1) * D], ALU.add).then_inc(s_y, 1)
                        dve.wait_ge(s_y, e * M + m + 1)
                        if m:
                            dve.wait_ge(s_y_chk, e * (M + 1) + m)
                        dve.sem_inc(s_tick)
                        v.tensor_tensor_reduce(junk[0:mn, 0:D], y_sb[0:mn, m, :], zero_rows[0:mn, 0:D], 1.0, 0.0,
                                               ALU.mult, ALU.add, y_zero[0:mn, m:m + 1]).then_inc(s_y_chk, 1)
                    dve.wait_ge(s_y_chk, e * (M + 1) + M)
                    dve.sem_inc(s_tick)
                    v.tensor_tensor(y_zeros, y_zeros, y_zero, ALU.add).then_inc(s_y_chk, 1)
                    dve.wait_ge(s_y_chk, e * (M + 1) + M + 1)
            link(v.tensor_reduce(bad[:, :], y_zeros, AX_X, ALU.add))
            link(v.tensor_scalar(bad[:, :], bad[:, :], 0.0, None, ALU.is_equal))
            v.tensor_scalar(bad[:, :], bad[:, :], -1.0, 1.0, ALU.mult, ALU.add).then_inc(s_bad, 1)
            dve.wait_ge(s_bad_sum, 1)
            v.tensor_scalar(not_finite[:, :], ps[0:1, 7, 0:1], 0.0, None, ALU.is_gt).then_inc(s_bad_flag, 1)
            dve.wait_ge(s_bad_flag, 1)
            bad_flag = nc.values_load(not_finite[0:1, 0:1], engines=DVE_ONLY, min_val=0, max_val=1,
                                      skip_runtime_bounds_check_because="DVE writes 0 or 1")
            with dve.If(bad_flag != 0):
                for c in range(CH):
                    dve.wait_ge(s_get[c], 16 * CB)
                link(v.tensor_tensor(XLn, XLn, wide(coef), ALU.mult))
                FMAX = 3.4028234663852886e38
                half = NB // 2
                cells = half * D
                for h in range(2):
                    y = XL[0:PB, h * half:(h + 1) * half, 0:D]
                    mask = XRf[0:PB, 0:cells].bitcast(I32).rearrange("p (b d) -> p b d", b=half)
                    clean = XRf[0:PB, cells:2 * cells].rearrange("p (b d) -> p b d", b=half)
                    link(v.memset(clean, 0.0))
                    link(v.tensor_tensor(mask, y, y, ALU.is_equal))
                    link(v.copy_predicated(clean, mask, y))
                    for op, bound, value in ((ALU.is_gt, FMAX, 1.0e4), (ALU.is_lt, -FMAX, -1.0e4)):
                        link(v.memset(junk[:, 0:1], value))
                        link(v.tensor_scalar(mask, y, bound, None, op))
                        link(v.copy_predicated(clean, mask, junk[0:PB, 0:1].unsqueeze(1).to_broadcast([PB, half, D])))
                    link(v.tensor_copy(y, clean))
                link(v.memset(coef, 1.0))
            for c in range(CH):
                dve.wait_ge(s_get[c], 16 * CB)
                with dve.Fori(0, CB // 5) as turn:
                    for u in range(5):
                        k = turn * 5 + (c * CB + u)
                        h = H[0:PB, bass.ds(k, 1), :].rearrange("p o d -> p (o d)")
                        v.scalar_tensor_tensor(h, XL[0:PB, bass.ds(k, 1), 0:D].rearrange("p o d -> p (o d)"),
                                               coef[0:PB, bass.ds(k, 1)], h, ALU.mult, ALU.add).then_inc(s_fin, 1)


_INS = ["x", "src", "dst", "edge_attr_2"]
_LAYER = ["Wl", "Wr", "We", "att", "b", "g", "beta", "a"]
_FFN = ["gate_w", "gate_b", "w1", "b1", "w2", "b2"]


def kernel(**inputs):
    import numpy as np
    import concourse.bacc as bacc
    from concourse.bass_utils import run_bass_kernel_spmd as run

    nc = bacc.Bacc("TRN2", target_bir_lowering=False, num_devices=1, dynamic_dma_scratch_size=8192)
    arrays = {}

    def given(name):
        a = np.ascontiguousarray(inputs[name])
        if a.ndim == 0:
            a = a.reshape(1)
        arrays["in_" + name] = a
        return nc.dram_tensor("in_" + name, a.shape, mybir.dt.from_np(a.dtype), kind="ExternalInput").ap()

    ins = [given(n) for n in _INS]
    layers = [[given(f"L0_gnn_{n}{l}") for n in _LAYER] for l in (1, 2)]
    ffn = [given("L0_ffn_" + n) for n in _FFN]
    out = nc.dram_tensor("out_0", inputs["x"].shape, F32, kind="ExternalOutput").ap()
    program(nc, *ins, layers, *ffn, out)
    return run(nc, [arrays], core_ids=[0]).results[0]["out_0"]
```

```python
from contextlib import ExitStack
from itertools import chain

import concourse.bass as bass
from concourse import mybir

ALU = mybir.AluOpType
ACT = mybir.ActivationFunctionType
AX_X = mybir.AxisListType.X
F32 = mybir.dt.float32
I32 = mybir.dt.int32
DVE_ONLY = (mybir.EngineType.DVE,)
ACT_ONLY = (mybir.EngineType.Activation,)
PE_ONLY = (mybir.EngineType.PE,)
POOL_ONLY = (mybir.EngineType.Pool,)
SP_ONLY = (mybir.EngineType.SP,)

BIG = 1.0e30
START = 1.0e29
EPS = 1e-5
PAD_DST = 1000000
IN_RANGE = "the staircase table holds block and tile numbers, which the chip works out in range"


def periods(engine, steps, unroll, lag):
    for k in range(unroll):
        yield k, k
    with engine.Fori(1, steps // unroll) as turn:
        for j in range(unroll):
            yield turn * unroll + j, j
    for k in range(steps, steps + lag):
        yield k, k % unroll


def live(k, lag, steps):
    return not isinstance(k, int) or 0 <= k - lag < steps


def reused(k, lag, ring):
    return not isinstance(k, int) or k - lag >= ring


def program(nc, x, src, dst, ea, layers, gate_w, gate_b, w1, b1, w2, b2, out):
    N, D = x.shape
    E = src.shape[0]
    NX, C_OUT = gate_w.shape[1], w1.shape[2]
    P = 128
    PB = 125
    NB = N // PB
    assert NB * PB == N and D == 256
    G = 2
    TE = G * P
    T = -(-E // TE)
    ROWS = T * G
    FULL = E // P
    REST = E - FULL * P
    K7 = -(-ROWS // P)
    LASTK = ROWS - (K7 - 1) * P
    STEPS = T + NB - 1
    W = D + 1
    UN = 8
    LAG = 5
    assert STEPS % UN == 0
    CAP = -(-5 * N // (4 * NX))
    HC = -(-CAP // 2)
    HALVES = [(0, HC), (HC, CAP - HC)]
    MT = [(m, min(P, CAP - m)) for m in range(0, CAP, P)]
    FC = C_OUT // P
    CH = 5
    CB = NB // CH
    assert CH * CB == NB
    SL = 5
    assert NB % SL == 0 and CB % 2 == 0 and CB == 2 * SL

    SC = E // PB
    assert SC * PB == E
    NPAD = ROWS * P - E
    assert NPAD <= P

    sorted_edges = nc.dram_tensor("sorted_edges", (ROWS * P, 4), F32, kind="Internal").ap()
    dst_rows = nc.dram_tensor("dst_rows", (ROWS * P,), F32, kind="Internal").ap()
    ea_rows = nc.dram_tensor("ea_rows", (2, ROWS * P), F32, kind="Internal").ap()
    xl_table = [nc.dram_tensor(f"xl_table{l}", (N, W), F32, kind="Internal").ap() for l in range(2)]
    tok_buf = nc.dram_tensor("tok_buf", (NX * CAP + N, W), F32, kind="Internal").ap()
    me_rows = nc.dram_tensor("me_rows", (2, N), F32, kind="Internal").ap()
    y_tok = nc.dram_tensor("y_tok", (N + len(MT) * P, D), F32, kind="Internal").ap()

    with ExitStack() as ctx:
        def sb(name, shape, dt=F32):
            return ctx.enter_context(nc.sbuf_tensor(name, shape, dt))

        def sem(name):
            return ctx.enter_context(nc.semaphore(name))

        H = sb("H", [P, NB, D])
        XR = sb("XR", [P, NB, W])
        XL = sb("XL", [P, NB, W])
        Hn, XRn, XLn = H[0:PB], XR[0:PB, :, 0:D], XL[0:PB, :, 0:D]
        XLf = XL[:, :, :].rearrange("p b w -> p (b w)")
        XRf = XR[:, :, :].rearrange("p b w -> p (b w)")
        ps = ctx.enter_context(nc.psum_tensor("ps", [P, 8, 512], F32))

        ident = sb("ident", [P, P])
        ones = sb("ones", [P, P])
        iota_i = sb("iota_i", [P, P], I32)
        iota_ci = sb("iota_ci", [P, 1], I32)
        iota_row = sb("iota_row", [P, P])
        iota_col = sb("iota_col", [P, 1])
        node_id = sb("node_id", [P, NB])
        eps_col = sb("eps_col", [P, 1])
        src_cols = sb("src_cols", [P, K7 * P], I32)
        block_of = sb("block_of", [1, STEPS], I32)
        tile_of = sb("tile_of", [1, STEPS], I32)

        Wlr = sb("Wlr", [P, 2, 2 * W])
        WeB = sb("WeB", [P, 2, W])
        att_relu = sb("att_relu", [P, D])
        att_lin = sb("att_lin", [P, D])
        rows = sb("rows", [P, 3, D])
        slope = sb("slope", [P, 1])
        junk = sb("junk", [P, W])
        ln_mean = sb("ln_mean", [P, NB])
        ln_rstd = sb("ln_rstd", [P, NB])
        col_a = sb("col_a", [P, NB])
        slope_1 = sb("slope_1", [P, 1])

        XJ = 8
        xj = sb("xj", [P, XJ, G, W])
        dst_b = sb("dst_b", [P, 4, TE])
        ST = sb("ST", [P, 4, TE])
        mpos = sb("mpos", [P, 4, TE])
        zs = sb("zs", [P, 2, G, W])
        mu, scale_row = zs[:, 0, 0, 0:D], zs[:, 0, 1, 0:D]
        mk = sb("mk", [P, 2, TE])
        ETs = sb("ETs", [P, 2, TE])
        Es = sb("Es", [P, 2, G, PB])
        staged = mk
        hT = Es
        Srow = sb("Srow", [P, 2, G, P])
        src_slot = sb("src_slot", [P, XJ, G], I32)
        nlog = sb("nlog", [P, 4, G])
        old_min = sb("old_min", [P, 4])
        new_min = sb("new_min", [P, 4])
        resc = sb("resc", [P, 4])
        den_t = sb("den_t", [P, 4])
        NM = sb("NM", [P, NB])
        DEN = sb("DEN", [P, NB])
        EAS = sb("EAS", [P, NB, 3])
        ME = sb("ME", [P, 2, NB])
        LS = sb("LS", [P, NB])
        RS = sb("RS", [P, NB])
        PS_ = sb("PS_", [P, NB])
        ls_slot = sb("ls_slot", [P, SL])
        STf = ST[:, :, :].rearrange("p s e -> p (s e)")
        eye = [STf[:, i * PB:(i + 1) * PB] for i in range(SL)]
        ME_T = Srow[0:2 * NB, 0, 0, 0:PB]
        bad = sb("bad", [P, 1])
        not_finite = sb("not_finite", [1, 1], I32)

        unsorted_f = sb("unsorted_f", [P, 1])
        unsorted = sb("unsorted", [1, 1], I32)
        place_f = sb("place_f", [P, 1])
        place = sb("place", [P, 1], I32)
        edge_slot = sb("edge_slot", [P, 4])

        o = 0
        def carve(base, n, dt=F32):
            nonlocal o
            v = base[:, o:o + n]
            o += n
            return v if dt == F32 else v.bitcast(dt)
        src_i = carve(XLf, K7 * P, I32).rearrange("p (k e) -> p k e", k=K7)
        dst_i = carve(XLf, K7 * P, I32).rearrange("p (k e) -> p k e", k=K7)
        src_f = carve(XLf, K7 * P).rearrange("p (k e) -> p k e", k=K7)
        dst_f = carve(XLf, K7 * P).rearrange("p (k e) -> p k e", k=K7)
        ea_in = carve(XLf, 2 * K7 * P).rearrange("p (k e j) -> p k e j", k=K7, j=2)
        loaded_edges = XLf[:, o:o + 4 * K7 * P].rearrange("p (k e f) -> p k e f", k=K7, f=4)
        ea_pl = carve(XLf, 2 * K7 * P).rearrange("p (k j e) -> p k j e", k=K7, j=2)
        last_dst = carve(XLf, K7 * P)
        reached = carve(XLf, 512)
        after = carve(XLf, STEPS)
        step_iota = carve(XLf, STEPS)
        step_iota_i = carve(XLf, STEPS, I32)
        block_f = carve(XLf, STEPS)
        tau = carve(XLf, 2)
        dst_s = carve(XLf, SC + 1, I32)
        descents = carve(XLf, SC)
        o = 0
        src_s = carve(XRf, SC, I32)
        ea_s = carve(XRf, 2 * SC).rearrange("p (c j) -> p c j", j=2)
        edge_s = carve(XRf, 4 * SC).rearrange("p (c f) -> p c f", f=4)
        edge_dst = carve(XRf, SC)
        block_start = carve(XRf, NB + 1)
        beyond = carve(XRf, NB + 1)
        is_beyond = carve(XRf, NB + 1)
        in_block = carve(XRf, NB)
        places = carve(XRf, NB)
        place_of = carve(XRf, NB)
        before = carve(XRf, PB)
        pad_edge = carve(XRf, 4)

        o = 0
        w1_sb = carve(XRf, 2 * 2 * C_OUT).rearrange("p (s c f) -> p s c f", s=2, c=2)
        w2_sb = carve(XRf, 2 * FC * D).rearrange("p (s f d) -> p s f d", s=2, f=FC)
        tok = carve(XRf, len(MT) * W).rearrange("p (m d) -> p m d", m=len(MT))
        y_sb = carve(XRf, len(MT) * D).rearrange("p (m d) -> p m d", m=len(MT))
        o = 0
        tokT = carve(XLf, 2 * CAP).rearrange("p (c t) -> p c t", c=2)
        hidT = carve(XLf, FC * CAP).rearrange("p (f t) -> p f t", f=FC)
        o = 0
        xjf = xj[:, :, :, :].rearrange("p s g w -> p (s g w)")
        NE = CB * NX
        def be(v):
            return v.rearrange("p (b e) -> p b e", e=NX)
        probs, onehot, cum, base_eb, tot_eb, chain_mask = (carve(xjf, NE) for _ in range(6))
        earlier = carve(xjf, NX)
        total = carve(xjf, NX)
        ln2_mean, ln2_rstd = carve(xjf, NB), carve(xjf, NB)
        stats = carve(xjf, NB * 6).rearrange("p (b s) -> p b s", s=6)
        y_zero = carve(xjf, len(MT))
        y_zeros = carve(xjf, len(MT))
        place_no = carve(xjf, len(MT))
        id_f = carve(xjf, len(MT))
        tok_id = [carve(xjf, len(MT), I32) for _ in range(2)]
        zf = zs[:, :, :, :].rearrange("p s g w -> p (s g w)")
        o = 2 * W
        gw_sb = carve(zf, 2 * NX).rearrange("p (c e) -> p c e", c=2)
        gb_sb = carve(zf, NX)
        e_off = carve(zf, NX)
        top, first_e, pos, kept, slot_f, coef = (carve(zf, NB) for _ in range(6))
        slot_put = carve(zf, NB, I32)
        assert o <= 4 * W
        triu = Srow[:, 0, 0, :]
        g_rows = [ST[:, i, :] for i in range(4)] + [dst_b[:, 0, :]]
        g_T = [Es[:, i, :, :] for i in range(2)] + [v[:, 0:2 * PB].rearrange("p (c n) -> p c n", c=2)
                                                    for v in (ETs[:, 1, :], dst_b[:, 1, :], dst_b[:, 2, :])]
        G_BANKS = (4, 5, 6, 2, 1)
        b1_rows = ETs[0:NX * FC, 0, 0:P]
        b1T = sb("b1T", [P, NX * FC])
        b2B = Wlr[:, :, :].rearrange("p c w -> p (c w)")
        zero_rows = mpos[:, 0:2, :].rearrange("p s e -> p (s e)")[:, 0:W]
        XR_zero = Srow[0:1, :, :, :].rearrange("p s g e -> p (s g e)")[:, 0:W].unsqueeze(1).to_broadcast([1, NB, W])

        s_pad = sem("s_pad")
        s_fixed = sem("s_fixed")
        s_edges = sem("s_edges")
        s_dst_s = sem("s_dst_s")
        s_descents = sem("s_descents")
        s_descents_sum = sem("s_descents_sum")
        s_flag = sem("s_flag")
        s_sort_in = sem("s_sort_in")
        s_sort_pad = sem("s_sort_pad")
        s_sort_link = sem("s_sort_link")
        s_sort_total = sem("s_sort_total")
        s_sort_rank = sem("s_sort_rank")
        s_sort_slot = sem("s_sort_slot")
        s_sort_put = sem("s_sort_put")
        s_sort_pads = sem("s_sort_pads")
        s_sort_back = sem("s_sort_back")
        s_edges_f = sem("s_edges_f")
        s_edges_out = sem("s_edges_out")
        s_consts = sem("s_consts")
        s_last = sem("s_last")
        s_srcT = sem("s_srcT")
        s_srcT_out = sem("s_srcT_out")
        s_after = sem("s_after")
        s_blocks = sem("s_blocks")
        s_stairs = sem("s_stairs")
        s_x = [sem(f"s_x_in{c}") for c in range(CH)]
        s_cleared = sem("s_cleared")
        s_var = sem("s_var")
        s_root = sem("s_root")
        s_w = sem("s_w")
        s_wext = sem("s_wext")
        s_we = sem("s_we")
        s_feat = sem("s_feat")
        s_in_link = sem("s_in_link")
        s_rows = sem("s_rows")
        s_me = sem("s_me")
        s_me_T = sem("s_me_T")
        s_me_T_out = sem("s_me_T_out")
        s_me_rows = sem("s_me_rows")
        s_eye = sem("s_eye")
        s_eye_me = [sem(f"s_eye_me{i}") for i in range(SL)]
        s_self_mm = sem("s_self_mm")
        s_staged = sem("s_staged")
        s_tp, s_hT, s_lin, s_xr, s_xl = (sem(n) for n in ("s_tp", "s_hT", "s_lin", "s_xr", "s_xl"))
        s_table = sem("s_table")
        s_state = sem("s_state")
        s_row = [sem(f"s_row{i}") for i in range(4)]
        s_xj = [sem(f"s_xj{i}") for i in range(XJ)]
        s_idx = sem("s_idx")
        s_tick = sem("s_tick")
        s_st, s_z, s_mpos, s_zs, s_relu, s_nlog, s_lbc, s_min, s_et, s_etT, s_e, s_agg, s_acc = (
            sem(n) for n in ("s_st", "s_z", "s_mpos", "s_zs", "s_relu", "s_nlog", "s_lbc", "s_min", "s_et", "s_etT",
                             "s_e", "s_agg", "s_acc"))
        s_sT, s_sT_out = sem("s_sT"), sem("s_sT_out")
        s_den = sem("s_den")
        s_old = sem("s_old")
        s_nm = sem("s_nm")
        s_eas = sem("s_eas")
        s_num = sem("s_num")
        s_self_q = sem("s_self_q")
        s_link = sem("s_link")
        s_self_z, s_self_relu, s_self_l = sem("s_self_z"), sem("s_self_relu"), sem("s_self_l")
        s_self_d, s_self_e = sem("s_self_d"), sem("s_self_e")
        s_self_w, s_self_t, s_self_h = sem("s_self_w"), sem("s_self_t"), sem("s_self_h")
        s_sum = sem("s_sum")
        s_sq_in, s_sq = sem("s_sq_in"), sem("s_sq")
        s_x2 = sem("s_x2")
        s_resid = sem("s_resid")
        s_sum_h = sem("s_sum_h")
        s_neg = sem("s_neg")
        s_free = sem("s_free")
        s_moe_w = sem("s_moe_w")
        s_b1T = sem("s_b1T")
        s_xl2 = sem("s_xl2")
        s_g_tp, s_g_T, s_gate = sem("s_g_tp"), sem("s_g_T"), sem("s_gate")
        s_shift, s_exp = sem("s_shift"), sem("s_exp")
        s_onehot, s_cum = sem("s_onehot"), sem("s_cum")
        s_slots = sem("s_slots")
        s_zero = sem("s_zero")
        s_zero_src = sem("s_zero_src")
        s_put = sem("s_put")
        s_wx = [sem(f"s_wx{i}") for i in range(2)]
        s_tok = sem("s_tok")
        s_tokT, s_tokT_out = sem("s_tokT"), sem("s_tokT_out")
        s_up, s_hid, s_down, s_y = sem("s_up"), sem("s_hid"), sem("s_down"), sem("s_y")
        s_id_f = sem("s_id_f")
        s_ids = sem("s_ids")
        s_y_put = sem("s_y_put")
        s_get = [sem(f"s_get{c}") for c in range(CH)]
        s_bad = sem("s_bad")
        s_bad_sum = sem("s_bad_sum")
        s_bad_flag = sem("s_bad_flag")
        s_y_chk = sem("s_y_chk")
        s_fin = sem("s_fin")
        s_out = sem("s_out")

        GATE = (7, 3)
        ZEROED = 16 * (2 + (NX * CAP % P > 0) + (N % P > 0))
        PARTS = [(0, 112), (112, PB)]

        def flag_of(engines):
            return nc.values_load(unsorted[0:1, 0:1], engines=engines, min_val=0, max_val=1,
                                  skip_runtime_bounds_check_because="DVE writes 0 or 1")

        STEP_LINKS = 5
        SORT_LINKS = 2 + SC

        def blocks_by_chunk(engine, l):
            if l:
                yield from periods(engine, NB, 2, 1)
                return
            for c in range(CH):
                for j in range(2):
                    yield c * CB + j, j
                with engine.Fori(1, CB // 2) as turn:
                    for j in range(2):
                        yield turn * 2 + (c * CB + j), j
            yield NB, 0

        def chunk(v, c):
            return v[:, c * CB:(c + 1) * CB]

        block = ctx.enter_context(nc.Block())

        @block.sync
        def _(sp):
            x_v = x.rearrange("(b p) d -> p b d", p=PB)
            out_v = out.rearrange("(b p) d -> p b d", p=PB)

            sp.wait_ge(s_pad, 1)
            KF = K7 - 1
            sp.dma_start(dst_s[0:PB, 0:SC], dst.rearrange("(p c) -> p c", p=PB)).then_inc(s_dst_s, 16)
            sp.dma_start(dst_s[0:PB - 1, SC:SC + 1], dst[SC:E].rearrange("(p c) -> p c", c=SC)[:, 0:1], allow_slow_non_contiguous=True).then_inc(s_dst_s, 16)
            for flat, tile in ((src, src_i), (dst, dst_i)):
                sp.dma_start(tile[:, 0:KF, :], flat[0:KF * P * P].rearrange("(k q e) -> q k e", q=P, e=P)).then_inc(s_edges, 16)
                sp.dma_start(tile[0:FULL - KF * P, KF, :], flat[KF * P * P:FULL * P].rearrange("(q e) -> q e", e=P)).then_inc(s_edges, 16)
                sp.dma_start(tile[FULL - KF * P:FULL - KF * P + 1, KF, 0:REST], flat[FULL * P:E].rearrange("(q e) -> q e", q=1)).then_inc(s_edges, 16)
            sp.dma_start(ea_in[:, 0:KF], ea[0:KF * P * P, :].rearrange("(k q e) j -> q k e j", q=P, e=P)).then_inc(s_edges, 16)
            sp.dma_start(ea_in[0:FULL - KF * P, KF], ea[KF * P * P:FULL * P, :].rearrange("(q e) j -> q e j", e=P)).then_inc(s_edges, 16)
            sp.dma_start(ea_in[FULL - KF * P:FULL - KF * P + 1, KF, 0:REST, :], ea[FULL * P:E, :].rearrange("(q e) j -> q e j", q=1)).then_inc(s_edges, 16)
            for c in range(CH):
                for a, b_ in PARTS:
                    sp.dma_start(chunk(H[a:b_], c), chunk(x_v[a:b_], c)).then_inc(s_x[c], 16)
            sp.wait_ge(s_fixed, 1)
            sp.dma_start(XR[P - 1:P, :, :], XR_zero).then_inc(s_we, 16)

            sp.wait_ge(s_flag, 1)
            with sp.If(flag_of(SP_ONLY) != 0):
                sp.wait_ge(s_sort_pad, 1)
                sp.dma_start(src_s[0:PB], src.rearrange("(p c) -> p c", p=PB)).then_inc(s_sort_in, 16)
                sp.dma_start(ea_s[0:PB], ea.rearrange("(p c) j -> p c j", p=PB)).then_inc(s_sort_in, 16)
                sp.dma_start(sorted_edges[E:ROWS * P, :], pad_edge[0:NPAD, :]).then_inc(s_sort_pads, 16)
                sp.wait_ge(s_sort_pads, 16)
                sp.wait_ge(s_sort_put, 16 * SC)
                sp.dma_start(loaded_edges[:, 0:KF], sorted_edges[0:KF * P * P, :].rearrange("(k q e) f -> q k e f", q=P, e=P)).then_inc(s_sort_back, 16)
                sp.dma_start(loaded_edges[0:LASTK, KF], sorted_edges[KF * P * P:, :].rearrange("(q e) f -> q e f", e=P)).then_inc(s_sort_back, 16)

            sp.wait_ge(s_edges_f, 2)
            sp.dma_start(dst_rows[0:KF * P * P].rearrange("(k q e) -> q k e", q=P, e=P), dst_f[:, 0:KF, :]).then_inc(s_edges_out, 16)
            sp.dma_start(dst_rows[KF * P * P:].rearrange("(q e) -> q e", e=P), dst_f[0:LASTK, KF, :]).then_inc(s_edges_out, 16)
            for j in range(2):
                sp.dma_start(ea_rows[j, 0:KF * P * P].rearrange("(k q e) -> q k e", q=P, e=P), ea_pl[:, 0:KF, j, :]).then_inc(s_edges_out, 16)
                sp.dma_start(ea_rows[j, KF * P * P:].rearrange("(q e) -> q e", e=P), ea_pl[0:LASTK, KF, j, :]).then_inc(s_edges_out, 16)

            for l, (Wl, Wr, We, att_d, b_d, g_d, beta_d, a_d) in enumerate(layers):
                base = l * STEPS
                if l:
                    sp.wait_ge(s_self_l, NB)
                sp.dma_start(Wlr[:, :, 0:D], Wl.rearrange("(c k) n -> k c n", c=2)).then_inc(s_w, 16)
                sp.dma_start(Wlr[:, :, W:W + D], Wr.rearrange("(c k) n -> k c n", c=2)).then_inc(s_w, 16)
                sp.dma_start(WeB[:, :, 0:D], We.partition_broadcast(P)).then_inc(s_w, 16)
                sp.dma_start(att_relu[:, :], att_d.partition_broadcast(P)).then_inc(s_w, 16)
                sp.wait_ge(s_wext, l + 1)
                for j in range(2):
                    sp.dma_start(XR[PB + j:PB + j + 1, :, :], WeB[0:1, j:j + 1, :].to_broadcast([1, NB, W])).then_inc(s_we, 16)
                if l:
                    sp.wait_ge(s_feat, NB // 2)
                for i, v in enumerate((b_d, g_d, beta_d)):
                    sp.dma_start(rows[:, i, :], v.partition_broadcast(P)).then_inc(s_rows, 16)
                sp.dma_start(slope[:, :], a_d.partition_broadcast(P)).then_inc(s_rows, 16)
                xl_v = xl_table[l].rearrange("(b p) w -> p b w", p=PB)
                for c in range(CH):
                    sp.wait_ge(s_xl, NB * l + CB * (c + 1))
                    for a, b_ in PARTS:
                        sp.dma_start(xl_v[a:b_, c * CB:(c + 1) * CB], XL[a:b_, c * CB:(c + 1) * CB]).then_inc(s_table, 16)
                sp.wait_ge(s_edges_out, 16 * 6)
                sp.wait_ge(s_stairs, 1)
                tiles = None
                for k, j in periods(sp, STEPS, UN, 0):
                    if j == 0:
                        _, tiles = nc.values_load_multi_w_load_instructions(
                            tile_of[0:1, bass.ds(k, UN)], engines=SP_ONLY, min_val=0, max_val=T - 1,
                            skip_runtime_bounds_check_because=IN_RANGE)
                    s = k % 4 if isinstance(k, int) else j % 4
                    if reused(k, 0, 4) or l:
                        sp.wait_ge(s_z, base + k - 3)
                    if l == 0 and reused(k, 0, 4):
                        sp.wait_ge(s_sT, k - 3)
                    sp.dma_start(dst_b[:, s, :], dst_rows[bass.ds(tiles[j] * TE, TE)].partition_broadcast(P)).then_inc(s_row[s], 16)
                    sp.dma_start(ST[PB:PB + 2, s, :], ea_rows[:, bass.ds(tiles[j] * TE, TE)]).then_inc(s_row[s], 16)
                if l == 0:
                    sp.wait_ge(s_me_T_out, 1)
                    sp.dma_start(me_rows.rearrange("j (b p) -> (j b) p", p=PB), ME_T).then_inc(s_me_rows, 16)
                    sp.wait_ge(s_me_rows, 16)
                sp.wait_ge(s_z, base + STEPS)
                for k, j in periods(sp, NB, SL, 0):
                    if reused(k, 0, SL) or l:
                        sp.wait_ge(s_self_mm, l * NB + k - SL + 1)
                    sp.dma_start(eye[j][PB:PB + 2, :], me_rows[:, bass.ds(k * PB, PB)]).then_inc(s_eye_me[j], 16)

            sp.wait_ge(s_self_h, 2 * NB)
            for a, b_ in PARTS:
                sp.dma_start(XL[a:b_, :, 0:D], x_v[a:b_]).then_inc(s_x2, 16)

            sp.dma_start(gw_sb, gate_w.rearrange("(c k) e -> k c e", c=2)).then_inc(s_moe_w, 16)
            sp.dma_start(gb_sb, gate_b.partition_broadcast(P)).then_inc(s_moe_w, 16)
            sp.dma_start(b1_rows, b1.rearrange("e (f k) -> (e f) k", k=P)).then_inc(s_moe_w, 16)
            sp.wait_ge(s_zero_src, 1)
            cleared = 0
            for buf, width, R in ((tok_buf, W, NX * CAP), (y_tok, D, N)):
                RP = R // P * P
                for r0, n, v in ((0, RP, buf[0:RP, :].rearrange("(p r) d -> p r d", p=P)), (RP, R - RP, buf[RP:R, :])):
                    if n:
                        z = zero_rows[0:min(n, P), 0:width]
                        sp.dma_start(v, z.unsqueeze(1).to_broadcast([P, RP // P, width]) if n == RP else z).then_inc(s_zero, 16)
                        cleared += 16
            assert cleared == ZEROED
            sp.wait_ge(s_free, 1)

            def expert_weights(e, s):
                sp.dma_start(w1_sb[:, s], w1[bass.ds(e, 1), :, :].rearrange("o (c k) f -> k (o c) f", c=2)).then_inc(s_wx[s], 16)
                sp.dma_start(w2_sb[:, s], w2[bass.ds(e, 1), :, :].rearrange("o (f k) d -> k (o f) d", f=FC)).then_inc(s_wx[s], 16)
                sp.dma_start(b2B[:, s * D:(s + 1) * D], b2[bass.ds(e, 1), :].rearrange("o d -> (o d)").partition_broadcast(P)).then_inc(s_wx[s], 16)

            M = len(MT)
            last = MT[-1][1]

            def tokens(e):
                sp.dma_start(tok[:, 0:M - 1, :], tok_buf[bass.ds(e * CAP, P * (M - 1)), :].rearrange("(m p) d -> p m d", p=P)).then_inc(s_tok, 16)
                sp.dma_start(tok[0:last, M - 1, :], tok_buf[bass.ds(e * CAP + P * (M - 1), last), :]).then_inc(s_tok, 16)

            expert_weights(0, 0)
            expert_weights(1, 1)
            sp.wait_ge(s_put, 16 * NB)
            tokens(0)

            def pair_of_experts(pair, more):
                for s in range(2):
                    e = pair * 2 + s
                    if s == 0 or more:
                        sp.wait_ge(s_tokT, (e + 1) * M)
                        sp.sem_inc(s_tick)
                        sp.wait_ge(s_ids, (e + 1) * 2)
                        sp.sem_inc(s_tick)
                        tokens(e + 1)
                    if more:
                        sp.wait_ge(s_y, (e + 1) * M)
                        sp.sem_inc(s_tick)
                        expert_weights(e + 2, s)

            with sp.Fori(0, NX // 2 - 1) as pair:
                pair_of_experts(pair, True)
            pair_of_experts(NX // 2 - 1, False)
            sp.wait_ge(s_y_put, 16 * NX * M)
            sp.wait_ge(s_down, NX * M)
            y_v = y_tok[0:N, :].rearrange("(b p) d -> p b d", p=PB)
            for c in range(CH):
                for a, b_ in PARTS:
                    sp.dma_start(chunk(XL[a:b_, :, 0:D], c), chunk(y_v[a:b_], c)).then_inc(s_get[c], 16)
            for c in range(CH):
                sp.wait_ge(s_fin, CB * (c + 1))
                for a, b_ in PARTS:
                    sp.dma_start(out_v[a:b_, c * CB:(c + 1) * CB], H[a:b_, c * CB:(c + 1) * CB]).then_inc(s_out, 16)
            sp.wait_ge(s_out, 32 * CH)

        @block.gpsimd
        def _(pool):
            g = nc.gpsimd
            g.memset(dst_s[:, SC:SC + 1], PAD_DST)
            g.memset(src_i, 0)
            g.memset(ea_in, 0.0)
            g.memset(dst_i, PAD_DST).then_inc(s_pad, 1)
            g.iota(iota_i[:, :], pattern=[[1, P]], base=0, channel_multiplier=0)
            g.iota(iota_ci[:, :], pattern=[[0, 1]], base=0, channel_multiplier=1)
            g.iota(step_iota_i, pattern=[[1, STEPS]], base=0, channel_multiplier=0).then_inc(s_pad, 1)

            pool.wait_ge(s_flag, 1)
            with pool.If(flag_of(POOL_ONLY) != 0):
                with pool.Fori(0, SC) as c:
                    pool.wait_ge(s_sort_link, SORT_LINKS + (c + 1) * STEP_LINKS)
                    pool.wait_ge(s_sort_put, c * 16)
                    pool.sem_inc(s_tick)
                    g.tensor_copy(edge_slot[0:PB, :].unsqueeze(1), edge_s[0:PB, bass.ds(c, 1), :]).then_inc(s_sort_slot, 1)
                    pool.wait_ge(s_sort_slot, c + 1)
                    pool.sem_inc(s_tick)
                    g.indirect_dma_start(sorted_edges, bass.IndirectOffsetOnAxis(place[0:PB, 0:1], 0),
                                         edge_slot[0:PB, :], None).then_inc(s_sort_put, 16)

            def slot_free(k, done, first):
                if not isinstance(k, int) or k >= 2 or first:
                    pool.wait_ge(done, first + k - 1)
                    pool.sem_inc(s_tick)

            def staged_copy(feats, k, j):
                g.tensor_copy(staged[0:PB, j:j + 1, :], feats[0:PB, bass.ds(k, 1), 0:D]).then_inc(s_staged, 1)

            for l in range(2):
                base = l * STEPS
                for c in range(CH):
                    if l:
                        with pool.Fori(0, CB // 2) as turn:
                            pool.wait_ge(s_feat, turn + (c * (CB // 2) + 1))
                            for j in range(2):
                                slot_free(turn * 2 + (c * CB + j), s_tp, NB)
                                staged_copy(H, turn * 2 + (c * CB + j), j)
                    pool.wait_ge(s_staged, l * NB + (c + 1) * CB)
                    g.memset(chunk(Hn, c), 0.0).then_inc(s_cleared, 1)
                pool.wait_ge(s_srcT_out, 1)
                pool.wait_ge(s_stairs, 1)
                pool.wait_ge(s_table, 32 * CH * (l + 1))
                tiles = None
                for k, j in periods(pool, STEPS, UN, 0):
                    if j == 0:
                        _, tiles = nc.values_load_multi_w_load_instructions(
                            tile_of[0:1, bass.ds(k, UN)], engines=POOL_ONLY, min_val=0, max_val=T - 1,
                            skip_runtime_bounds_check_because=IN_RANGE)
                    s = j % XJ
                    if reused(k, 0, XJ) or l:
                        pool.wait_ge(s_agg, base + k - XJ + 1)
                        pool.sem_inc(s_tick)
                    g.tensor_copy(src_slot[:, s, :], src_cols[:, bass.ds(tiles[j] * G, G)]).then_inc(s_idx, 1)
                    pool.wait_ge(s_idx, base + k + 1)
                    pool.sem_inc(s_tick)
                    for u in range(G):
                        g.indirect_dma_start(xj[:, s, u, :], None, xl_table[l],
                                             bass.IndirectOffsetOnAxis(src_slot[:, s, u:u + 1], 0)).then_inc(s_xj[s], 16)
            pool.wait_ge(s_x2, 32)
            pool.wait_ge(s_sum, 4)
            for c in range(CH):
                mean_c = chunk(ln_mean, c)[0:PB].unsqueeze(2).to_broadcast([PB, CB, D])
                g.tensor_tensor(chunk(XRn, c), chunk(XLn, c), mean_c, ALU.subtract).then_inc(s_resid, 1)
            pool.wait_ge(s_zero, ZEROED)
            for c in range(CH):
                pool.wait_ge(s_slots, c + 1)
                pool.wait_ge(s_xl2, (c + 1) * CB)
                for b_ in range(c * CB, (c + 1) * CB):
                    g.indirect_dma_start(tok_buf, bass.IndirectOffsetOnAxis(slot_put[0:PB, b_:b_ + 1], 0),
                                         XL[0:PB, b_, :], None).then_inc(s_put, 16)
            M = len(MT)
            with pool.Fori(0, NX // 2) as pair:
                for s in range(2):
                    e = pair * 2 + s
                    pool.wait_ge(s_ids, (e + 1) * 2)
                    for m, (m0, mn) in enumerate(MT):
                        pool.wait_ge(s_y, e * M + m + 1)
                        pool.sem_inc(s_tick)
                        g.indirect_dma_start(y_tok, bass.IndirectOffsetOnAxis(tok_id[s][0:mn, m:m + 1], 0),
                                             y_sb[0:mn, m, :], None).then_inc(s_y_put, 16)

        @block.scalar
        def _(act):
            a = nc.scalar
            def root(rstd, c, n):
                act.wait_ge(s_var, n)
                a.activation(chunk(rstd[0:PB], c), chunk(col_a[0:PB], c), ACT.Sqrt, bias=eps_col[0:PB, :], scale=1.0 / D).then_inc(s_root, 1)

            root(ln_rstd, 0, 1)
            for l in range(2):
                base = l * STEPS
                if l == 0:
                    act.wait_ge(s_edges_out, 16 * 6)
                    act.wait_ge(s_srcT_out, 1)
                    act.wait_ge(s_stairs, 1)
                for k, j in blocks_by_chunk(act, l):
                    if l == 0 and j == 0 and isinstance(k, int) and 0 < k < NB:
                        root(ln_rstd, k // CB, k // CB + 1)
                    if live(k, 0, NB):
                        s = j % 2
                        act.wait_ge(s_tp, l * NB + k + 1)
                        if reused(k, 0, 2) or l:
                            act.wait_ge(s_lin, l * NB + k - 1)
                        a.activation(hT[:, s, :, :], ps[:, 4 + s, 0:2 * PB].rearrange("p (c n) -> p c n", c=2), ACT.Copy).then_inc(s_hT, 1)
                    if live(k, 1, NB):
                        s = (j - 1) % 2
                        act.wait_ge(s_lin, l * NB + k)
                        act.sem_inc(s_tick)
                        a.activation(XL[0:PB, bass.ds(k - 1, 1), :], ps[0:PB, 2 * s:2 * s + 1, 0:W], ACT.Copy).then_inc(s_xl, 1)
                act.wait_ge(s_stairs, 1)
                act.wait_ge(s_state, l + 1)
                old = [act.alloc_register(f"old_block_act{l}_{i}") for i in range(LAG)]
                blocks = held = None
                for k, j in periods(act, STEPS, UN, LAG):
                    if j == 0:
                        held = [act.snap(r, min_val=0, max_val=NB - 1) for r in old] if not (isinstance(k, int) and k == 0) else None
                        if live(k, 0, STEPS):
                            _, blocks = nc.values_load_multi_w_load_instructions(
                                block_of[0:1, bass.ds(k, UN)], engines=ACT_ONLY, min_val=0, max_val=NB - 1,
                                skip_runtime_bounds_check_because=IN_RANGE)
                    if live(k, 2, STEPS):
                        s = (j - 2) % 2
                        act.wait_ge(s_zs, base + k - 1)
                        a.activation(zs[:, s, :, 0:D], zs[:, s, :, 0:D], ACT.Relu).then_inc(s_relu, 1)
                    if live(k, 4, STEPS):
                        s = (j - 4) % 2
                        act.wait_ge(s_etT, base + k - 3)
                        if reused(k, 4, 2) or l:
                            act.wait_ge(s_agg, base + k - 5)
                        a.activation(Es[:, s, :, :], ps[:, 5, 0:G * PB].rearrange("p (g n) -> p g n", g=G), ACT.Copy).then_inc(s_e, 1)
                    if live(k, 3, STEPS):
                        s, q = (j - 3) % 2, (j - 3) % 4
                        b_ = blocks[j - 3] if j >= 3 else held[LAG + j - 3]
                        act.wait_ge(s_min, base + k - 2)
                        if reused(k, 3, 2) or l:
                            act.wait_ge(s_etT, base + k - 4)
                        if reused(k, 3, 4) or l:
                            act.wait_ge(s_acc, base + k - 6)
                        if reused(k, 3, 1):
                            act.wait_ge(s_den, base + k - 3)
                        act.sem_inc(s_tick)
                        a.activation(ETs[0:PB, s, :], mk[0:PB, s, :], ACT.Exp, bias=new_min[0:PB, q:q + 1], scale=-1.0,
                                     accum_out=den_t[0:PB, q:q + 1]).then_inc(s_num, 1)
                        a.activation(resc[0:PB, q:q + 1], old_min[0:PB, q:q + 1], ACT.Exp, bias=new_min[0:PB, q:q + 1],
                                     scale=-1.0).then_inc(s_et, 1)
                        a.activation(NM[0:PB, bass.ds(b_, 1)], new_min[0:PB, q:q + 1], ACT.Copy).then_inc(s_nm, 1)
                        act.wait_ge(s_et, base + k - 2)
                        act.sem_inc(s_tick)
                        a.activation(DEN[0:PB, bass.ds(b_, 1)], DEN[0:PB, bass.ds(b_, 1)], ACT.Identity, bias=den_t[0:PB, q:q + 1],
                                     scale=resc[0:PB, q:q + 1]).then_inc(s_den, 1)
                    if live(k, 3, STEPS) and live(k, 2, STEPS):
                        b_ = blocks[j - 2] if j >= 2 else held[LAG + j - 2]
                        act.wait_ge(s_nm, base + k - 2)
                        act.sem_inc(s_tick)
                        a.activation(old_min[0:PB, (j - 2) % 4:(j - 2) % 4 + 1], NM[0:PB, bass.ds(b_, 1)], ACT.Copy).then_inc(s_old, 1)
                    if l == 0 and live(k, 1, STEPS):
                        act.wait_ge(s_sT, k)
                        if reused(k, 1, 2):
                            act.wait_ge(s_lbc, k - 2)
                        a.activation(Srow[:, (j - 1) % 2, :, :], ps[:, 7, 0:TE].rearrange("p (g n) -> p g n", g=G), ACT.Copy).then_inc(s_sT_out, 1)
                    if live(k, 0, STEPS):
                        s = j % 4
                        act.wait_ge(s_st, base + k + 1)
                        if reused(k, 0, 4) or l:
                            act.wait_ge(s_min, base + k - 3)
                        a.activation(mpos[0:PB, s, :], ST[0:PB, s, :], ACT.Copy, bias=BIG, scale=-BIG).then_inc(s_mpos, 1)
                    if j == UN - 1 and live(k, 0, STEPS):
                        for i in range(LAG):
                            act.reg_mov(old[i], blocks[UN - LAG + i])
                for k, j in periods(act, NB, SL, 0):
                    act.wait_ge(s_self_z, l * NB + k + 1)
                    a.activation(xj[0:PB, j, 0, 0:D], xj[0:PB, j, 0, 0:D], ACT.Relu).then_inc(s_self_relu, 1)
                act.wait_ge(s_self_d, l + 1)
                a.activation(RS[0:PB, :], RS[0:PB, :], ACT.Exp)
                a.activation(PS_[0:PB, :], PS_[0:PB, :], ACT.Exp).then_inc(s_self_e, 1)
                act.wait_ge(s_self_w, l + 1)
                for k, j in periods(act, NB, SL, 0):
                    if reused(k, 0, SL) or l:
                        act.wait_ge(s_self_h, l * NB + k - SL + 1)
                        act.sem_inc(s_tick)
                    a.activation(xj[0:PB, j, 1, 0:D].unsqueeze(1), H[0:PB, bass.ds(k, 1), :], ACT.Copy,
                                 scale=RS[0:PB, bass.ds(k, 1)]).then_inc(s_self_t, 1)
                for c in range(CH):
                    act.wait_ge(s_sq_in, l * CH + c + 1)
                    a.activation(chunk(XRn, c), chunk(Hn, c), ACT.Square).then_inc(s_sq, 1)
                act.wait_ge(s_var, CH + 1 + l)
                a.activation(scale_row, scale_row, ACT.Sqrt, bias=eps_col[:, :], scale=1.0).then_inc(s_root, 1)
            def tokens_copied(k0):
                if k0:
                    act.wait_ge(s_gate, k0)
                for j in range(SL):
                    act.wait_ge(s_g_tp, k0 + j + 1)
                    a.activation(g_T[j], ps[:, G_BANKS[j], 0:2 * PB].rearrange("p (c n) -> p c n", c=2), ACT.Copy).then_inc(s_g_T, 1)
                for j in range(SL):
                    a.activation(XL[0:PB, k0 + j, 0:D], g_rows[j][0:PB, :], ACT.Copy).then_inc(s_xl2, 1)

            for c in range(CH + 3):
                if 2 <= c < CH + 2:
                    tokens_copied((c - 2) * CB)
                if c < CH:
                    act.wait_ge(s_sum_h, (c + 1) * CB)
                    a.activation(chunk(XRn, c), chunk(Hn, c), ACT.Relu, scale=-1.0).then_inc(s_neg, 1)
                if 2 <= c < CH + 2:
                    tokens_copied((c - 2) * CB + SL)
                if 1 <= c <= CH:
                    root(ln2_rstd, c - 1, CH + 2 + c)
                if c >= 3:
                    act.wait_ge(s_shift, c - 2)
                    a.activation(probs[0:PB, :], probs[0:PB, :], ACT.Exp).then_inc(s_exp, 1)
            act.wait_ge(s_b1T, 2)
            with act.Fori(0, NX) as e:
                for f in range(FC):
                    for h, (t0, tn) in enumerate(HALVES):
                        i = 2 * f + h
                        act.wait_ge(s_up, e * 2 * FC + i + 1)
                        act.sem_inc(s_tick)
                        a.activation(hidT[:, f, t0:t0 + tn], ps[:, i % 4, 0:tn], ACT.Relu,
                                     bias=b1T[:, bass.ds(e * FC + f, 1)]).then_inc(s_hid, 1)

        @block.tensor
        def _(pe):
            t = nc.tensor
            pe.wait_ge(s_consts, 1)
            pe.wait_ge(s_descents, 1)
            t.matmul(ps[0:1, 7, 0:1], ones[0:PB, 0:1], unsorted_f[0:PB, :], start=True, stop=True).then_inc(s_descents_sum, 1)
            pe.wait_ge(s_flag, 1)
            with pe.If(flag_of(PE_ONLY) != 0):
                pe.wait_ge(s_sort_link, SORT_LINKS - 1)
                t.matmul(ps[0:PB, 0, 0:NB + 1], ones[0:PB, 0:PB], beyond[0:PB, :], start=True, stop=True).then_inc(s_sort_total, 1)
                with pe.Fori(0, SC) as c:
                    pe.wait_ge(s_sort_link, SORT_LINKS + c * STEP_LINKS + 2)
                    pe.sem_inc(s_tick)
                    t.matmul(ps[0:PB, 1, 0:NB], before[0:PB, :], in_block[0:PB, :], start=True, stop=True)
                    t.matmul(ps[0:PB, 2, 0:NB], ones[0:PB, 0:PB], in_block[0:PB, :], start=True, stop=True).then_inc(s_sort_rank, 1)
            pe.wait_ge(s_edges_f, 2)
            for k in range(K7):
                mm = t.matmul(ps[0:NB - 1, k // 4, (k % 4) * P:(k % 4 + 1) * P], dst_f[:, k, P - 1:P].to_broadcast([P, NB - 1]), ident[:, :], start=True, stop=True)
            mm.then_inc(s_last, 1)
            for k in range(K7):
                mm = t.transpose(ps[:, 2 + k // 4, (k % 4) * P:(k % 4 + 1) * P], src_f[:, k, :], ident[:, :])
            mm.then_inc(s_srcT, 1)
            pe.wait_ge(s_after, 1)
            t.matmul(ps[0:1, 4, 0:STEPS], ones[0:NB - 1, 0:1], after[0:NB - 1, :], start=True, stop=True).then_inc(s_blocks, 1)

            def node_sum(srcv, b_, **flags):
                return t.matmul(ps[:, 0, 0:D], ones[0:PB, :], srcv[0:PB, bass.ds(b_, 1), 0:D], **flags)

            def transposed(j, done):
                for c in range(2):
                    mm = t.transpose(ps[:, 4 + j % 2, c * PB:(c + 1) * PB],
                                     staged[0:PB, j % 2, c * P:(c + 1) * P], ident[0:PB, 0:PB])
                mm.then_inc(done, 1)

            for l in range(2):
                base = l * STEPS
                pe.wait_ge(s_wext, l + 1)
                for k, j in periods(pe, NB, 2, 1):
                    if live(k, 0, NB):
                        if reused(k, 0, 2) or l:
                            pe.wait_ge(s_hT, l * NB + k - 1)
                        pe.wait_ge(s_staged, l * NB + k + 1)
                        transposed(j, s_tp)
                    if live(k, 1, NB):
                        s = (j - 1) % 2
                        pe.wait_ge(s_hT, l * NB + k)
                        if reused(k, 1, 2) or l:
                            pe.wait_ge(s_xl, l * NB + k - 2)
                            pe.wait_ge(s_xr, l * NB + k - 2)
                        for h in range(2):
                            for c in range(2):
                                mm = t.matmul(ps[0:PB, 2 * s + h, 0:W], hT[:, s, c, :], Wlr[:, c, h * W:(h + 1) * W], start=c == 0, stop=c == 1)
                        mm.then_inc(s_lin, 1)
                pe.wait_ge(s_we, 16 + 32 * (l + 1))
                pe.wait_ge(s_xr, NB * (l + 1))
                pe.wait_ge(s_xl, NB * (l + 1))
                pe.wait_ge(s_stairs, 1)
                blocks = None
                for k, j in periods(pe, STEPS, UN, LAG):
                    if live(k, 4, STEPS):
                        s, r = (j - 4) % 2, (j - 4) % XJ
                        pe.wait_ge(s_e, base + k - 3)
                        if reused(k, 4, 1) or l:
                            pe.wait_ge(s_acc, base + k - 4)
                        for u in range(G):
                            mm = t.matmul(ps[0:PB, 6, 0:D], Es[:, s, u, :], xj[:, r, u, 0:D], start=u == 0, stop=u == G - 1)
                        mm.then_inc(s_agg, 1)
                    if live(k, 2, STEPS):
                        s, r = (j - 2) % 2, (j - 2) % 4
                        pe.wait_ge(s_nlog, base + k - 1)
                        if reused(k, 2, 1) or l:
                            pe.wait_ge(s_min, base + k - 2)
                        if l == 0 and reused(k, 2, 1):
                            pe.wait_ge(s_eas, k - 2)
                        for u in range(G):
                            mm = t.matmul(ps[0:PB, 4, u * P:(u + 1) * P], nlog[:, r, u:u + 1].to_broadcast([P, PB]), ident[:, :], start=True, stop=True)
                        if l == 0:
                            pe.wait_ge(s_sT_out, k - 1)
                            for u in range(G):
                                mm = t.matmul(ps[0:PB, 4, TE:TE + 3], Srow[:, s, u, 0:PB], Srow[:, s, u, PB:P], start=u == 0, stop=u == G - 1)
                        mm.then_inc(s_lbc, 1)
                    if live(k, 3, STEPS):
                        s = (j - 3) % 2
                        pe.wait_ge(s_num, base + k - 2)
                        if reused(k, 3, 1) or l:
                            pe.wait_ge(s_e, base + k - 3)
                        for u in range(G):
                            mm = t.transpose(ps[:, 5, u * PB:(u + 1) * PB], ETs[0:PB, s, u * P:(u + 1) * P], ident[0:PB, 0:PB])
                        mm.then_inc(s_etT, 1)
                    if live(k, 0, STEPS):
                        if j == 0:
                            _, blocks = nc.values_load_multi_w_load_instructions(
                                block_of[0:1, bass.ds(k, UN)], engines=PE_ONLY, min_val=0, max_val=NB - 1,
                                skip_runtime_bounds_check_because=IN_RANGE)
                        s, r = j % 2, j % 4
                        pe.wait_ge(s_st, base + k + 1)
                        if reused(k, 0, 2) or l:
                            pe.wait_ge(s_zs, base + k - 1)
                        for u in range(G):
                            mm = t.matmul(ps[:, 2 * s + u, 0:W], ST[:, r, u * P:(u + 1) * P],
                                          XR[:, bass.ds(blocks[j], 1), :].rearrange("p o w -> p (o w)"), start=True, stop=True)
                        mm.then_inc(s_z, 1)
                    if l == 0 and live(k, 0, STEPS):
                        if reused(k, 0, 1):
                            pe.wait_ge(s_sT_out, k)
                        for u in range(G):
                            mm = t.transpose(ps[:, 7, u * P:(u + 1) * P], ST[:, j % 4, u * P:(u + 1) * P], ident[:, :])
                        mm.then_inc(s_sT, 1)
                if l == 0:
                    pe.wait_ge(s_me, 1)
                    t.transpose(ps[0:2 * NB, 5, 0:PB], ME[0:PB, :, :].rearrange("p j b -> p (j b)"), ident[0:PB, 0:PB]).then_inc(s_me_T, 1)
                pe.wait_ge(s_eye, l + 1)
                for k, j in periods(pe, NB, SL, 0):
                    turn = (k - j) // SL if isinstance(k, int) else None
                    done = NB // SL * 16 * l
                    pe.wait_ge(s_eye_me[j], done + (turn + 1) * 16 if turn is not None else (k - j) * 16 // SL + (done + 16))
                    if reused(k, 0, SL) or l:
                        pe.wait_ge(s_self_z, l * NB + k - SL + 1)
                    t.matmul(ps[0:PB, j, 0:W], eye[j], XR[:, bass.ds(k, 1), :].rearrange("p o w -> p (o w)"),
                             start=True, stop=True).then_inc(s_self_mm, 1)
                pe.wait_ge(s_self_z, NB * (l + 1))
                for k, j in periods(pe, NB - SL, SL, SL):
                    pe.wait_ge(s_self_h, l * NB + k + 1)
                    ins = node_sum(H, k, start=isinstance(k, int) and k == 0, stop=isinstance(k, int) and k == NB - 1)
                ins.then_inc(s_sum, 1)
                for c in range(CH):
                    pe.wait_ge(s_sq, l * CH + c + 1)
                    node_sum(XR, c * CB, start=c == 0, stop=False)
                    with pe.Fori(0, CB // 2 - 1) as turn:
                        for u in range(2):
                            node_sum(XR, turn * 2 + (c * CB + 1 + u), start=False, stop=False)
                    ins = node_sum(XR, (c + 1) * CB - 1, start=False, stop=c == CH - 1)
                ins.then_inc(s_sum, 1)
            pe.wait_ge(s_moe_w, 48)
            t.transpose(ps[:, 6, 0:NX * FC], b1_rows, ident[0:NX * FC, 0:NX * FC]).then_inc(s_b1T, 1)
            pe.wait_ge(s_b1T, 2)
            for c in range(CH + 1):
                if c < CH:
                    if c >= 2:
                        pe.wait_ge(s_shift, c - 1)
                    with pe.Fori(0, CB // SL) as turn:
                        for j in range(SL):
                            k = turn * SL + (c * CB + j)
                            if j == 0:
                                pe.wait_ge(s_g_T, turn * SL + c * CB)
                            pe.wait_ge(s_staged, k + (2 * NB + 1))
                            for h in range(2):
                                mm = t.transpose(ps[:, G_BANKS[j], h * PB:(h + 1) * PB], g_rows[j][0:PB, h * P:(h + 1) * P], ident[0:PB, 0:PB])
                            mm.then_inc(s_g_tp, 1)
                        for j in range(SL):
                            k = turn * SL + (c * CB + j)
                            pe.wait_ge(s_g_T, k + 1)
                            for h in range(2):
                                mm = t.matmul(ps[0:PB, GATE[c % 2], bass.ds(turn * (SL * NX) + j * NX, NX)], g_T[j][:, h, :], gw_sb[:, h, :], start=h == 0, stop=h == 1)
                            mm.then_inc(s_gate, 1)
                if c:
                    pe.wait_ge(s_onehot, c)
                    t.matmul(ps[0:PB, 0, 0:NE], triu[0:PB, 0:PB], onehot[0:PB, :], start=True, stop=True)
                    t.matmul(ps[0:PB, 0, NE:2 * NE], ones[0:PB, 0:PB], onehot[0:PB, :], start=True, stop=True).then_inc(s_cum, 1)
            pe.wait_ge(s_slots, CH)
            M = len(MT)

            def tokens_T(e):
                pe.wait_ge(s_tok, (e + 1) * 32)
                for m, (m0, mn) in enumerate(MT):
                    if m >= 2:
                        pe.wait_ge(s_tokT_out, e * M + m - 1)
                    for c in range(2):
                        mm = t.transpose(ps[:, 6 + m % 2, c * P:c * P + mn], tok[0:mn, m, c * P:(c + 1) * P], ident[0:mn, 0:mn])
                    mm.then_inc(s_tokT, 1)

            def expert(pair, s, more):
                e = pair * 2 + s
                pe.wait_ge(s_tokT_out, (e + 1) * M)
                pe.wait_ge(s_wx[s], pair * 48 + 48)
                for f in range(FC):
                    for h, (t0, tn) in enumerate(HALVES):
                        i = 2 * f + h
                        if i >= 4:
                            pe.wait_ge(s_hid, e * 2 * FC + i - 3)
                        for c in range(2):
                            mm = t.matmul(ps[:, i % 4, 0:tn], w1_sb[:, s, c, f * P:(f + 1) * P], tokT[:, c, t0:t0 + tn], start=c == 0, stop=c == 1)
                        mm.then_inc(s_up, 1)
                if more:
                    tokens_T(e + 1)
                pe.wait_ge(s_hid, (e + 1) * 2 * FC)
                pe.wait_ge(s_y, e * M)
                for m, (m0, mn) in enumerate(MT):
                    if m >= 2:
                        pe.wait_ge(s_y, e * M + m - 1)
                    for f in range(FC):
                        mm = t.matmul(ps[0:mn, 4 + m % 2, 0:D], hidT[:, f, m0:m0 + mn], w2_sb[:, s, f, :], start=f == 0, stop=f == FC - 1)
                    mm.then_inc(s_down, 1)

            tokens_T(0)
            with pe.Fori(0, NX // 2 - 1) as pair:
                for s in range(2):
                    expert(pair, s, True)
            for s in range(2):
                expert(NX // 2 - 1, s, s == 0)
            pe.wait_ge(s_bad, 1)
            t.matmul(ps[0:1, 7, 0:1], ones[:, 0:1], bad[:, :], start=True, stop=True).then_inc(s_bad_sum, 1)

        @block.vector
        def _(dve):
            v = nc.vector
            links = [0]

            def link(ins):
                links[0] += 1
                ins.then_inc(s_link, 1)
                dve.wait_ge(s_link, links[0])

            dve.wait_ge(s_pad, 2)
            v.memset(Srow[0:1, :, :, :], 0.0)
            link(v.memset(ST[96:P, :, :], 1.0))
            v.engine_nop().then_inc(s_fixed, 1)
            v.memset(ones[:, :], 1.0)
            v.memset(eps_col[:, :], EPS)
            link(v.tensor_copy(iota_row[:, :], iota_i[:, :]))
            link(v.tensor_copy(iota_col[:, :], iota_ci[:, :]))
            v.tensor_scalar(ident[:, :], iota_row[:, :], iota_col[:, :], None, ALU.is_equal)
            link(v.tensor_scalar(node_id[:, :], iota_row[:, 0:NB], float(PB), iota_col[:, :], ALU.mult, ALU.add))
            v.engine_nop().then_inc(s_consts, 1)
            dve.wait_ge(s_dst_s, 32)
            link(v.tensor_tensor(descents[0:PB], dst_s[0:PB, 0:SC], dst_s[0:PB, 1:SC + 1], ALU.is_gt))
            v.tensor_reduce(unsorted_f[0:PB, :], descents[0:PB], AX_X, ALU.add).then_inc(s_descents, 1)
            dve.wait_ge(s_descents_sum, 1)
            v.tensor_scalar(unsorted[:, :], ps[0:1, 7, 0:1], 0.0, None, ALU.is_gt).then_inc(s_flag, 1)
            dve.wait_ge(s_flag, 1)
            dve.wait_ge(s_edges, 16 * 9)
            with dve.If(flag_of(DVE_ONLY) != 0):
                def sort_link(ins, count):
                    ins.then_inc(s_sort_link, 1)
                    dve.wait_ge(s_sort_link, count)
                    dve.sem_inc(s_tick)

                v.memset(pad_edge[0:NPAD, :], 0.0)
                v.memset(beyond[0:PB, :], 0.0)
                v.tensor_scalar(before[0:PB, :], iota_row[0:PB, 0:PB], iota_col[0:PB, :], None, ALU.is_gt)
                v.tensor_scalar(block_start[0:PB, :], iota_row[0:PB, 0:NB + 1], float(PB), None, ALU.mult)
                sort_link(v.tensor_copy(edge_dst[0:PB], dst_s[0:PB, 0:SC]), 1)
                v.memset(pad_edge[0:NPAD, 1:2], float(PAD_DST)).then_inc(s_sort_pad, 1)
                dve.wait_ge(s_sort_in, 32)
                v.tensor_copy(edge_s[0:PB, :, 0], src_s[0:PB])
                v.tensor_copy(edge_s[0:PB, :, 1], dst_s[0:PB, 0:SC])
                v.tensor_copy(edge_s[0:PB, :, 2:4], ea_s[0:PB])
                with dve.Fori(0, SC) as c:
                    sort_link(v.scalar_tensor_tensor(beyond[0:PB, :], block_start[0:PB, :], edge_dst[0:PB, bass.ds(c, 1)],
                                                     beyond[0:PB, :], ALU.is_le, ALU.add), c + 2)
                dve.wait_ge(s_sort_total, 1)
                sort_link(v.tensor_scalar(places[0:PB, :], ps[0:PB, 0, 0:NB], -1.0, float(E), ALU.mult, ALU.add), SORT_LINKS)
                with dve.Fori(0, SC) as c:
                    first = SORT_LINKS + c * STEP_LINKS
                    sort_link(v.tensor_scalar(is_beyond[0:PB, :], block_start[0:PB, :], edge_dst[0:PB, bass.ds(c, 1)], None, ALU.is_le), first + 1)
                    sort_link(v.tensor_tensor(in_block[0:PB, :], is_beyond[0:PB, 0:NB], is_beyond[0:PB, 1:NB + 1], ALU.subtract), first + 2)
                    dve.wait_ge(s_sort_rank, c + 1)
                    dve.sem_inc(s_tick)
                    sort_link(v.tensor_tensor(place_of[0:PB, :], places[0:PB, :], ps[0:PB, 1, 0:NB], ALU.add), first + 3)
                    v.tensor_tensor(places[0:PB, :], places[0:PB, :], ps[0:PB, 2, 0:NB], ALU.add)
                    sort_link(v.tensor_tensor_reduce(place_of[0:PB, :], place_of[0:PB, :], in_block[0:PB, :], 1.0, 0.0,
                                                     ALU.mult, ALU.add, place_f[0:PB, :]), first + 4)
                    dve.wait_ge(s_sort_put, c * 16)
                    dve.sem_inc(s_tick)
                    sort_link(v.tensor_copy(place[0:PB, :], place_f[0:PB, :]), first + 5)
                dve.wait_ge(s_sort_back, 32)
                KF = K7 - 1
                for tile, f in ((src_i, 0), (dst_i, 1)):
                    v.tensor_copy(tile[:, 0:KF, :], loaded_edges[:, 0:KF, :, f])
                    v.tensor_copy(tile[0:LASTK, KF, :], loaded_edges[0:LASTK, KF, :, f])
                v.tensor_copy(ea_in[:, 0:KF], loaded_edges[:, 0:KF, :, 2:4])
                sort_link(v.tensor_copy(ea_in[0:LASTK, KF], loaded_edges[0:LASTK, KF, :, 2:4]), SORT_LINKS + SC * STEP_LINKS + 1)
            v.tensor_copy(src_f, src_i)
            v.tensor_copy(dst_f, dst_i).then_inc(s_edges_f, 1)
            v.tensor_copy(ea_pl.rearrange("p k j e -> p k e j"), ea_in).then_inc(s_edges_f, 1)
            dve.wait_ge(s_srcT, 1)
            v.tensor_copy(src_cols[:, 0:512], ps[:, 2, :])
            v.tensor_copy(src_cols[:, 512:K7 * P], ps[:, 3, 0:K7 * P - 512]).then_inc(s_srcT_out, 1)
            dve.wait_ge(s_last, 1)
            q = NB - 1
            v.tensor_copy(last_dst[0:q, 0:512], ps[0:q, 0, :])
            link(v.tensor_copy(last_dst[0:q, 512:K7 * P], ps[0:q, 1, 0:K7 * P - 512]))
            link(v.tensor_scalar(tau[0:q, 0:1], iota_col[0:q, :], float(PB), float(PB), ALU.mult, ALU.add))
            link(v.tensor_scalar(reached[0:q, 0:T - 1], last_dst[0:q, 1:2 * (T - 1):2], tau[0:q, 0:1], None, ALU.is_lt))
            link(v.tensor_reduce(tau[0:q, 1:2], reached[0:q, 0:T - 1], AX_X, ALU.add))
            link(v.tensor_scalar(tau[0:q, 1:2], tau[0:q, 1:2], iota_col[0:q, :], 1.0, ALU.add, ALU.add))
            link(v.tensor_copy(step_iota, step_iota_i))
            v.tensor_scalar(after[0:q, :], step_iota[0:q, :], tau[0:q, 1:2], None, ALU.is_ge).then_inc(s_after, 1)
            dve.wait_ge(s_blocks, 1)
            link(v.tensor_copy(block_f[0:1, :], ps[0:1, 4, 0:STEPS]))
            v.tensor_copy(block_of[:, :], block_f[0:1, :])
            link(v.tensor_tensor(step_iota[0:1, :], step_iota[0:1, :], block_f[0:1, :], ALU.subtract))
            v.tensor_copy(tile_of[:, :], step_iota[0:1, :]).then_inc(s_stairs, 1)

            def wide(col):
                return col[0:PB, :].unsqueeze(2).to_broadcast([PB, NB, D])

            def over(row, blocks):
                return row[0:PB, :].unsqueeze(1).to_broadcast([PB, blocks, D])

            def block_stats(srcv, k):
                v.bn_stats(stats[0:PB, bass.ds(k, 1), :].rearrange("p o s -> p (o s)"), srcv[:, bass.ds(k, 1), :].rearrange("p o d -> p (o d)"))

            def stats_of_chunk(srcv, c):
                with dve.Fori(0, CB // 5) as turn:
                    for u in range(5):
                        block_stats(srcv, turn * 5 + (c * CB + u))

            def layer_norm_sums(mean, c):
                link(v.engine_nop())
                st, mean, sq = chunk(stats[0:PB], c), chunk(mean[0:PB], c), chunk(col_a[0:PB], c)
                v.tensor_tensor(mean, st[:, :, 1], st[:, :, 4], ALU.add)
                link(v.tensor_tensor(sq, st[:, :, 1], st[:, :, 4], ALU.subtract))
                v.tensor_scalar(mean, mean, 0.5, None, ALU.mult)
                link(v.tensor_tensor(sq, sq, sq, ALU.mult))
                link(v.scalar_tensor_tensor(sq, sq, D / 4.0, st[:, :, 2], ALU.mult, ALU.add))
                v.tensor_tensor(sq, sq, st[:, :, 5], ALU.add).then_inc(s_var, 1)

            dve.wait_ge(s_x[0], 32)
            stats_of_chunk(Hn, 0)
            layer_norm_sums(ln_mean, 0)

            def weight_products(l):
                dve.wait_ge(s_w, 16 * 4 * (l + 1))
                v.tensor_scalar(att_lin[:, :], att_relu[:, :], -0.2, None, ALU.mult)
                link(v.tensor_scalar(att_relu[:, :], att_relu[:, :], -0.8, None, ALU.mult))
                for view in (Wlr[:, 0, 0:W], Wlr[:, 0, W:2 * W], Wlr[:, 1, 0:W], Wlr[:, 1, W:2 * W], WeB[:, 0, :], WeB[:, 1, :]):
                    link(v.tensor_tensor_reduce(junk[:, 0:D], view[:, 0:D], att_lin[:, :], 1.0, 0.0, ALU.mult, ALU.add, view[:, D:D + 1]))
                v.engine_nop().then_inc(s_wext, 1)

            def scaled(c):
                h = chunk(Hn, c)
                link(v.tensor_tensor(h, h, over(scale_row, CB), ALU.mult))
                link(v.tensor_tensor(h, h, over(rows[:, 2, :], CB), ALU.add))

            def next_input(t):
                h, neg = H[0:PB, bass.ds(t * 2, 2), :], XR[0:PB, bass.ds(t * 2, 2), 0:D]
                ops = [lambda: v.tensor_tensor(h, h, over(scale_row, 2), ALU.mult),
                       lambda: v.tensor_tensor(h, h, over(rows[:, 2, :], 2), ALU.add),
                       lambda: v.tensor_scalar(neg, h, 0.0, slope_1[0:PB, :], ALU.min, ALU.mult),
                       lambda: v.tensor_tensor(h, h, neg, ALU.add)]
                for i, op in enumerate(ops):
                    if i:
                        dve.wait_ge(s_in_link, t * 3 + i)
                        dve.sem_inc(s_tick)
                    op().then_inc(s_feat if i == 3 else s_in_link, 1)

            def xr_out(l, k, j):
                dve.wait_ge(s_lin, l * NB + k + 1)
                v.tensor_copy(XR[0:PB, bass.ds(k, 1), :], ps[0:PB, 2 * (j % 2) + 1:2 * (j % 2) + 2, 0:W]).then_inc(s_xr, 1)

            for l in range(2):
                base = l * STEPS
                if l == 0:
                    weight_products(0)
                    for k, j in chain(blocks_by_chunk(dve, 0), [(NB + 1, 1)]):
                        if j == 0 and isinstance(k, int) and k < NB:
                            c = k // CB
                            if c:
                                layer_norm_sums(ln_mean, c)
                            if c + 1 < CH:
                                dve.wait_ge(s_x[c + 1], 32)
                            dve.wait_ge(s_root, c + 1)
                            link(v.reciprocal(chunk(ln_rstd[0:PB], c), chunk(ln_rstd[0:PB], c)))
                        if live(k, 0, NB):
                            if reused(k, 0, 2):
                                dve.wait_ge(s_tp, k - 1)
                                dve.sem_inc(s_tick)
                            v.tensor_scalar(staged[0:PB, j, :], H[0:PB, bass.ds(k, 1), :].rearrange("p o d -> p (o d)"),
                                            ln_mean[0:PB, bass.ds(k, 1)], ln_rstd[0:PB, bass.ds(k, 1)],
                                            ALU.subtract, ALU.mult).then_inc(s_staged, 1)
                            if c + 1 < CH:
                                block_stats(Hn, k + CB)
                        if live(k, 2, NB):
                            xr_out(l, k - 2, j)
                else:
                    for t, j in periods(dve, NB // 2, 5, 2):
                        if live(t, 0, NB // 2):
                            next_input(t)
                        if live(t, 2, NB // 2):
                            for u in range(2):
                                xr_out(l, t * 2 - 4 + u, u)
                v.memset(NM[:, :], START)
                v.memset(old_min[:, 0:1], START)
                v.memset(DEN[:, :], 0.0)
                if l == 0:
                    v.memset(EAS[:, :, :], 0.0)
                v.engine_nop().then_inc(s_state, 1)
                dve.wait_ge(s_state, l + 1)
                dve.wait_ge(s_cleared, CH * (l + 1))
                dve.wait_ge(s_stairs, 1)
                old = [dve.alloc_register(f"old_block{l}_{i}") for i in range(LAG)]
                blocks = held = None
                for k, j in periods(dve, STEPS, UN, LAG):
                    if j == 0:
                        held = [dve.snap(r, min_val=0, max_val=NB - 1) for r in old] if not (isinstance(k, int) and k == 0) else None
                        if live(k, 0, STEPS):
                            _, blocks = nc.values_load_multi_w_load_instructions(
                                block_of[0:1, bass.ds(k, UN)], engines=DVE_ONLY, min_val=0, max_val=NB - 1,
                                skip_runtime_bounds_check_because=IN_RANGE)

                    def block_at(lag):
                        return blocks[j - lag] if j >= lag else held[LAG + j - lag]

                    if live(k, 5, STEPS):
                        r = (j - 5) % 4
                        b_ = block_at(5)
                        dve.wait_ge(s_agg, base + k - 4)
                        dve.wait_ge(s_et, base + k - 4)
                        if reused(k, 5, 1):
                            dve.wait_ge(s_acc, base + k - 5)
                        dve.sem_inc(s_tick)
                        v.scalar_tensor_tensor(H[0:PB, bass.ds(b_, 1), :].rearrange("p o d -> p (o d)"), H[0:PB, bass.ds(b_, 1), :].rearrange("p o d -> p (o d)"),
                                               resc[0:PB, r:r + 1], ps[0:PB, 6, 0:D], ALU.mult, ALU.add).then_inc(s_acc, 1)
                    if live(k, 3, STEPS):
                        s, r = (j - 3) % 2, (j - 3) % 4
                        if reused(k, 3, 1):
                            dve.wait_ge(s_old, l * (STEPS - 1) + k - 3)
                        if reused(k, 3, 4) or l:
                            dve.wait_ge(s_et, base + k - 6)
                        dve.wait_ge(s_lbc, base + k - 2)
                        dve.wait_ge(s_mpos, base + k - 2)
                        if reused(k, 3, 2) or l:
                            dve.wait_ge(s_num, base + k - 4)
                        b_ = block_at(3)
                        if l == 0 and reused(k, 3, 1):
                            dve.wait_ge(s_eas, k - 3)
                        dve.sem_inc(s_tick)
                        v.tensor_tensor_reduce(mk[0:PB, s, :], mpos[0:PB, r, :], ps[0:PB, 4, 0:TE], 1.0, old_min[0:PB, r:r + 1],
                                               ALU.add, ALU.min, new_min[0:PB, r:r + 1]).then_inc(s_min, 1)
                        if l == 0:
                            v.tensor_tensor(EAS[0:PB, bass.ds(b_, 1), :], EAS[0:PB, bass.ds(b_, 1), :],
                                            ps[0:PB, 4, TE:TE + 3].unsqueeze(1), ALU.add).then_inc(s_eas, 1)

                    def weighted(u):
                        s, r = (j - 2) % 2, (j - 2) % 4
                        return v.tensor_tensor_reduce(zs[:, s, u, 0:D], zs[:, s, u, 0:D], att_relu[:, :], 1.0, zs[:, s, u, D:W],
                                                      ALU.mult, ALU.add, nlog[:, r, u:u + 1])

                    if live(k, 2, STEPS):
                        dve.wait_ge(s_relu, base + k - 1)
                        if reused(k, 2, 4) or l:
                            dve.wait_ge(s_lbc, base + k - 5)
                        weighted(0)
                    if live(k, 0, STEPS):
                        s = j % 4
                        dve.wait_ge(s_row[s], (base + k - s) // 4 * 32 + 32 if isinstance(k, int) else (base // 4 + 1) * 32 + (k - s) * 8)
                        if reused(k, 0, 4) or l:
                            dve.wait_ge(s_mpos, base + k - 3)
                        v.tensor_scalar(ST[0:PB, s, :], dst_b[0:PB, s, :], node_id[0:PB, bass.ds(block_at(0), 1)], None, ALU.is_equal).then_inc(s_st, 1)
                    if live(k, 2, STEPS):
                        weighted(1).then_inc(s_nlog, 1)
                    if live(k, 1, STEPS):
                        s, r = (j - 1) % 2, (j - 1) % XJ
                        dve.wait_ge(s_z, base + k)
                        kk = k - 1
                        dve.wait_ge(s_xj[r], (base + kk - r) // XJ * 32 + 32 if isinstance(k, int) else (base // XJ + 1) * 32 + (kk - r) * (32 // XJ))
                        if reused(k, 1, 2) or l:
                            dve.wait_ge(s_nlog, base + k - 2)
                        v.tensor_tensor(zs[:, s, :, :], xj[:, r, :, :], ps[:, 2 * s:2 * s + 2, 0:W], ALU.add).then_inc(s_zs, 1)
                    if j == UN - 1 and live(k, 0, STEPS):
                        for i in range(LAG):
                            dve.reg_mov(old[i], blocks[UN - LAG + i])
                dve.wait_ge(s_acc, base + STEPS)
                dve.wait_ge(s_nm, base + STEPS)
                dve.wait_ge(s_den, base + STEPS)
                if l == 0:
                    link(v.tensor_scalar(col_a[0:PB, :], EAS[0:PB, :, 2], 1.0, None, ALU.max))
                    link(v.reciprocal(col_a[0:PB, :], col_a[0:PB, :]))
                    for i in range(2):
                        link(v.tensor_tensor(ME[0:PB, i, :], EAS[0:PB, :, i], col_a[0:PB, :], ALU.mult))
                    v.engine_nop().then_inc(s_me, 1)
                    dve.wait_ge(s_me_T, 1)
                    dve.wait_ge(s_sT_out, STEPS)
                    v.tensor_copy(ME_T, ps[0:2 * NB, 5, 0:PB]).then_inc(s_me_T_out, 1)
                dve.wait_ge(s_mpos, base + STEPS)
                for i in range(SL):
                    ins = v.tensor_copy(eye[i][0:PB, :], ident[0:PB, 0:PB])
                ins.then_inc(s_eye, 1)
                if l:
                    v.memset(zero_rows[:, 0:D], 0.0)
                    v.memset(zero_rows[:, D:W], float(N)).then_inc(s_zero_src, 1)
                for k, j in periods(dve, NB, SL, 2):
                    if live(k, 0, NB):
                        dve.wait_ge(s_self_mm, l * NB + k + 1)
                        if reused(k, 0, SL):
                            dve.wait_ge(s_self_q, l * NB + k - SL + 1)
                        dve.sem_inc(s_tick)
                        v.tensor_tensor(xj[0:PB, j, 0:1, :], XL[0:PB, bass.ds(k, 1), :], ps[0:PB, j:j + 1, 0:W], ALU.add).then_inc(s_self_z, 1)
                    if live(k, 2, NB):
                        i = (j - 2) % SL
                        dve.wait_ge(s_self_relu, l * NB + k - 1)
                        if i == 0 and reused(k, 2, SL):
                            dve.wait_ge(s_self_l, l * NB + k - 2)
                        v.tensor_tensor_reduce(xj[0:PB, i, 0, 0:D], xj[0:PB, i, 0, 0:D], att_relu[0:PB, :], 1.0, xj[0:PB, i, 0, D:W],
                                               ALU.mult, ALU.add, ls_slot[0:PB, i:i + 1]).then_inc(s_self_q, 1)
                    if j == 1 and live(k, SL + 1, NB):
                        dve.wait_ge(s_self_q, l * NB + k - 1)
                        dve.sem_inc(s_tick)
                        v.tensor_copy(LS[0:PB, bass.ds(k - SL - 1, SL)], ls_slot[0:PB, :]).then_inc(s_self_l, SL)
                dve.wait_ge(s_self_l, NB * (l + 1))
                link(v.tensor_tensor(col_a[0:PB, :], NM[0:PB, :], LS[0:PB, :], ALU.min))
                v.tensor_tensor(RS[0:PB, :], col_a[0:PB, :], NM[0:PB, :], ALU.subtract)
                v.tensor_tensor(PS_[0:PB, :], col_a[0:PB, :], LS[0:PB, :], ALU.subtract).then_inc(s_self_d, 1)
                dve.wait_ge(s_self_e, l + 1)
                link(v.tensor_tensor(DEN[0:PB, :], DEN[0:PB, :], RS[0:PB, :], ALU.mult))
                link(v.tensor_tensor(DEN[0:PB, :], DEN[0:PB, :], PS_[0:PB, :], ALU.add))
                link(v.reciprocal(DEN[0:PB, :], DEN[0:PB, :]))
                v.tensor_tensor(RS[0:PB, :], RS[0:PB, :], DEN[0:PB, :], ALU.mult)
                link(v.tensor_tensor(PS_[0:PB, :], PS_[0:PB, :], DEN[0:PB, :], ALU.mult))
                v.engine_nop().then_inc(s_self_w, 1)
                for k, j in periods(dve, NB, SL, 0):
                    dve.wait_ge(s_self_t, l * NB + k + 1)
                    dve.sem_inc(s_tick)
                    v.scalar_tensor_tensor(H[0:PB, bass.ds(k, 1), :].rearrange("p o d -> p (o d)"), XL[0:PB, bass.ds(k, 1), 0:D].rearrange("p o d -> p (o d)"),
                                           PS_[0:PB, bass.ds(k, 1)], xj[0:PB, j, 1, 0:D], ALU.mult, ALU.add).then_inc(s_self_h, 1)
                dve.wait_ge(s_self_h, NB * (l + 1))
                dve.wait_ge(s_sum, 2 * l + 1)
                dve.wait_ge(s_rows, 64 * (l + 1))
                link(v.scalar_tensor_tensor(mu, ps[:, 0, 0:D], 1.0 / N, rows[:, 0, :], ALU.mult, ALU.add))
                link(v.tensor_tensor(mu, rows[:, 0, :], mu, ALU.subtract))
                for c in range(CH):
                    v.tensor_tensor(chunk(Hn, c), chunk(Hn, c), over(mu, CB), ALU.add).then_inc(s_sq_in, 1)
                if l == 0:
                    weight_products(1)
                link(v.tensor_scalar(slope_1[:, :], slope[:, :], 1.0, -1.0 if l else 1.0, ALU.subtract, ALU.mult))
                dve.wait_ge(s_sum, 2 * l + 2)
                v.tensor_scalar(scale_row, ps[:, 0, 0:D], 1.0 / N, None, ALU.mult).then_inc(s_var, 1)
                dve.wait_ge(s_root, CH + 1 + l)
                link(v.reciprocal(scale_row, scale_row))
                link(v.tensor_tensor(scale_row, scale_row, rows[:, 1, :], ALU.mult))
            v.tensor_copy(XL[0:PB, :, D], node_id[0:PB, :])
            v.tensor_scalar(triu[0:PB, 0:PB], iota_row[0:PB, 0:PB], iota_col[0:PB, :], None, ALU.is_ge)
            v.tensor_scalar(e_off, iota_row[:, 0:NX], -float(NX), None, ALU.add)
            v.memset(earlier, 0.0)
            link(v.memset(chain_mask, 1.0))
            link(v.memset(chain_mask.rearrange("p (e b) -> p e b", e=NX)[:, :, 0:1], 0.0))
            n = PB

            def per_b(col):
                return col.unsqueeze(2).to_broadcast([PB, CB, NX])

            def per_e(row):
                return row[0:PB, :].unsqueeze(1).to_broadcast([PB, CB, NX])

            def route(c):
                top_c, first_c, pos_c, kept_c, slot_c, coef_c, id_c = (chunk(v_[0:n], c) for v_ in (top, first_e, pos, kept, slot_f, coef, node_id))
                pr, oh = be(probs[0:n]), be(onehot[0:n])
                dve.wait_ge(s_gate, (c + 1) * CB)
                link(v.tensor_tensor(pr, be(ps[0:n, GATE[c % 2], 0:NE]), per_e(gb_sb), ALU.add))
                link(v.tensor_reduce(top_c, pr, AX_X, ALU.max))
                v.tensor_tensor(pr, pr, per_b(top_c), ALU.subtract).then_inc(s_shift, 1)
                dve.wait_ge(s_exp, c + 1)
                link(v.tensor_reduce(top_c, pr, AX_X, ALU.add))
                link(v.reciprocal(top_c, top_c))
                link(v.tensor_tensor(pr, pr, per_b(top_c), ALU.mult))
                link(v.tensor_reduce(top_c, pr, AX_X, ALU.max))
                link(v.tensor_tensor(oh, pr, per_b(top_c), ALU.is_ge))
                link(v.tensor_tensor(oh, oh, per_e(e_off), ALU.mult))
                link(v.tensor_reduce(first_c, oh, AX_X, ALU.min))
                v.tensor_tensor(oh, per_e(e_off), per_b(first_c), ALU.is_equal).then_inc(s_onehot, 1)
                dve.wait_ge(s_cum, c + 1)
                link(v.tensor_copy(tot_eb[0:n].rearrange("p (e b) -> p b e", e=NX), be(ps[0:n, 0, NE:2 * NE])))
                base_v = base_eb[0:n].rearrange("p (e b) -> p e b", e=NX)
                v.tensor_reduce(total[0:n], tot_eb[0:n].rearrange("p (e b) -> p e b", e=NX), AX_X, ALU.add)
                link(v.tensor_tensor_scan(base_eb[0:n], chain_mask[0:n], tot_eb[0:n], 0.0, ALU.mult, ALU.add))
                link(v.tensor_tensor(base_eb[0:n], base_eb[0:n], tot_eb[0:n], ALU.subtract))
                link(v.tensor_tensor(base_v, base_v, earlier[0:n].unsqueeze(2).to_broadcast([n, NX, CB]), ALU.add))
                v.tensor_tensor(earlier[0:n], earlier[0:n], total[0:n], ALU.add)
                link(v.tensor_tensor(be(cum[0:n]), be(ps[0:n, 0, 0:NE]), base_eb[0:n].rearrange("p (e b) -> p b e", e=NX), ALU.add))
                link(v.tensor_tensor(be(cum[0:n]), be(cum[0:n]), oh, ALU.mult))
                link(v.tensor_reduce(pos_c, be(cum[0:n]), AX_X, ALU.add))
                link(v.tensor_scalar(pos_c, pos_c, -1.0, None, ALU.add))
                link(v.tensor_scalar(kept_c, pos_c, float(CAP), None, ALU.is_lt))
                v.tensor_tensor(coef_c, top_c, kept_c, ALU.mult)
                link(v.tensor_scalar(first_c, first_c, float(NX), float(CAP), ALU.add, ALU.mult))
                link(v.tensor_tensor(slot_c, first_c, pos_c, ALU.add))
                link(v.scalar_tensor_tensor(slot_c, slot_c, -float(NX * CAP), id_c, ALU.add, ALU.subtract))
                link(v.tensor_tensor(slot_c, slot_c, kept_c, ALU.mult))
                link(v.scalar_tensor_tensor(slot_c, slot_c, float(NX * CAP), id_c, ALU.add, ALU.add))
                v.tensor_copy(chunk(slot_put[0:n], c), slot_c).then_inc(s_slots, 1)

            dve.wait_ge(s_b1T, 1)
            v.tensor_copy(b1T[:, :], ps[:, 6, 0:NX * FC]).then_inc(s_b1T, 1)

            def second_ln(k0):
                if k0:
                    dve.wait_ge(s_g_tp, k0)
                    dve.wait_ge(s_xl2, k0)
                for j in range(SL):
                    v.tensor_scalar(g_rows[j][0:PB, :], H[0:PB, k0 + j, :], ln2_mean[0:PB, k0 + j:k0 + j + 1], ln2_rstd[0:PB, k0 + j:k0 + j + 1],
                                    ALU.subtract, ALU.mult).then_inc(s_staged, 1)

            for c in range(CH + 3):
                if 2 <= c < CH + 2:
                    dve.wait_ge(s_root, CH + 1 + c)
                    rstd_c = chunk(ln2_rstd[0:PB], c - 2)
                    link(v.reciprocal(rstd_c, rstd_c))
                    second_ln((c - 2) * CB)
                if c < CH:
                    scaled(c)
                    dve.wait_ge(s_resid, c + 1)
                    with dve.Fori(0, CB // 5) as turn:
                        for u in range(5):
                            k = turn * 5 + (c * CB + u)
                            h = H[0:PB, bass.ds(k, 1), :].rearrange("p o d -> p (o d)")
                            v.scalar_tensor_tensor(h, XR[0:PB, bass.ds(k, 1), 0:D].rearrange("p o d -> p (o d)"), ln_rstd[0:PB, bass.ds(k, 1)],
                                                   h, ALU.mult, ALU.add).then_inc(s_sum_h, 1)
                if 2 <= c < CH + 2:
                    second_ln((c - 2) * CB + SL)
                if 1 <= c <= CH:
                    h = chunk(Hn, c - 1)
                    dve.wait_ge(s_neg, c)
                    link(v.scalar_tensor_tensor(h, chunk(XRn, c - 1), slope_1[0:PB, :], h, ALU.mult, ALU.add))
                    link(v.tensor_tensor(h, h, chunk(XLn, c - 1), ALU.add))
                    if c == CH:
                        v.engine_nop().then_inc(s_free, 1)
                    stats_of_chunk(Hn, c - 1)
                    layer_norm_sums(ln2_mean, c - 1)
                if c >= 3:
                    route(c - 3)
            M = len(MT)
            n = PB
            last = MT[-1][1]
            v.tensor_scalar(place_no, iota_row[:, 0:M], float(P), iota_col[:, :], ALU.mult, ALU.add)
            v.memset(y_zero, 0.0)
            link(v.memset(y_zeros, 0.0))
            link(v.tensor_scalar(slot_f[0:n], coef[0:n], 0.0, None, ALU.mult))
            link(v.tensor_reduce(y_zeros[0:n, 0:1], slot_f[0:n], AX_X, ALU.add))
            dve.wait_ge(s_put, 16 * NB)
            def tokens_out(e, slot):
                if not (isinstance(e, int) and e == 0):
                    dve.wait_ge(s_up, e * (2 * FC))
                for m, (m0, mn) in enumerate(MT):
                    dve.wait_ge(s_tokT, e * M + m + 1)
                    v.tensor_copy(tokT[:, :, m0:m0 + mn], ps[:, 6 + m % 2, 0:D].rearrange("p (c t) -> p c t", c=2)[:, :, 0:mn]).then_inc(s_tokT_out, 1)
                parts = [(tok[:, 0:M - 1, D], slice(0, P), slice(0, M - 1)), (tok[0:last, M - 1, D:W], slice(0, last), slice(M - 1, M))]
                for i, (ids, q, ms) in enumerate(parts):
                    v.scalar_tensor_tensor(id_f[q, ms], ids, float(N), place_no[q, ms], ALU.is_ge, ALU.mult).then_inc(s_id_f, 1)
                dve.wait_ge(s_id_f, (e + 1) * 2)
                if slot or not isinstance(e, int):
                    dve.wait_ge(s_y_put, (e - 1) * (16 * M))
                dve.sem_inc(s_tick)
                for i, (ids, q, ms) in enumerate(parts):
                    v.tensor_tensor(tok_id[slot][q, ms], ids, id_f[q, ms], ALU.add).then_inc(s_ids, 1)

            def expert(pair, s, more):
                e = pair * 2 + s
                if more:
                    tokens_out(e + 1, 1 - s)
                for m, (m0, mn) in enumerate(MT):
                    dve.wait_ge(s_down, e * M + m + 1)
                    if m == 0:
                        dve.wait_ge(s_y_put, e * (16 * M))
                        dve.wait_ge(s_wx[s], pair * 48 + 48)
                    v.tensor_tensor(y_sb[0:mn, m, :], ps[0:mn, 4 + m % 2, 0:D], b2B[0:mn, s * D:(s + 1) * D], ALU.add).then_inc(s_y, 1)
                    dve.wait_ge(s_y, e * M + m + 1)
                    if m:
                        dve.wait_ge(s_y_chk, e * (M + 1) + m)
                    dve.sem_inc(s_tick)
                    v.tensor_tensor_reduce(junk[0:mn, 0:D], y_sb[0:mn, m, :], zero_rows[0:mn, 0:D], 1.0, 0.0,
                                           ALU.mult, ALU.add, y_zero[0:mn, m:m + 1]).then_inc(s_y_chk, 1)
                dve.wait_ge(s_y_chk, e * (M + 1) + M)
                dve.sem_inc(s_tick)
                v.tensor_tensor(y_zeros, y_zeros, y_zero, ALU.add).then_inc(s_y_chk, 1)
                dve.wait_ge(s_y_chk, e * (M + 1) + M + 1)

            tokens_out(0, 0)
            with dve.Fori(0, NX // 2 - 1) as pair:
                for s in range(2):
                    expert(pair, s, True)
            for s in range(2):
                expert(NX // 2 - 1, s, s == 0)
            link(v.tensor_reduce(bad[:, :], y_zeros, AX_X, ALU.add))
            link(v.tensor_scalar(bad[:, :], bad[:, :], 0.0, None, ALU.is_equal))
            v.tensor_scalar(bad[:, :], bad[:, :], -1.0, 1.0, ALU.mult, ALU.add).then_inc(s_bad, 1)
            dve.wait_ge(s_bad_sum, 1)
            v.tensor_scalar(not_finite[:, :], ps[0:1, 7, 0:1], 0.0, None, ALU.is_gt).then_inc(s_bad_flag, 1)
            dve.wait_ge(s_bad_flag, 1)
            bad_flag = nc.values_load(not_finite[0:1, 0:1], engines=DVE_ONLY, min_val=0, max_val=1,
                                      skip_runtime_bounds_check_because="DVE writes 0 or 1")
            with dve.If(bad_flag != 0):
                for c in range(CH):
                    dve.wait_ge(s_get[c], 32)
                link(v.tensor_tensor(XLn, XLn, wide(coef), ALU.mult))
                FMAX = 3.4028234663852886e38
                half = NB // 2
                cells = half * D
                for h in range(2):
                    y = XL[0:PB, h * half:(h + 1) * half, 0:D]
                    mask = XRf[0:PB, 0:cells].bitcast(I32).rearrange("p (b d) -> p b d", b=half)
                    clean = XRf[0:PB, cells:2 * cells].rearrange("p (b d) -> p b d", b=half)
                    link(v.memset(clean, 0.0))
                    link(v.tensor_tensor(mask, y, y, ALU.is_equal))
                    link(v.copy_predicated(clean, mask, y))
                    for op, bound, value in ((ALU.is_gt, FMAX, 1.0e4), (ALU.is_lt, -FMAX, -1.0e4)):
                        link(v.memset(junk[:, 0:1], value))
                        link(v.tensor_scalar(mask, y, bound, None, op))
                        link(v.copy_predicated(clean, mask, junk[0:PB, 0:1].unsqueeze(1).to_broadcast([PB, half, D])))
                    link(v.tensor_copy(y, clean))
                link(v.memset(coef, 1.0))
            for c in range(CH):
                dve.wait_ge(s_get[c], 32)
                with dve.Fori(0, CB // 5) as turn:
                    for u in range(5):
                        k = turn * 5 + (c * CB + u)
                        h = H[0:PB, bass.ds(k, 1), :].rearrange("p o d -> p (o d)")
                        v.scalar_tensor_tensor(h, XL[0:PB, bass.ds(k, 1), 0:D].rearrange("p o d -> p (o d)"),
                                               coef[0:PB, bass.ds(k, 1)], h, ALU.mult, ALU.add).then_inc(s_fin, 1)


_INS = ["x", "src", "dst", "edge_attr_2"]
_LAYER = ["Wl", "Wr", "We", "att", "b", "g", "beta", "a"]
_FFN = ["gate_w", "gate_b", "w1", "b1", "w2", "b2"]


def kernel(**inputs):
    import numpy as np
    import concourse.bacc as bacc
    from concourse.bass_utils import run_bass_kernel_spmd as run

    nc = bacc.Bacc("TRN2", target_bir_lowering=False, num_devices=1, dynamic_dma_scratch_size=8192)
    arrays = {}

    def given(name):
        a = np.ascontiguousarray(inputs[name])
        if a.ndim == 0:
            a = a.reshape(1)
        arrays["in_" + name] = a
        return nc.dram_tensor("in_" + name, a.shape, mybir.dt.from_np(a.dtype), kind="ExternalInput").ap()

    ins = [given(n) for n in _INS]
    layers = [[given(f"L0_gnn_{n}{l}") for n in _LAYER] for l in (1, 2)]
    ffn = [given("L0_ffn_" + n) for n in _FFN]
    out = nc.dram_tensor("out_0", inputs["x"].shape, F32, kind="ExternalOutput").ap()
    program(nc, *ins, layers, *ffn, out)
    return run(nc, [arrays], core_ids=[0]).results[0]["out_0"]
```
